# Optimizing a Trainium2 kernel written in Bass

```python
import numpy as np
import jax
import jax.numpy as jnp

def _softmax(x, axis=-1):
    return jax.nn.softmax(x, axis=axis)

def _gelu(x):
    return jax.nn.gelu(x, approximate=True)

def _silu(x):
    return jax.nn.silu(x)

def _sigmoid(x):
    return jax.nn.sigmoid(x)

def _layernorm(x, axis=-1, eps=1e-05):
    m = jnp.mean(x, axis=axis, keepdims=True)
    v = jnp.var(x, axis=axis, keepdims=True)
    return (x - m) / jnp.sqrt(v + eps)

def _scatter_add(tgt, idx, src, axis=0):
    return tgt.at[idx].add(src)

def _segment_sum(src, seg, n):
    return jax.ops.segment_sum(src, seg, n)
kernel_name = 'mk_seq_preln_d1_jaxref_r4_06a885'

def setup_inputs(seed: int=0):
    np.random.seed(seed)
    _w = jnp.asarray

    def _L0_attn_setup():
        import jax, jax.numpy as jnp
        import numpy as np
        D_MODEL = 256
        H = 4
        DK = 128
        DV = 64
        EPS = 1e-05
        SCALE = DK ** (-0.5)

        def _delta_rule(q, k, v, beta):
            b = q.shape[0]
            qt = jnp.moveaxis(q, 1, 0)
            kt = jnp.moveaxis(k, 1, 0)
            vt = jnp.moveaxis(v, 1, 0)
            bt = jnp.moveaxis(beta, 1, 0)
            S0 = jnp.zeros((b, H, DK, DV), q.dtype)

            def step(S, inp):
                q_t, k_t, v_t, b_t = inp
                pred = jnp.einsum('bhk,bhkv->bhv', k_t, S)
                delta = (v_t - pred) * b_t[..., None]
                S = S + k_t[..., :, None] * delta[..., None, :]
                o_t = jnp.einsum('bhk,bhkv->bhv', q_t, S)
                return (S, o_t)
            _, o = jax.lax.scan(step, S0, (qt, kt, vt, bt))
            return jnp.moveaxis(o, 0, 1)
        key = jax.random.key(seed)
        ks = jax.random.split(key, 8)
        w = lambda k, i, o: jax.random.normal(k, (i, o), jnp.float32) * 2.0 ** (-2.5) * (6.0 / (i + o)) ** 0.5 * 2
        return {'x': jax.random.normal(ks[0], (2, 1024, D_MODEL), jnp.float32), 'Wq': w(ks[1], D_MODEL, H * DK), 'Wk': w(ks[2], D_MODEL, H * DK), 'Wv': w(ks[3], D_MODEL, H * DV), 'Wb': w(ks[4], D_MODEL, H), 'Wg': w(ks[5], D_MODEL, H * DV), 'Wo': w(ks[6], H * DV, D_MODEL), 'norm_w': jnp.ones((DV,), jnp.float32)}
    _L0_attn_in = _L0_attn_setup()

    def _L0_ffn_setup():
        import jax, jax.numpy as jnp
        import numpy as np
        B, S, D, E, K = (4, 512, 256, 8, 2)
        H = 4 * D
        key = jax.random.key(seed)
        k0, k1, k2, k3 = jax.random.split(key, 4)
        x = jax.random.normal(k0, (B, S, D), dtype=jnp.float32)
        router_w = jax.random.normal(k1, (E, D), dtype=jnp.float32) * 0.02
        w1 = jax.random.normal(k2, (E, H, D), dtype=jnp.float32) * 0.02
        w2 = jax.random.normal(k3, (E, D, H), dtype=jnp.float32) * 0.02
        return {'x': x, 'router_w': router_w, 'w1': w1, 'w2': w2}
    _L0_ffn_in = _L0_ffn_setup()
    _d = {'L0_attn_x': _L0_attn_in['x'], 'L0_attn_Wq': _L0_attn_in['Wq'], 'L0_attn_Wk': _L0_attn_in['Wk'], 'L0_attn_Wv': _L0_attn_in['Wv'], 'L0_attn_Wb': _L0_attn_in['Wb'], 'L0_attn_Wg': _L0_attn_in['Wg'], 'L0_attn_Wo': _L0_attn_in['Wo'], 'L0_attn_norm_w': _L0_attn_in['norm_w'], 'L0_ffn_router_w': _L0_ffn_in['router_w'], 'L0_ffn_w1': _L0_ffn_in['w1'], 'L0_ffn_w2': _L0_ffn_in['w2']}
    _x0 = _d['L0_attn_x']
    _d['L0_attn_x'] = jax.random.normal(jax.random.fold_in(jax.random.key(seed), 1), (8, 512, 256), dtype=_x0.dtype)
    del _x0
    return _d

def reference(L0_attn_x, L0_attn_Wq, L0_attn_Wk, L0_attn_Wv, L0_attn_Wb, L0_attn_Wg, L0_attn_Wo, L0_attn_norm_w, L0_ffn_router_w, L0_ffn_w1, L0_ffn_w2):

    def _L0_attn_ref(x, Wq, Wk, Wv, Wb, Wg, Wo, norm_w):
        import jax, jax.numpy as jnp
        import numpy as np
        D_MODEL = 256
        H = 4
        DK = 128
        DV = 64
        EPS = 1e-05
        SCALE = DK ** (-0.5)

        def _delta_rule(q, k, v, beta):
            b = q.shape[0]
            qt = jnp.moveaxis(q, 1, 0)
            kt = jnp.moveaxis(k, 1, 0)
            vt = jnp.moveaxis(v, 1, 0)
            bt = jnp.moveaxis(beta, 1, 0)
            S0 = jnp.zeros((b, H, DK, DV), q.dtype)

            def step(S, inp):
                q_t, k_t, v_t, b_t = inp
                pred = jnp.einsum('bhk,bhkv->bhv', k_t, S)
                delta = (v_t - pred) * b_t[..., None]
                S = S + k_t[..., :, None] * delta[..., None, :]
                o_t = jnp.einsum('bhk,bhkv->bhv', q_t, S)
                return (S, o_t)
            _, o = jax.lax.scan(step, S0, (qt, kt, vt, bt))
            return jnp.moveaxis(o, 0, 1)
        b, n, _ = x.shape
        q = (x @ Wq).reshape(b, n, H, DK)
        k = (x @ Wk).reshape(b, n, H, DK)
        v = (x @ Wv).reshape(b, n, H, DV)
        beta = jax.nn.sigmoid(x @ Wb)
        k = k * jax.lax.rsqrt(jnp.sum(k * k, axis=-1, keepdims=True) + 1e-12)
        q = q * SCALE
        o = _delta_rule(q, k, v, beta)
        g = (x @ Wg).reshape(b, n, H, DV)
        o = o * jax.lax.rsqrt(jnp.mean(o * o, axis=-1, keepdims=True) + EPS) * norm_w
        o = o * (g * jax.nn.sigmoid(g))
        return o.reshape(b, n, H * DV) @ Wo

    def _L0_ffn_ref(x, router_w, w1, w2):
        import jax, jax.numpy as jnp
        import numpy as np
        B, S, D, E, K = (4, 512, 256, 8, 2)
        H = 4 * D
        b, s, d = x.shape
        e = router_w.shape[0]
        logits = jnp.einsum('bsd,ed->bse', x, router_w)
        probs = jax.nn.softmax(logits, axis=-1)
        topk_vals, topk_idx = jax.lax.top_k(probs, K)
        x_flat = x.reshape(b * s, d)
        vals = topk_vals.reshape(b * s, K)
        idx = topk_idx.reshape(b * s, K)
        out = jnp.zeros_like(x_flat)
        for eid in range(e):
            w = jnp.sum(jnp.where(idx == eid, vals, jnp.zeros((), x.dtype)), axis=-1)
            h = jax.nn.gelu(x_flat @ w1[eid].T, approximate=False)
            y = h @ w2[eid].T
            out = out + w[:, None] * y
        return out.reshape(b, s, d)
    x = L0_attn_x
    x = x + _L0_attn_ref(_layernorm(x, axis=-1), L0_attn_Wq, L0_attn_Wk, L0_attn_Wv, L0_attn_Wb, L0_attn_Wg, L0_attn_Wo, L0_attn_norm_w)
    x = x + _L0_ffn_ref(_layernorm(x, axis=-1), L0_ffn_router_w, L0_ffn_w1, L0_ffn_w2)
    return x

_drawn_inputs = setup_inputs


def setup_inputs(seed=0):
    import zlib

    import numpy as np

    out = dict(_drawn_inputs(seed))
    spreads = {'L0_attn_norm_w': (1.0, 0.2)}
    factors = {}
    for name, (base, spread) in spreads.items():
        noise = np.random.default_rng([zlib.crc32(name.encode()), seed]).standard_normal(out[name].shape)
        drawn = base * np.exp(spread * noise) if base else spread * noise
        out[name] = jnp.asarray(drawn.astype(out[name].dtype))
    for name, factor in factors.items():
        out[name] = (out[name] * factor).astype(out[name].dtype)
    return out
```

```python
import concourse.bass as bass
from concourse import mybir
from contextlib import ExitStack

P = 128
B, N, D = 8, 512, 256
H, DK, DV = 4, 128, 64
E, HID = 8, 1024
T = B * N // P
C = N // P
KC = D // P
KH = HID // P
EPS = 1e-5
REGION = B * N + P
SPARE = E * REGION
ROWS = SPARE + P
RW = D + 2
MAXT = 2 * B * N // P + E
LEVELS = 7
W_SCALE = 256.0
H_SCALE = 64.0
PIECE = 2 * E * HID // T


def build(nc, x, wq, wk, wvg, wb, wo, norm_w, router, w1, w2, fconst, iconst, out):
    fp32, fp16, i32 = mybir.dt.float32, mybir.dt.float16, mybir.dt.int32
    ALU, ACT, AX = mybir.AluOpType, mybir.ActivationFunctionType, mybir.AxisListType
    ctx = ExitStack()
    with ctx:
        def sb(name, shape, dt=fp32):
            return ctx.enter_context(nc.sbuf_tensor(name, shape, dt))

        def sem(name):
            return ctx.enter_context(nc.semaphore(name))

        routed = nc.dram_tensor("routed_rows", [ROWS, RW], fp32, kind="Internal").ap()
        table_dram = nc.dram_tensor("tile_table_dram", [P, 2], i32, kind="Internal").ap()

        w1_hi = sb("w1_hi", [P, KC * E * HID], fp16)
        w1_lo = sb("w1_lo", [P, KC * E * HID], fp16)
        w2_hi = sb("w2_hi", [P, KH * E * D], fp16)
        w2_lo = sb("w2_lo", [P, KH * E * D], fp16)
        wq_s = sb("wq_s", [P, KC, H * DK])
        wk_s = sb("wk_s", [P, KC, H * DK])
        wvg_s = sb("wvg_s", [P, KC, 2 * H * DV])
        wb_s = sb("wb_s", [P, KC, H])
        wo_s = sb("wo_s", [P, KC, D])
        router_s = sb("router_s", [P, KC, E])
        normw_s = sb("normw_s", [P, DV])
        fc = sb("fc", [P, FCONST])
        ident = fc[:, 0:128]
        causal = fc[:, 128:256]
        before = fc[:, 256:384]
        ones = fc[:, 384:512]
        pref = fc[:, 512:520]
        region = fc[:, 520:528]
        lane = fc[:, 528:529]
        token_id = fc[:, 529:529 + T]
        half_neg = fc[:, 561:577]
        mask_s = sb("mask_s", [P, 2 * LEVELS, 64], mybir.dt.int8)

        x_s = sb("x_s", [P, C, D])
        xn = sb("xn", [P, D])
        xnT = sb("xnT", [P, KC, P])
        KQ = sb("KQ", [P, 2, H, 2, P])
        Kp = sb("Kp", [P, 2, H, DK])
        mask_in = Kp[:, :, :, :].rearrange("p s h n -> p (s h n)")[:, 0:2 * LEVELS * 64].bitcast(i32)
        Vp = sb("Vp", [P, 2, H, DV])
        gs = sb("gs", [P, 2, H, DV])
        AT = sb("AT", [P, 2, H, P])
        XT = sb("XT", [P, 2, H, P])
        nG = sb("nG", [P, 2, H, P])
        X = sb("X", [P, H, P])
        Y = sb("Y", [P, H, P])
        S = sb("S", [P, H, DV])
        R = sb("R", [P, H, DV])
        W = sb("W", [P, H, DV])
        sq = sb("sq", [P, H, DK])
        osq = sb("osq", [P, H, DV])
        oo = sb("oo", [P, H, DV])
        oT = sb("oT", [P, KC, P])
        rowA = sb("rowA", [P, C, RW])
        rowB = sb("rowB", [P, C, RW])
        xn2T = sb("xn2T", [P, KC, P])
        wst = sb("wst", [P, 2, PIECE])
        st6 = sb("st6", [P, 6])
        mv = sb("mv", [P, 2])
        rstd = sb("rstd", [P, 1])
        eb = sb("eb", [P, H])
        ks = sb("ks", [P, 2 * H])
        karg = sb("karg", [P, 2 * H])
        kscale = sb("kscale", [P, 2 * H])
        osum = sb("osum", [P, H])
        oarg = sb("oarg", [P, H])
        ors = sb("ors", [P, H])
        st6b = sb("st6b", [P, 6])
        mv2 = sb("mv2", [P, 2])
        rstd2 = sb("rstd2", [P, 1])
        logits = sb("logits", [P, C, E])
        r8 = [sb(f"r8_{i}", [P, C, E]) for i in range(8)]
        r1 = [sb(f"r1_{i}", [P, C]) for i in range(8)]
        first = sb("first", [P, C, E])
        second = sb("second", [P, C, E])
        both = sb("both", [P, C, E])
        run = sb("run", [P, E])
        rbase = sb("rbase", [P, C, E])
        pos = sb("pos", [P, C, E])
        slot = sb("slot", [P, 2, C], i32)
        zrow = sq[:, :, :].rearrange("p h n -> p (h n)")[:, 0:RW]
        t8 = [sb(f"t8_{i}", [P, E]) for i in range(8)]
        t8i = sb("t8i", [P, E], i32)
        t8j = sb("t8j", [P, E], i32)
        pad_idx = sb("pad_idx", [P, E], i32)
        tab_f = sb("tab_f", [P, 2])
        tab_i = sb("tab_i", [P, 2], i32)
        tab = W[:, :, :].rearrange("p h n -> p (h n)").bitcast(i32)
        xg = rowA
        xTh = oT[:, :, :].rearrange("p a b -> p (a b)").bitcast(fp16).rearrange("p (s k n) -> p s k n", s=2, k=KC)
        xTl = xn2T[:, :, :].rearrange("p a b -> p (a b)").bitcast(fp16).rearrange("p (s k n) -> p s k n", s=2, k=KC)
        hf = KQ[:, :, :, :, :].rearrange("p s h a n -> p s (h a n)")[:, :, 0:HID]
        hhi = Kp[:, :, :, :].rearrange("p s h n -> p s (h n)").bitcast(fp16)
        hlo = AT[:, :, :, :].rearrange("p s h n -> p s (h n)").bitcast(fp16)
        yrow = Vp[:, :, :, :].rearrange("p s h n -> p s (h n)")
        yidx = sb("yidx", [P, 4], i32)

        PS = [ctx.enter_context(nc.psum_tensor(f"ps{i}", [P, 512], fp32)) for i in range(8)]
        def heads(ap, n):
            return ap.rearrange("p (h n) -> p h n", h=n)
        p_y = [heads(PS[a][:, 0:128], 2) for a in range(2)]
        p_x = [heads(PS[a][:, 128:256], 2) for a in range(2)]
        p_xt = [heads(PS[a][:, 256:384], 2) for a in range(2)]
        p_kv = PS[2][:, :]
        p_q = heads(PS[3][:, :], H)
        p_o = heads(PS[3][:, 0:256], H)
        p_p = heads(PS[4][:, 0:256], H)
        p_u = heads(PS[4][:, 256:512], H)
        p_kT = heads(PS[5][:, :], H)
        p_gram = [PS[5 + a][:, :].rearrange("p (h a n) -> p h a n", h=2, a=2) for a in range(2)]
        p_xnT = PS[6][:, 0:256]
        p_rank = PS[6][:, 0:C * E]
        p_tot = PS[6][:, C * E:2 * C * E]
        p_beta = PS[7][:, 0:H]
        p_oT = PS[7][:, 0:256]
        p_wo = PS[7][:, 0:256]
        p_xn2T = PS[7][:, 0:256]
        p_lg = PS[7][:, 0:E]
        p_gT = [PS[a][:, 0:256] for a in range(2)]
        p_h = [[PS[2 + 2 * a + m] for m in range(2)] for a in range(2)]
        p_yo = [PS[6 + a][:, 0:D] for a in range(2)]

        s_const = sem("const_loaded")
        s_x = [sem(f"x_loaded{c}") for c in range(C)]
        s_x1out = [sem(f"x1_stored{c}") for c in range(C)]
        s_w = [sem(f"w_loaded{q}") for q in range(2)]
        s_whi = sem("w_hi_ready")
        s_wlo = sem("w_lo_ready")
        s_init = sem("buffers_initialised")
        s_held = [sem("vector_waits_held"), sem("pool_waits_held")]
        pool_engine = nc.gpsimd
        s_xn = sem("xn_ready")
        s_xnTp = sem("xnT_in_psum")
        s_xnTs = sem("xnT_in_sbuf")
        s_kps = sem("k_and_beta_in_psum")
        s_ksq = sem("k_squared")
        s_eb = sem("exp_beta_ready")
        s_karg = sem("k_scale_argument")
        s_kscale = sem("k_scale_ready")
        s_kp = sem("kprime_ready")
        s_kTp = sem("kT_in_psum")
        s_kTs = sem("kT_in_sbuf")
        s_qps = sem("qT_in_psum")
        s_qs = sem("qT_in_sbuf")
        s_vgps = sem("v_g_in_psum")
        s_th = sem("tanh_g_ready")
        s_gs = sem("v_and_gate_ready")
        s_gram = sem("gram_in_psum")
        s_nG = sem("neg_gram_ready")
        s_AT = sem("masked_scores_ready")
        s_Xi = sem("inverse_initialised")
        s_X0 = sem("level_one_ready")
        s_yps = sem("y_in_psum")
        s_ys = sem("y_in_sbuf")
        s_xps = sem("update_in_psum")
        s_xup = sem("inverse_updated")
        s_pps = sem("state_product_in_psum")
        s_r = sem("r_ready")
        s_wps = sem("w_in_psum")
        s_ws = sem("w_in_sbuf")
        s_ops = sem("o_in_psum")
        s_ups = sem("state_update_in_psum")
        s_s = sem("state_ready")
        s_osq = sem("o_squared")
        s_oarg = sem("o_scale_argument")
        s_ors = sem("o_scale_ready")
        s_on = sem("o_normalised")
        s_oTp = sem("oT_in_psum")
        s_oTs = sem("oT_in_sbuf")
        s_wops = sem("attention_out_in_psum")
        s_res = sem("residual_ready")
        s_mv = sem("ln1_variance")
        s_rstd = sem("ln1_rstd")
        s_mv2 = sem("ln2_variance")
        s_rstd2 = sem("ln2_rstd")
        s_xn2 = sem("xn2_ready")
        s_rowB = sem("row_copy_ready")
        s_xn2Tp = sem("xn2T_in_psum")
        s_xn2Ts = sem("xn2T_in_sbuf")
        s_lgps = sem("logits_in_psum")
        s_lg = sem("logits_ready")
        s_rd = sem("logit_differences")
        s_rexp = sem("logit_exponentials")
        s_both = sem("expert_masks_ready")
        s_rank = sem("ranks_in_psum")
        s_slot = sem("slots_ready")
        s_scat = [sem(f"rows_scattered{c}") for c in range(C)]
        s_tail = sem("tail_tables_ready")
        s_pads = sem("pads_written")
        s_tabd = sem("table_in_dram")
        s_tab = sem("table_loaded")
        s_dve = sem("dve_step")
        s_xg = [sem(f"xg_loaded{q}") for q in range(4)]
        s_gTp = sem("xgT_in_psum")
        s_gTh = sem("xgT_hi_ready")
        s_gTl = sem("xgT_lo_ready")
        s_hps = sem("hidden_in_psum")
        s_gelu = sem("gelu_ready")
        s_hhi = sem("hidden_hi_ready")
        s_hlo = sem("hidden_lo_ready")
        s_yops = sem("expert_out_in_psum")
        s_yrow = sem("expert_rows_ready")
        s_acc = sem("rows_accumulated")

        block = ctx.enter_context(nc.Block())

        def up_to(eng, s, per, t, k):
            b, c = t
            value = b * (per * C) + (per * c + k)
            if not (isinstance(value, int) and value <= 0):
                eng.wait_ge(s, value)

        def hold(eng):
            eng.sem_inc(s_held[eng is pool_engine])

        def before_(t, n):
            return (t[0], t[1] - n)

        def after_(t, n=1):
            return (t[0], t[1] + n)

        def sequences(eng, body):
            body(0, True, False)
            with eng.Fori(1, B - 1) as b:
                body(b, False, False)
            body(B - 1, False, True)

        def even(ap, lev):
            s = 1 << lev
            return ap.rearrange("p h (n two s) -> p h n two s", two=2, s=s)[:, :, :, 0, :]

        def odd(ap, lev):
            s = 1 << lev
            return ap.rearrange("p h (n two s) -> p h n two s", two=2, s=s)[:, :, :, 1, :]

        def packed(ap, lev):
            return ap.rearrange("p h (n s) -> p h n s", s=1 << lev)

        def level_mask(lev, transposed, heads):
            m = mask_s[:, 2 * lev + transposed, :].rearrange("p (n s) -> p n s", s=1 << lev).unsqueeze(1)
            return m.broadcast_to([P, heads, 64 >> lev, 1 << lev])

        def col(ap, n):
            return ap.unsqueeze(2).broadcast_to([P, ap.shape[1], n])

        @block.sync
        def _(sp):
            loads = [(fc[:, :], fconst), (mask_in, iconst.rearrange("p a b -> p (a b)")),
                     (wk_s[:, :, :], wk.rearrange("(k p) n -> p k n", p=P)),
                     (wb_s[:, :, :], wb.rearrange("(k p) n -> p k n", p=P)),
                     (wvg_s[:, :, :], wvg.rearrange("(k p) n -> p k n", p=P)),
                     (wq_s[:, :, :], wq.rearrange("(k p) n -> p k n", p=P)),
                     (wo_s[:, :, :], wo.rearrange("(k p) n -> p k n", p=P)),
                     (router_s[:, :, :], router.rearrange("(k p) n -> p k n", p=P)),
                     (normw_s[:, :], norm_w.partition_broadcast(P))]
            sp.dma_start(x_s[:, 0, :], x[0, :, :]).then_inc(s_x[0], 16)
            for dst, src in loads:
                sp.dma_start(dst, src).then_inc(s_const, 16)
            assert len(loads) == CONST_LOADS
            for c in range(1, 3):
                sp.dma_start(x_s[:, c, :], x[c, :, :]).then_inc(s_x[c], 16)

            def store(b, c):
                up_to(sp, s_res, 1, (b, c), 1)
                sp.dma_start(out[bass.ds((b * C + c) * P, P), :], x_s[:, c % C, :]).then_inc(s_x1out[c % C], 16)

            def body(b, first, last):
                for c in range(C):
                    up_to(sp, s_wlo, 2, (b, c), 0)
                    for q, src in enumerate((w1, w2)):
                        sp.dma_start(wst[:, q, :], src[bass.ds(b * C + c, 1), :, :].rearrange("a p n -> p (a n)")).then_inc(s_w[q], 16)
                    if not (first and c == 0):
                        store(b, c - 1)
                    if not (last and c >= 1):
                        if not (first and c == 0):
                            sp.wait_ge(s_x1out[(c - 1) % C], b * 16 + (16 if c else 0))
                            up_to(sp, s_xn2, 1, (b, c - 1), 1)
                        d = (c + 3) % C
                        sp.dma_start(x_s[:, d, :], x[bass.ds(b * C + (c + 3), 1), :, :].rearrange("a p n -> p (a n)")).then_inc(s_x[d], 16)
            sequences(sp, body)
            store(B - 1, C - 1)
            sp.wait_ge(s_tail, 1)
            sp.dma_start(table_dram, tab_i[:, :]).then_inc(s_tabd, 16)
            sp.wait_ge(s_tabd, 16)
            sp.dma_start(tab[0:1, :], table_dram.rearrange("p n -> (p n)").unsqueeze(0)).then_inc(s_tab, 16)
            sp.wait_ge(s_tab, 16)
            sp.wait_ge(s_pads, 16 * (E + 2))
            for c in range(C):
                sp.wait_ge(s_scat[c], 32 * B)

            def load_rows(i, q):
                row = sp.value_load(tab[0:1, bass.ds(i * 8 + (2 * q + 1), 1)], min_val=0, max_val=SPARE)
                sp.dma_start(xg[:, q % 4, :], routed[bass.ds(row, P), :]).then_inc(s_xg[q % 4], 16)

            for q in range(3):
                load_rows(0, q)

            def expert_body(i, last):
                for q in range(4):
                    if last and q >= 1:
                        continue
                    value = i * 4 + q
                    if not (isinstance(value, int) and value <= 0):
                        sp.wait_ge(s_yrow, value)
                    load_rows(i, q + 3)
            expert_body(0, False)
            with sp.Fori(1, MAXT // 4 - 1) as i:
                expert_body(i, False)
            expert_body(MAXT // 4 - 1, True)

        @block.gpsimd
        def _(pool):
            pool.memset(Y[:, :, :], 0.0).then_inc(s_init, 1)
            pool.memset(S[:, :, :], 0.0).then_inc(s_init, 1)
            pool.wait_ge(s_const, 16 * CONST_LOADS)

            def rsqrt(dst, src, n):
                return pool.tensor_tensor(dst, src, half_neg[:, 0:n], ALU.pow)

            def ln1(t):
                up_to(pool, s_mv, 1, t, 1)
                rsqrt(rstd[:, :], mv[:, 1:2], 1).then_inc(s_rstd, 1)

            def kscale_(t):
                up_to(pool, s_karg, 1, t, 1)
                rsqrt(kscale[:, :], karg[:, :], 2 * H).then_inc(s_kscale, 1)

            def init_inverse(t):
                par = t[1] % 2
                ident_h = ident.unsqueeze(1).broadcast_to([P, H, P])
                up_to(pool, s_wps, 1, before_(t, 2), 1)
                hold(pool)
                pool.tensor_copy(XT[:, par, :, :], ident_h).then_inc(s_Xi, 1)
                up_to(pool, s_yps, 12, before_(t, 1), 12)
                hold(pool)
                pool.tensor_copy(X[:, :, :], ident_h).then_inc(s_Xi, 1)

            def epilogue(t):
                up_to(pool, s_oarg, 1, t, 1)
                rsqrt(ors[:, :], oarg[:, :], H).then_inc(s_ors, 1)

            def epilogue2(t):
                up_to(pool, s_mv2, 1, t, 1)
                rsqrt(rstd2[:, :], mv2[:, 1:2], 1).then_inc(s_rstd2, 1)

            def copy_row(t):
                up_to(pool, s_xn2, 1, t, 1)
                hold(pool)
                s_ = t[1] % C
                pool.tensor_copy(rowB[:, s_, 0:D], rowA[:, s_, 0:D]).then_inc(s_rowB, 1)

            def scatter(b):
                pool.wait_ge(s_slot, b + 1)
                up_to(pool, s_rowB, 1, (b, 0), C)
                hold(pool)
                for c in range(C):
                    for k, rows in enumerate((rowA, rowB)):
                        pool.indirect_dma_start(
                            out=routed, out_offset=bass.IndirectOffsetOnAxis(ap=slot[:, k, c:c + 1], axis=0),
                            in_=rows[:, c, :], in_offset=None).then_inc(s_scat[c], 16)

            ln1((0, 0))
            kscale_((0, 0))
            init_inverse((0, 0))

            def body(b, first, last):
                for c in range(C):
                    t = (b, c)
                    if not (first and c == 0):
                        epilogue(before_(t, 1))
                    if not (last and c == C - 1):
                        ln1(after_(t))
                        kscale_(after_(t))
                    if c == 1 and not first:
                        scatter(b - 1)
                    if not (first and c == 0):
                        epilogue2(before_(t, 1))
                        copy_row(before_(t, 1))
                    if not (last and c == C - 1):
                        init_inverse(after_(t))
            sequences(pool, body)
            epilogue((B - 1, C - 1))
            epilogue2((B - 1, C - 1))
            copy_row((B - 1, C - 1))
            scatter(B - 1)
            pool.wait_ge(s_tail, 1)
            for e in range(E):
                pool.indirect_dma_start(
                    out=routed, out_offset=bass.IndirectOffsetOnAxis(ap=pad_idx[:, e:e + 1], axis=0),
                    in_=zrow[:, :], in_offset=None).then_inc(s_pads, 16)
            pool.dma_start(routed[SPARE:ROWS, :], zrow[:, :]).then_inc(s_pads, 16)
            pool.dma_start(out[B * N:B * N + P, :], zrow[:, 0:D]).then_inc(s_pads, 16)
            pool.wait_ge(s_pads, 16 * (E + 2))
            for c in range(C):
                pool.wait_ge(s_x1out[c], 16 * B)

            def accumulate(i, q):
                pool.wait_ge(s_yrow, i * 4 + (q + 1))
                value = i * 64 + 16 * q
                if not (isinstance(value, int) and value <= 0):
                    pool.wait_ge(s_acc, value)
                hold(pool)
                pool.indirect_dma_start(
                    out=out, out_offset=bass.IndirectOffsetOnAxis(ap=yidx[:, q:q + 1], axis=0),
                    in_=yrow[:, q % 2, :], in_offset=None, compute_op=ALU.add).then_inc(s_acc, 16)
            for q in range(4):
                accumulate(0, q)
            with pool.Fori(1, MAXT // 4) as i:
                for q in range(4):
                    accumulate(i, q)
            pool.wait_ge(s_acc, 16 * MAXT)

        @block.scalar
        def _(act):
            def evac(dst, src, scale=1.0):
                return act.activation(dst, src, ACT.Copy, scale=scale)

            def xnT_evac(t):
                up_to(act, s_qps, 1, before_(t, 1), 1)
                up_to(act, s_vgps, 1, before_(t, 1), 1)
                up_to(act, s_xnTp, 1, t, 1)
                evac(xnT[:, :, :].rearrange("p k n -> p (k n)"), p_xnT).then_inc(s_xnTs, 1)

            def k_square(t):
                up_to(act, s_karg, 1, before_(t, 1), 1)
                up_to(act, s_kps, 1, t, 1)
                act.activation(sq[:, :, :].rearrange("p h n -> p (h n)"), p_kv, ACT.Square).then_inc(s_ksq, 1)
                act.activation(eb[:, :], p_beta, ACT.Exp, scale=-1.0).then_inc(s_eb, 1)

            def q_evac(t):
                up_to(act, s_ops, 1, before_(t, 2), 1)
                up_to(act, s_qps, 1, t, 1)
                act.activation(KQ[:, t[1] % 2, :, 1, :], p_q, ACT.Copy,
                               scale=float(DK) ** -0.5).then_inc(s_qs, 1)

            def kT_evac(t):
                up_to(act, s_kTp, 1, t, 1)
                evac(KQ[:, t[1] % 2, :, 0, :], p_kT).then_inc(s_kTs, 1)

            def tanh_g(t):
                up_to(act, s_on, 1, before_(t, 2), 1)
                up_to(act, s_vgps, 1, t, 1)
                act.activation(gs[:, t[1] % 2, :, :], p_kv[:, 256:512].rearrange("p (h n) -> p h n", h=H), ACT.Tanh,
                               scale=0.5).then_inc(s_th, 1)

            def neg_gram(t, a):
                up_to(act, s_gram, 2, t, a + 1)
                evac(nG[:, t[1] % 2, 2 * a:2 * a + 2, :], p_gram[a][:, :, 0, :], -1.0).then_inc(s_nG, 1)

            def y_evac(t, lev):
                for a in range(2):
                    k = 2 * (lev - 1) + a + 1
                    up_to(act, s_yps, 12, t, k)
                    evac(even(Y[:, 2 * a:2 * a + 2, :], lev), packed(p_y[a], lev)).then_inc(s_ys, 1)

            def w_evac(t):
                up_to(act, s_ops, 1, before_(t, 1), 1)
                up_to(act, s_s, 1, before_(t, 1), 1)
                up_to(act, s_wps, 1, t, 1)
                evac(W[:, :, :], p_p).then_inc(s_ws, 1)

            def o_square(t):
                up_to(act, s_on, 1, before_(t, 1), 1)
                up_to(act, s_ops, 1, t, 1)
                act.activation(osq[:, :, :], p_o, ACT.Square).then_inc(s_osq, 1)

            def oT_evac(t):
                up_to(act, s_oTp, 1, t, 1)
                evac(oT[:, :, :].rearrange("p k n -> p (k n)"), p_oT).then_inc(s_oTs, 1)

            def xn2T_evac(t):
                up_to(act, s_xn2Tp, 1, t, 1)
                evac(xn2T[:, :, :].rearrange("p k n -> p (k n)"), p_xn2T).then_inc(s_xn2Ts, 1)

            def split_hi(b, c):
                for q, dst in enumerate((w1_hi, w2_hi)):
                    act.wait_ge(s_w[q], b * (16 * C) + 16 * (c + 1))
                    evac(dst[:, bass.ds(b * (C * PIECE) + c * PIECE, PIECE)], wst[:, q, :], W_SCALE).then_inc(s_whi, 1)

            def route_exp(b):
                act.wait_ge(s_rd, b + 1)
                act.activation(r8[1][:, :, :], r8[0][:, :, :], ACT.Exp).then_inc(s_rexp, 1)

            act.wait_ge(s_const, 16 * CONST_LOADS)
            act.wait_ge(s_init, 2)
            xnT_evac((0, 0))
            k_square((0, 0))
            q_evac((0, 0))
            kT_evac((0, 0))
            tanh_g((0, 0))
            for a in range(2):
                neg_gram((0, 0), a)

            def body(b, first, last):
                for c in range(C):
                    t = (b, c)
                    front, epi = not (last and c == C - 1), not (first and c == 0)
                    nxt, prv = after_(t), before_(t, 1)
                    y_evac(t, 1)
                    if front:
                        xnT_evac(nxt)
                        k_square(nxt)
                    y_evac(t, 2)
                    if epi:
                        oT_evac(prv)
                    y_evac(t, 3)
                    if front:
                        q_evac(nxt)
                    y_evac(t, 4)
                    if front:
                        kT_evac(nxt)
                        tanh_g(nxt)
                    y_evac(t, 5)
                    y_evac(t, 6)
                    if epi:
                        xn2T_evac(prv)
                    if front:
                        neg_gram(nxt, 0)
                        neg_gram(nxt, 1)
                    w_evac(t)
                    split_hi(b, c)
                    o_square(t)
                    if c == 0 and not first:
                        route_exp(b - 1)
            sequences(act, body)
            last_tile = (B - 1, C - 1)
            oT_evac(last_tile)
            xn2T_evac(last_tile)
            route_exp(B - 1)

            def xT_hi(i, q):
                act.wait_ge(s_gTp, i * 4 + (q + 1))
                if not (isinstance(i, int) and i * 4 + q < 2):
                    act.wait_ge(s_hps, i * 8 + 2 * (q - 1))
                evac(xTh[:, q % 2, :, :], p_gT[q % 2].rearrange("p (k n) -> p k n", k=KC)).then_inc(s_gTh, 1)

            def hidden(i, q):
                for m in range(2):
                    act.wait_ge(s_hps, i * 8 + (2 * q + m + 1))
                    if not (isinstance(i, int) and i * 4 + q < 2):
                        act.wait_ge(s_hlo, i * 8 + (2 * (q - 2) + m + 1))
                        act.wait_ge(s_yops, i * 4 + (q - 1))
                    cols = slice(512 * m, 512 * m + 512)
                    act.activation(hf[:, q % 2, cols], p_h[q % 2][m][:, :], ACT.Gelu,
                                   scale=1.0 / W_SCALE).then_inc(s_gelu, 1)
                    act.wait_ge(s_gelu, i * 8 + (2 * q + m + 1))
                    evac(hhi[:, q % 2, cols], hf[:, q % 2, cols], H_SCALE).then_inc(s_hhi, 1)

            xT_hi(0, 0)
            xT_hi(0, 1)
            hidden(0, 0)

            def expert_body(i, last):
                for q in range(4):
                    if not (last and q >= 2):
                        xT_hi(i, q + 2)
                    if not (last and q == 3):
                        hidden(i, q + 1)
            expert_body(0, False)
            with act.Fori(1, MAXT // 4 - 1) as i:
                expert_body(i, False)
            expert_body(MAXT // 4 - 1, True)

        @block.tensor
        def _(pe):
            def mm(dst, lhsT, rhs, start=True, stop=True):
                return pe.matmul(dst, lhsT, rhs, start=start, stop=stop)

            def xnT_make(t):
                up_to(pe, s_AT, 2, before_(t, 1), 2)
                up_to(pe, s_xn, 1, t, 1)
                for k in range(KC):
                    last = pe.transpose(p_xnT[:, k * P:(k + 1) * P], xn[:, k * P:(k + 1) * P], ident)
                last.then_inc(s_xnTp, 1)

            def k_proj(t):
                up_to(pe, s_gs, 1, before_(t, 1), 1)
                up_to(pe, s_xnTs, 1, t, 1)
                up_to(pe, s_lg, 1, before_(t, 3), 1)
                for k in range(KC):
                    mm(p_beta, xnT[:, k, :], wb_s[:, k, :], k == 0, k == KC - 1)
                for k in range(KC):
                    last = mm(p_kv, xnT[:, k, :], wk_s[:, k, :], k == 0, k == KC - 1)
                last.then_inc(s_kps, 1)

            def q_proj(t, a):
                if a == 0:
                    up_to(pe, s_on, 1, before_(t, 2), 1)
                for h in range(2 * a, 2 * a + 2):
                    for k in range(KC):
                        last = mm(p_q[:, h, :], wq_s[:, k, h * DK:(h + 1) * DK], xnT[:, k, :], k == 0, k == KC - 1)
                if a == 1:
                    last.then_inc(s_qps, 1)

            def k_transposes(t):
                up_to(pe, s_AT, 2, before_(t, 1), 2)
                up_to(pe, s_nG, 2, before_(t, 1), 2)
                up_to(pe, s_kp, 1, t, 1)
                for h in range(H):
                    last = pe.transpose(p_kT[:, h, :], Kp[:, t[1] % 2, h, :], ident)
                last.then_inc(s_kTp, 1)

            def vg_proj(t):
                up_to(pe, s_kp, 1, t, 1)
                for k in range(KC):
                    last = mm(p_kv, xnT[:, k, :], wvg_s[:, k, :], k == 0, k == KC - 1)
                last.then_inc(s_vgps, 1)

            def gram(t, a, ranked=None):
                up_to(pe, s_kTs, 1, t, 1)
                up_to(pe, s_qs, 1, t, 1)
                if ranked is not None:
                    pe.wait_ge(s_slot, ranked)
                for h in range(2):
                    hh = KQ[:, t[1] % 2, 2 * a + h, :, :]
                    last = mm(p_gram[a][:, h, :, :], hh[:, 0, :], hh)
                last.then_inc(s_gram, 1)

            def y_make(t, lev):
                for a in range(2):
                    if lev == 1:
                        up_to(pe, s_X0, 1, t, 1)
                    else:
                        up_to(pe, s_xup, 12, t, 2 * (lev - 2) + a + 1)
                    for h in range(2):
                        last = mm(packed(p_y[a], lev)[:, h], nG[:, t[1] % 2, 2 * a + h, :],
                                  even(X[:, 2 * a:2 * a + 2, :], lev)[:, h])
                    last.then_inc(s_yps, 1)

            def x_make(t, lev):
                for a in range(2):
                    up_to(pe, s_ys, 12, t, 2 * (lev - 1) + a + 1)
                    XTa = XT[:, t[1] % 2, 2 * a:2 * a + 2, :]
                    for h in range(2):
                        if lev < LEVELS - 1:
                            mm(packed(p_x[a], lev)[:, h], XTa[:, h, :], even(Y[:, 2 * a:2 * a + 2, :], lev)[:, h])
                        last = mm(packed(p_xt[a], lev)[:, h], Y[:, 2 * a + h, :], odd(XTa, lev)[:, h])
                    last.then_inc(s_xps, 1)

            def p_make(t):
                up_to(pe, s_ws, 1, before_(t, 1), 1)
                up_to(pe, s_s, 1, before_(t, 1), 1)
                for h in range(H):
                    last = mm(p_p[:, h, :], KQ[:, t[1] % 2, h, 0, :], S[:, h, :])
                last.then_inc(s_pps, 1)

            def w_make(t):
                up_to(pe, s_r, 1, t, 1)
                up_to(pe, s_xup, 12, t, 12)
                for h in range(H):
                    last = mm(p_p[:, h, :], XT[:, t[1] % 2, h, :], R[:, h, :])
                last.then_inc(s_wps, 1)

            def out_make(t, final):
                up_to(pe, s_qs, 1, t if final else after_(t), 1)
                up_to(pe, s_ws, 1, t, 1)
                up_to(pe, s_AT, 2, t, 2)
                par = t[1] % 2
                if final:
                    up_to(pe, s_on, 1, before_(t, 1), 1)
                if t[1] < C - 1:
                    for h in range(H):
                        last = mm(p_u[:, h, :], Kp[:, par, h, :], W[:, h, :])
                    last.then_inc(s_ups, 1)
                for h in range(H):
                    mm(p_o[:, h, :], KQ[:, par, h, 1, :], S[:, h, :], True, False)
                    last = mm(p_o[:, h, :], AT[:, par, h, :], W[:, h, :], False, True)
                last.then_inc(s_ops, 1)

            def oT_make(t, beta_tile):
                up_to(pe, s_eb, 1, beta_tile, 1)
                up_to(pe, s_oTs, 1, before_(t, 1), 1)
                up_to(pe, s_on, 1, t, 1)
                for k in range(KC):
                    last = pe.transpose(p_oT[:, k * P:(k + 1) * P], oo[:, 2 * k:2 * k + 2, :].rearrange("p h n -> p (h n)"), ident)
                last.then_inc(s_oTp, 1)

            def wo_make(t):
                up_to(pe, s_oTs, 1, t, 1)
                for k in range(KC):
                    last = mm(p_wo, oT[:, k, :], wo_s[:, k, :], k == 0, k == KC - 1)
                last.then_inc(s_wops, 1)

            def xn2T_make(t):
                up_to(pe, s_xn2, 1, t, 1)
                for k in range(KC):
                    last = pe.transpose(p_xn2T[:, k * P:(k + 1) * P], rowA[:, t[1] % C, k * P:(k + 1) * P], ident)
                last.then_inc(s_xn2Tp, 1)

            def logits_make(t):
                up_to(pe, s_lg, 1, before_(t, 1), 1)
                up_to(pe, s_xn2Ts, 1, t, 1)
                for k in range(KC):
                    last = mm(p_lg, xn2T[:, k, :], router_s[:, k, :], k == 0, k == KC - 1)
                last.then_inc(s_lgps, 1)

            def rank(b):
                pe.wait_ge(s_both, b + 1)
                m = both[:, :, :].rearrange("p c e -> p (c e)")
                mm(p_rank, before, m)
                mm(p_tot, ones, m).then_inc(s_rank, 1)

            pe.wait_ge(s_const, 16 * CONST_LOADS)
            pe.wait_ge(s_init, 2)
            t0 = (0, 0)
            xnT_make(t0)
            k_proj(t0)
            q_proj(t0, 0)
            q_proj(t0, 1)
            k_transposes(t0)
            vg_proj(t0)
            gram(t0, 0)
            gram(t0, 1)

            def body(b, first, last):
                for c in range(C):
                    t = (b, c)
                    front, epi = not (last and c == C - 1), not (first and c == 0)
                    nxt, prv = after_(t), before_(t, 1)
                    y_make(t, 1)
                    p_make(t)
                    if front:
                        xnT_make(nxt)
                    x_make(t, 1)
                    if front:
                        k_proj(nxt)
                    y_make(t, 2)
                    if epi:
                        oT_make(prv, nxt if front else t)
                    x_make(t, 2)
                    if c == 1 and not first:
                        up_to(pe, s_xnTs, 1, nxt, 1)
                        rank(b - 1)
                    if front:
                        q_proj(nxt, 0)
                    y_make(t, 3)
                    if epi:
                        wo_make(prv)
                    x_make(t, 3)
                    if front:
                        q_proj(nxt, 1)
                    y_make(t, 4)
                    if front:
                        k_transposes(nxt)
                    x_make(t, 4)
                    if front:
                        vg_proj(nxt)
                    y_make(t, 5)
                    x_make(t, 5)
                    if epi:
                        xn2T_make(prv)
                    y_make(t, 6)
                    if front:
                        gram(nxt, 0)
                    x_make(t, 6)
                    if front:
                        gram(nxt, 1, b if c == 1 and not first else None)
                    w_make(t)
                    if epi:
                        logits_make(prv)
                    out_make(t, last and c == C - 1)
            sequences(pe, body)
            last_tile = (B - 1, C - 1)
            oT_make(last_tile, last_tile)
            wo_make(last_tile)
            xn2T_make(last_tile)
            logits_make(last_tile)
            rank(B - 1)

            pe.wait_ge(s_tab, 16)
            pe.wait_ge(s_whi, 2 * T)
            pe.wait_ge(s_wlo, 2 * T)
            pe.wait_ge(s_slot, B)

            def xT_make(i, q):
                pe.wait_ge(s_xg[q % 4], i * 16 + 16 * (q // 4 + 1))
                if not (isinstance(i, int) and i * 4 + q < 2):
                    pe.wait_ge(s_gTl, i * 4 + (q - 1))
                for k in range(KC):
                    last = pe.transpose(p_gT[q % 2][:, k * P:(k + 1) * P],
                                        xg[:, q % 4, k * P:(k + 1) * P], ident)
                last.then_inc(s_gTp, 1)

            def expert_of(i, q):
                return pe.value_load(tab[0:1, bass.ds(i * 8 + 2 * q, 1)], min_val=0, max_val=E - 1)

            def up(i, q):
                e = expert_of(i, q)
                pe.wait_ge(s_gTh, i * 4 + (q + 1))
                pe.wait_ge(s_gTl, i * 4 + (q + 1))
                hi, lo = xTh[:, q % 2, :, :], xTl[:, q % 2, :, :]
                for m in range(KH):
                    if m % 4 == 0 and not (isinstance(i, int) and i * 4 + q < 2):
                        pe.wait_ge(s_gelu, i * 8 + (2 * (q - 2) + m // 4 + 1))
                    dst = p_h[q % 2][m // 4][:, (m % 4) * P:(m % 4 + 1) * P]
                    for k in range(KC):
                        off = e * HID + (k * E * HID + m * P)
                        wh, wl = w1_hi[:, bass.ds(off, P)], w1_lo[:, bass.ds(off, P)]
                        mm(dst, wh, hi[:, k, :], k == 0, False)
                        mm(dst, wh, lo[:, k, :], False, False)
                        last = mm(dst, wl, hi[:, k, :], False, k == KC - 1)
                    if m % 4 == 3:
                        last.then_inc(s_hps, 1)

            def down(i, q):
                e = expert_of(i, q)
                dst = p_yo[q % 2]
                if not (isinstance(i, int) and i * 4 + q < 2):
                    pe.wait_ge(s_yrow, i * 4 + (q - 1))
                for m in range(KH):
                    if m % 4 == 0:
                        pe.wait_ge(s_hhi, i * 8 + (2 * q + m // 4 + 1))
                        pe.wait_ge(s_hlo, i * 8 + (2 * q + m // 4 + 1))
                    off = e * D + m * E * D
                    wh, wl = w2_hi[:, bass.ds(off, D)], w2_lo[:, bass.ds(off, D)]
                    cols = slice(m * P, (m + 1) * P)
                    mm(dst, hhi[:, q % 2, cols], wh, m == 0, False)
                    mm(dst, hhi[:, q % 2, cols], wl, False, False)
                    last = mm(dst, hlo[:, q % 2, cols], wh, False, m == KH - 1)
                last.then_inc(s_yops, 1)

            xT_make(0, 0)
            xT_make(0, 1)
            up(0, 0)

            def expert_body(i, last):
                for q in range(4):
                    if not (last and q >= 2):
                        xT_make(i, q + 2)
                    if not (last and q == 3):
                        up(i, q + 1)
                    down(i, q)
            expert_body(0, False)
            with pe.Fori(1, MAXT // 4 - 1) as i:
                expert_body(i, False)
            expert_body(MAXT // 4 - 1, True)

        @block.vector
        def _(dve):
            class Own:
                base, n = 0, 0

            def step(ins):
                Own.n += 1
                ins.then_inc(s_dve, 1)

            def settled():
                dve.wait_ge(s_dve, Own.base + Own.n)

            def link(ins):
                step(ins)
                settled()

            def ln1_stats(t):
                b, c = t
                dve.wait_ge(s_x[c % C], (b + c // C) * 16 + 16)
                link(dve.bn_stats(st6[:, :], x_s[:, c % C, :]))
                hold(dve)
                link(dve.bn_aggr(mv[:, :], st6[:, :]))
                dve.tensor_scalar(mv[:, 1:2], mv[:, 1:2], EPS, None, ALU.add).then_inc(s_mv, 1)

            def ln1(t):
                up_to(dve, s_rstd, 1, t, 1)
                up_to(dve, s_xnTp, 1, before_(t, 1), 1)
                dve.tensor_scalar(xn[:, :], x_s[:, t[1] % C, :], mv[:, 0:1], rstd[:, 0:1],
                                  ALU.subtract, ALU.mult).then_inc(s_xn, 1)

            def k_norm(t):
                up_to(dve, s_ksq, 1, t, 1)
                up_to(dve, s_eb, 1, t, 1)
                link(dve.tensor_reduce(ks[:, 0:H], sq[:, :, :], AX.X, ALU.add))
                step(dve.tensor_scalar(karg[:, H:2 * H], eb[:, :], 1.0, None, ALU.add))
                link(dve.tensor_scalar(ks[:, H:2 * H], ks[:, 0:H], 1e-12, None, ALU.add))
                dve.tensor_tensor(karg[:, 0:H], ks[:, H:2 * H], karg[:, H:2 * H], ALU.mult).then_inc(s_karg, 1)

            def k_prime(t):
                up_to(dve, s_ops, 1, before_(t, 2), 1)
                up_to(dve, s_kscale, 1, t, 1)
                dve.tensor_tensor(Kp[:, t[1] % 2, :, :], p_kv.rearrange("p (h n) -> p h n", h=H),
                                  col(kscale[:, 0:H], DK), ALU.mult).then_inc(s_kp, 1)

            def v_gate(t):
                up_to(dve, s_vgps, 1, t, 1)
                up_to(dve, s_th, 1, t, 1)
                par = t[1] % 2
                v, g = p_kv[:, 0:256].rearrange("p (h n) -> p h n", h=H), p_kv[:, 256:512].rearrange("p (h n) -> p h n", h=H)
                step(dve.tensor_tensor(Vp[:, par, :, :], v, col(kscale[:, H:2 * H], DV), ALU.mult))
                link(dve.scalar_tensor_tensor(gs[:, par, :, :], gs[:, par, :, :], 1.0, g, ALU.add, ALU.mult))
                dve.tensor_tensor(gs[:, par, :, :], gs[:, par, :, :], normw_s[:, :].unsqueeze(1).broadcast_to([P, H, DV]),
                                  ALU.mult).then_inc(s_gs, 1)

            def masked_scores(t, a):
                up_to(dve, s_ops, 1, before_(t, 2), 1)
                up_to(dve, s_nG, 2, t, a + 1)
                dve.tensor_tensor(AT[:, t[1] % 2, 2 * a:2 * a + 2, :], p_gram[a][:, :, 1, :],
                                  causal.unsqueeze(1).broadcast_to([P, 2, P]), ALU.mult).then_inc(s_AT, 1)

            def level_one(t):
                up_to(dve, s_Xi, 2, t, 2)
                up_to(dve, s_nG, 2, t, 2)
                hold(dve)
                par = t[1] % 2
                dve.copy_predicated(even(X[:, :, :], 0), level_mask(0, 0, H), even(nG[:, par, :, :], 0))
                dve.copy_predicated(odd(XT[:, par, :, :], 0), level_mask(0, 1, H), odd(nG[:, par, :, :], 0)).then_inc(s_X0, 1)

            def level_update(t, lev):
                for a in range(2):
                    up_to(dve, s_xps, 12, t, 2 * (lev - 1) + a + 1)
                    hold(dve)
                    if lev < LEVELS - 1:
                        dve.copy_predicated(even(X[:, 2 * a:2 * a + 2, :], lev), level_mask(lev, 0, 2), packed(p_x[a], lev))
                    dve.copy_predicated(odd(XT[:, t[1] % 2, 2 * a:2 * a + 2, :], lev), level_mask(lev, 1, 2),
                                        packed(p_xt[a], lev)).then_inc(s_xup, 1)

            def r_make(t):
                up_to(dve, s_wps, 1, before_(t, 1), 1)
                up_to(dve, s_pps, 1, t, 1)
                dve.tensor_tensor(R[:, :, :], Vp[:, t[1] % 2, :, :], p_p, ALU.subtract).then_inc(s_r, 1)

            def state(t):
                up_to(dve, s_ops, 1, t, 1)
                if t[1] < C - 1:
                    dve.wait_ge(s_ups, t[0] * (C - 1) + (t[1] + 1))
                    dve.tensor_tensor(S[:, :, :], S[:, :, :], p_u, ALU.add).then_inc(s_s, 1)
                else:
                    dve.memset(S[:, :, :], 0.0).then_inc(s_s, 1)

            def o_scale(t):
                up_to(dve, s_osq, 1, t, 1)
                link(dve.tensor_reduce(osum[:, :], osq[:, :, :], AX.X, ALU.add))
                dve.tensor_scalar(oarg[:, :], osum[:, :], 1.0 / DV, EPS, ALU.mult, ALU.add).then_inc(s_oarg, 1)

            def o_norm(t):
                up_to(dve, s_ors, 1, t, 1)
                up_to(dve, s_oTp, 1, before_(t, 1), 1)
                link(dve.tensor_tensor(osq[:, :, :], p_o, col(ors[:, :], DV), ALU.mult))
                dve.tensor_tensor(oo[:, :, :], osq[:, :, :], gs[:, t[1] % 2, :, :], ALU.mult).then_inc(s_on, 1)

            def residual(t):
                up_to(dve, s_wops, 1, t, 1)
                s_ = t[1] % C
                dve.tensor_tensor(x_s[:, s_, :], x_s[:, s_, :], p_wo, ALU.add).then_inc(s_res, 1)
                up_to(dve, s_res, 1, t, 1)
                link(dve.bn_stats(st6b[:, :], x_s[:, s_, :]))
                hold(dve)
                link(dve.bn_aggr(mv2[:, :], st6b[:, :]))
                dve.tensor_scalar(mv2[:, 1:2], mv2[:, 1:2], EPS, None, ALU.add).then_inc(s_mv2, 1)

            def ln2(t, scattered):
                s_ = t[1] % C
                if scattered is not None:
                    dve.wait_ge(s_scat[s_], scattered)
                up_to(dve, s_rstd2, 1, t, 1)
                dve.tensor_scalar(rowA[:, s_, 0:D], x_s[:, s_, :], mv2[:, 0:1], rstd2[:, 0:1],
                                  ALU.subtract, ALU.mult).then_inc(s_xn2, 1)

            def logits_copy(t):
                up_to(dve, s_lgps, 1, t, 1)
                dve.tensor_copy(logits[:, t[1] % C, :], p_lg).then_inc(s_lg, 1)

            def split_lo(b, c):
                for q, (hi, lo) in enumerate(((w1_hi, w1_lo), (w2_hi, w2_lo))):
                    dve.wait_ge(s_whi, b * (2 * C) + (2 * c + q + 1))
                    at = bass.ds(b * (C * PIECE) + c * PIECE, PIECE)
                    dve.scalar_tensor_tensor(lo[:, at], wst[:, q, :], W_SCALE, hi[:, at],
                                             ALU.mult, ALU.subtract).then_inc(s_wlo, 1)

            def route_masks(b):
                diff, ex, a0, a1, a2, a3 = r8[0:6]
                m1, tm, m2, ssum, g1, g2, g2s = r1[0:7]
                dve.wait_ge(s_lg, b * C + C)
                link(dve.tensor_reduce(m1[:, :], logits[:, :, :], AX.X, ALU.max))
                dve.tensor_tensor(diff[:, :, :], logits[:, :, :], col(m1[:, :], E), ALU.subtract).then_inc(s_rd, 1)
                dve.wait_ge(s_rd, b + 1)
                pref_c = pref.unsqueeze(1).broadcast_to([P, C, E])
                link(dve.scalar_tensor_tensor(a0[:, :, :], diff[:, :, :], 0.0, pref_c, ALU.is_equal, ALU.mult))
                link(dve.tensor_reduce(tm[:, :], a0[:, :, :], AX.X, ALU.max))
                link(dve.tensor_tensor(first[:, :, :], a0[:, :, :], col(tm[:, :], E), ALU.is_equal))
                link(dve.scalar_tensor_tensor(a1[:, :, :], first[:, :, :], -1e30, diff[:, :, :], ALU.mult, ALU.add))
                link(dve.tensor_reduce(m2[:, :], a1[:, :, :], AX.X, ALU.max))
                link(dve.tensor_tensor(a2[:, :, :], a1[:, :, :], col(m2[:, :], E), ALU.is_equal))
                link(dve.tensor_tensor(a3[:, :, :], a2[:, :, :], pref_c, ALU.mult))
                link(dve.tensor_reduce(tm[:, :], a3[:, :, :], AX.X, ALU.max))
                link(dve.tensor_tensor(second[:, :, :], a3[:, :, :], col(tm[:, :], E), ALU.is_equal))
                dve.tensor_tensor(both[:, :, :], first[:, :, :], second[:, :, :], ALU.add).then_inc(s_both, 1)
                dve.wait_ge(s_rexp, b + 1)
                link(dve.tensor_reduce(ssum[:, :], ex[:, :, :], AX.X, ALU.add))
                link(dve.tensor_tensor(a0[:, :, :], ex[:, :, :], second[:, :, :], ALU.mult))
                link(dve.tensor_reduce(g2[:, :], a0[:, :, :], AX.X, ALU.add))
                link(dve.reciprocal(g1[:, :], ssum[:, :]))
                link(dve.tensor_tensor(g2s[:, :], g2[:, :], g1[:, :], ALU.mult))
                step(dve.tensor_copy(rowA[:, :, D], g1[:, :]))
                step(dve.tensor_copy(rowB[:, :, D], g2s[:, :]))
                ids = fc[:, bass.ds(b * C + 529, C)]
                step(dve.tensor_copy(rowA[:, :, D + 1], ids))
                link(dve.tensor_copy(rowB[:, :, D + 1], ids))

            def route_slots(b, wait_scattered):
                dve.wait_ge(s_rank, b + 1)
                step(dve.tensor_copy(rbase[:, 0, :], run[:, :]))
                for c in range(C):
                    settled()
                    dst = rbase[:, c + 1, :] if c < C - 1 else run[:, :]
                    step(dve.tensor_tensor(dst, rbase[:, c, :], p_tot[:, c * E:(c + 1) * E], ALU.add))
                settled()
                link(dve.tensor_tensor(pos[:, :, :], rbase[:, :, :], p_rank.rearrange("p (c e) -> p c e", c=C), ALU.add))
                if wait_scattered is not None:
                    for c in range(C):
                        dve.wait_ge(s_scat[c], wait_scattered)
                for k, m in enumerate((first, second)):
                    link(dve.tensor_tensor(r8[6 + k][:, :, :], pos[:, :, :], m[:, :, :], ALU.mult))
                    link(dve.tensor_reduce(r1[k][:, :], r8[6 + k][:, :, :], AX.X, ALU.add))
                    last = dve.tensor_copy(slot[:, k, :], r1[k][:, :])
                    if k == 0:
                        step(last)
                last.then_inc(s_slot, 1)

            dve.wait_ge(s_const, 16 * CONST_LOADS)
            dve.wait_ge(s_init, 2)
            step(dve.tensor_scalar(normw_s[:, :], normw_s[:, :], 0.5, None, ALU.mult))
            step(dve.tensor_copy(mask_s[:, :, :].rearrange("p a b -> p (a b)"), mask_in))
            link(dve.tensor_copy(run[:, :], region))
            t0 = (0, 0)
            ln1_stats(t0)
            ln1(t0)
            k_norm(t0)
            k_prime(t0)
            v_gate(t0)
            masked_scores(t0, 0)
            masked_scores(t0, 1)
            level_one(t0)

            def body(b, first_, last_):
                for c in range(C):
                    t = (b, c)
                    front, epi = not (last_ and c == C - 1), not (first_ and c == 0)
                    nxt, prv = after_(t), before_(t, 1)
                    if epi:
                        o_scale(prv)
                    if front:
                        ln1_stats(nxt)
                    r_make(t)
                    if epi:
                        o_norm(prv)
                    if front:
                        ln1(nxt)
                    level_update(t, 1)
                    if front:
                        k_norm(nxt)
                    level_update(t, 2)
                    if c == 1 and not first_:
                        route_slots(b - 1, None if isinstance(b, int) and b == 1 else (b - 1) * 32)
                    if front:
                        k_prime(nxt)
                    level_update(t, 3)
                    if epi:
                        residual(prv)
                    level_update(t, 4)
                    if epi:
                        ln2(prv, None if first_ or (c == 0 and isinstance(b, int) and b == 1) else (b * 32 if c > 0 else (b - 1) * 32))
                    if front:
                        v_gate(nxt)
                    level_update(t, 5)
                    if front:
                        masked_scores(nxt, 0)
                    level_update(t, 6)
                    if front:
                        masked_scores(nxt, 1)
                        level_one(nxt)
                    if epi:
                        logits_copy(prv)
                    state(t)
                    split_lo(b, c)
                    if c == 0 and not first_:
                        route_masks(b - 1)

            start = Own.n
            body(0, True, False)
            per_seq = OWN_PER_SEQ
            first_n = Own.n
            with dve.Fori(1, B - 1) as b:
                Own.base, Own.n = first_n - per_seq + b * per_seq, 0
                body(b, False, False)
                assert Own.n == per_seq, Own.n
            Own.base, Own.n = first_n + (B - 2) * per_seq, 0
            body(B - 1, False, True)
            last_tile = (B - 1, C - 1)
            o_scale(last_tile)
            o_norm(last_tile)
            residual(last_tile)
            ln2(last_tile, 32 * (B - 1))
            logits_copy(last_tile)
            route_masks(B - 1)
            route_slots(B - 1, 32 * (B - 1))

            cnt, ntf, cum, prev, ge, oneh, rw, tmp = t8
            settled()
            step(dve.memset(zrow[:, 0:D + 1], 0.0))
            step(dve.tensor_scalar(zrow[:, D + 1:D + 2], lane, float(B * N), None, ALU.add))
            link(dve.tensor_tensor(cnt[:, :], run[:, :], region, ALU.subtract))
            step(dve.tensor_scalar(pad_idx[:, :], run[:, :], lane, None, ALU.add))
            link(dve.tensor_scalar(t8i[:, :], cnt[:, :], float(P - 1), None, ALU.add))
            link(dve.tensor_scalar(t8j[:, :], t8i[:, :], 7, None, ALU.arith_shift_right))
            link(dve.tensor_copy(ntf[:, :], t8j[:, :]))
            link(dve.tensor_tensor_scan(cum[:, :], ones[:, 0:E], ntf[:, :], 0.0, ALU.mult, ALU.add))
            link(dve.tensor_tensor(prev[:, :], cum[:, :], ntf[:, :], ALU.subtract))
            link(dve.tensor_scalar(ge[:, :], cum[:, :], lane, None, ALU.is_le))
            step(dve.tensor_scalar(oneh[:, 0:1], ge[:, 0:1], -1.0, 1.0, ALU.mult, ALU.add))
            step(dve.tensor_tensor(oneh[:, 1:E], ge[:, 0:E - 1], ge[:, 1:E], ALU.subtract))
            link(dve.tensor_scalar(rw[:, :], prev[:, :], lane, -float(P), ALU.subtract, ALU.mult))
            link(dve.tensor_tensor(tmp[:, :], rw[:, :], region, ALU.add))
            link(dve.tensor_tensor(rw[:, :], tmp[:, :], oneh[:, :], ALU.mult))
            step(dve.tensor_reduce(tab_f[:, 0:1], ge[:, 0:E - 1], AX.X, ALU.add))
            link(dve.tensor_reduce(cnt[:, 0:1], rw[:, :], AX.X, ALU.add))
            link(dve.scalar_tensor_tensor(tab_f[:, 1:2], ge[:, E - 1:E], float(SPARE), cnt[:, 0:1], ALU.mult, ALU.add))
            dve.tensor_copy(tab_i[:, :], tab_f[:, :]).then_inc(s_tail, 1)

            def xT_lo(i, q):
                dve.wait_ge(s_gTh, i * 4 + (q + 1))
                dve.tensor_tensor(xTl[:, q % 2, :, :], p_gT[q % 2].rearrange("p (k n) -> p k n", k=KC),
                                  xTh[:, q % 2, :, :], ALU.subtract).then_inc(s_gTl, 1)

            def hidden_lo(i, q):
                for m in range(2):
                    dve.wait_ge(s_hhi, i * 8 + (2 * q + m + 1))
                    cols = slice(512 * m, 512 * m + 512)
                    dve.scalar_tensor_tensor(hlo[:, q % 2, cols], hf[:, q % 2, cols], H_SCALE, hhi[:, q % 2, cols],
                                             ALU.mult, ALU.subtract).then_inc(s_hlo, 1)

            def rows_out(i, q):
                dve.wait_ge(s_yops, i * 4 + (q + 1))
                if not (isinstance(i, int) and i * 4 + q < 2):
                    dve.wait_ge(s_acc, i * 64 + 16 * (q - 1))
                dve.tensor_copy(yidx[:, q:q + 1], xg[:, q, D + 1:D + 2])
                dve.tensor_scalar(yrow[:, q % 2, :], p_yo[q % 2], xg[:, q, D:D + 1],
                                  1.0 / (W_SCALE * H_SCALE), ALU.mult, ALU.mult).then_inc(s_yrow, 1)

            dve.wait_ge(s_xg[0], 16)
            xT_lo(0, 0)
            xT_lo(0, 1)
            hidden_lo(0, 0)

            def expert_body(i, last):
                for q in range(4):
                    if not (last and q >= 2):
                        xT_lo(i, q + 2)
                    if not (last and q == 3):
                        hidden_lo(i, q + 1)
                    rows_out(i, q)
            expert_body(0, False)
            with dve.Fori(1, MAXT // 4 - 1) as i:
                expert_body(i, False)
            expert_body(MAXT // 4 - 1, True)


FCONST = 577
CONST_LOADS = 9
OWN_PER_SEQ = 74


def constants():
    import numpy as np
    f = np.zeros((P, FCONST), np.float32)
    j, i = np.arange(P)[:, None], np.arange(P)[None, :]
    f[:, 0:128] = j == i
    f[:, 128:256] = j <= i
    f[:, 256:384] = j < i
    f[:, 384:512] = 1.0
    f[:, 512:520] = E - np.arange(E)
    f[:, 520:528] = REGION * np.arange(E)
    f[:, 528] = np.arange(P)
    f[:, 529:529 + T] = P * np.arange(T)[None, :] + j
    f[:, 561:577] = -0.5
    m = np.zeros((P, 2 * LEVELS, 64), np.int32)
    for lev in range(LEVELS):
        s = 1 << lev
        lower = (j // s == i // s + 1) & ((i // s) % 2 == 0)
        m[:, 2 * lev, :] = lower.reshape(P, -1, 2, s)[:, :, 0, :].reshape(P, 64)
        m[:, 2 * lev + 1, :] = lower.T.reshape(P, -1, 2, s)[:, :, 1, :].reshape(P, 64)
    return f, m


def kernel(**inputs):
    import numpy as np
    import concourse.bacc as bacc
    from concourse.bass_utils import run_bass_kernel_spmd

    g = {k: np.asarray(v) for k, v in inputs.items()}
    fconst, iconst = constants()
    w1 = g["L0_ffn_w1"].transpose(2, 0, 1).reshape(KC, P, T // KC, PIECE).transpose(0, 2, 1, 3).reshape(T, P, PIECE)
    w2 = g["L0_ffn_w2"].transpose(2, 0, 1).reshape(KH, P, T // KH, PIECE).transpose(0, 2, 1, 3).reshape(T, P, PIECE)
    arrays = {
        "x": g["L0_attn_x"].reshape(T, P, D),
        "wq": g["L0_attn_Wq"], "wk": g["L0_attn_Wk"],
        "wvg": np.concatenate([g["L0_attn_Wv"], g["L0_attn_Wg"]], axis=1),
        "wb": g["L0_attn_Wb"], "wo": g["L0_attn_Wo"], "norm_w": g["L0_attn_norm_w"],
        "router": g["L0_ffn_router_w"].T,
        "w1": w1, "w2": w2, "fconst": fconst, "iconst": iconst,
    }
    arrays = {k: np.ascontiguousarray(v) for k, v in arrays.items()}
    nc = bacc.Bacc("TRN2", target_bir_lowering=False, num_devices=1)
    args = [nc.dram_tensor(k, a.shape, mybir.dt.from_np(a.dtype), kind="ExternalInput").ap() for k, a in arrays.items()]
    out = nc.dram_tensor("out", (B * N + P, D), mybir.dt.float32, kind="ExternalOutput").ap()
    build(nc, *args, out)
    r = run_bass_kernel_spmd(nc, [arrays], core_ids=[0])
    return r.results[0]["out"][:B * N].reshape(B, N, D)
```

```python
import concourse.bass as bass
from concourse import mybir
from contextlib import ExitStack

P = 128
B, N, D = 8, 512, 256
H, DK, DV = 4, 128, 64
E, HID = 8, 1024
T = B * N // P
C = N // P
KC = D // P
KH = HID // P
EPS = 1e-5
PE_TOK = 2 * P
REGION = B * N + PE_TOK
SPARE = E * REGION
ROWS = SPARE + PE_TOK
RW = D + 4
MAXT = 2 * B * N // PE_TOK + E
A_SCALE = 64.0
PADS = 2 * E + 1
LEVELS = 7
W_SCALE = 256.0
H_SCALE = 64.0
PIECE = 2 * E * HID // T


def build(nc, x, wq, wk, wvg, wb, wo, norm_w, router, w1, w2, fconst, iconst, out):
    fp32, fp16, i32 = mybir.dt.float32, mybir.dt.float16, mybir.dt.int32
    ALU, ACT, AX = mybir.AluOpType, mybir.ActivationFunctionType, mybir.AxisListType
    ctx = ExitStack()
    with ctx:
        def sb(name, shape, dt=fp32):
            return ctx.enter_context(nc.sbuf_tensor(name, shape, dt))

        def sem(name):
            return ctx.enter_context(nc.semaphore(name))

        routed = nc.dram_tensor("routed_rows", [ROWS, RW], fp32, kind="Internal").ap()
        table_dram = nc.dram_tensor("tile_table_dram", [P, 2], i32, kind="Internal").ap()
        table_f_dram = nc.dram_tensor("tile_experts_dram", [P, 1], fp32, kind="Internal").ap()

        w1_hi = sb("w1_hi", [P, KC * E * HID], fp16)
        w1_lo = sb("w1_lo", [P, KC * E * HID], fp16)
        w2_s = sb("w2_s", [P, KH * E, 2, D], fp16)
        wqk = sb("wqk", [P, 2, 2, KC, H * DK], fp16)
        wq_s, wk_s = wqk[:, 0, :, :, :], wqk[:, 1, :, :, :]
        wvg_s = sb("wvg_s", [P, 2, KC, 2 * H * DV], fp16)
        wb_s = sb("wb_s", [P, 2, KC, H], fp16)
        wo_s = sb("wo_s", [P, 2, KC, D], fp16)
        wb_in = sb("wb_in", [P, KC, H])
        router_s = sb("router_s", [P, KC, E])
        normw_s = sb("normw_s", [P, DV])
        stage = w2_s[:, :, :, :].rearrange("p m v n -> p (m v n)").bitcast(fp32)
        def staged(width, before):
            n = KC * width
            at = KH * E * D - before - n
            return stage[:, at:at + n].rearrange("p (k n) -> p k n", k=KC), before + n
        wk_in, used = staged(H * DK, 0)
        wvg_in, used = staged(2 * H * DV, used)
        wq_in, used = staged(H * DK, used)
        wo_in, used = staged(D, used)
        fc = sb("fc", [P, FCONST + 128])
        ident = fc[:, 0:128]
        causal = fc[:, 128:256]
        before = fc[:, 256:384]
        before_neg = fc[:, FCONST:FCONST + 128]
        ones = fc[:, 384:512]
        pref = fc[:, 512:520]
        region = fc[:, 520:528]
        lane = fc[:, 528:529]
        token_id = fc[:, 529:529 + T]
        half_neg = fc[:, 561:577]
        mask_s = sb("mask_s", [P, 2 * LEVELS, 64], mybir.dt.int8)

        x_s = sb("x_s", [P, C, D])
        xn = sb("xn", [P, D])
        xnT = sb("xnT", [P, 2, KC, P], fp16)
        KQ = sb("KQ", [P, 2, H, 2, P])
        KpAT = sb("KpAT", [P, 2, 2, H, DK])
        Kp = KpAT[:, 0, :, :, :]
        mask_in = Kp[:, :, :, :].rearrange("p s h n -> p (s h n)")[:, 0:2 * LEVELS * 64].bitcast(i32)
        Vp = sb("Vp", [P, 2, H, DV])
        gs = sb("gs", [P, 2, H, DV])
        AT = KpAT[:, 1, :, :, :]
        Lh = sb("Lh", [P, 2, H, P], fp16)
        Ll = sb("Ll", [P, H, P], fp16)
        X = sb("X", [P, 2, H, P], fp16)
        XT = sb("XT", [P, 2, H, P], fp16)
        Y = sb("Y", [P, H, P], fp16)
        ER = sb("ER", [P, H, P], fp16)
        Z = sb("Z", [P, H, P])
        negI = sb("negI", [P, P], fp16)
        S = sb("S", [P, H, DV])
        R = sb("R", [P, H, DV])
        W = sb("W", [P, H, DV])
        sq = sb("sq", [P, H, DK])
        nL = sq[:, :, :]
        osq = sb("osq", [P, H, DV])
        oo = sb("oo", [P, H, DV])
        oT = sb("oT", [P, 2, KC, P], fp16)
        rowA = sb("rowA", [P, 2 * C, RW])
        xn2T = sb("xn2T", [P, KC, P])
        wst = sb("wst", [P, 2, PIECE])
        st6 = sb("st6", [P, 6])
        mv = sb("mv", [P, 2])
        rstd = sb("rstd", [P, 1])
        eb = sb("eb", [P, H])
        ks = sb("ks", [P, 2 * H])
        karg = sb("karg", [P, 2 * H])
        kscale = sb("kscale", [P, 2 * H])
        osum = sb("osum", [P, H])
        oarg = sb("oarg", [P, H])
        ors = sb("ors", [P, H])
        st6b = sb("st6b", [P, 6])
        mv2 = sb("mv2", [P, 2])
        rstd2 = sb("rstd2", [P, 1])
        logits = sb("logits", [P, C, E])
        r8 = [sb(f"r8_{i}", [P, C, E]) for i in range(8)]
        r1 = [sb(f"r1_{i}", [P, C]) for i in range(9)]
        first = sb("first", [P, C, E])
        second = sb("second", [P, C, E])
        both = sb("both", [P, C, E])
        run = sb("run", [P, E])
        rbase = sb("rbase", [P, C, E])
        pos = sb("pos", [P, C, E])
        slot = sb("slot", [P, 2, C], i32)
        zrow = Z[:, :, :].rearrange("p h n -> p (h n)")[:, 0:RW]
        t8 = [sb(f"t8_{i}", [P, E]) for i in range(8)]
        t8i = sb("t8i", [P, E], i32)
        t8j = sb("t8j", [P, E], i32)
        pad_idx = sb("pad_idx", [P, 2, E], i32)
        tab_f = sb("tab_f", [P, 2])
        tab_i = sb("tab_i", [P, 2], i32)
        tab = W[:, :, :].rearrange("p h n -> p (h n)").bitcast(i32)
        experts_b = R[:, :, :].rearrange("p h n -> p (h n)")
        xg = rowA[:, :, :].rearrange("p (q a) n -> p q a n", a=2)
        x_f = x_s[:, :, :].rearrange("p c n -> p (c n)").bitcast(fp16).rearrange("p (s k n) -> p s k n", s=4, k=KC)
        xTh, xTl = x_f[:, 0:2, :, :], x_f[:, 2:4, :, :]
        hf = KQ[:, :, :, :, :].rearrange("p s h a n -> p (s h a n)").rearrange("p (m n) -> p m n", m=4)
        hhi = wqk[:, :, :, :, :].rearrange("p s v k n -> p (s v k n)").rearrange("p (s m n) -> p s m n", s=2, m=KH)
        hlo = KpAT[:, :, :, :, :].rearrange("p a s h n -> p (a s h n)").bitcast(fp16).rearrange("p (s m n) -> p s m n", s=2, m=KH)
        yrow = wst[:, :, :].rearrange("p q (a n) -> p q a n", a=2)
        yidx = sb("yidx", [P, 4, 2], i32)
        gate = sb("gate", [P, 2, 2])
        gsel = sb("gsel", [P, 2, 2])

        PS = [ctx.enter_context(nc.psum_tensor(f"ps{i}", [P, 512], fp32)) for i in range(8)]
        def heads(ap, n):
            return ap.rearrange("p (h n) -> p h n", h=n)
        p_y = heads(PS[0][:, 0:256], H)
        p_x = heads(PS[1][:, 0:256], H)
        p_xt = heads(PS[1][:, 256:512], H)
        p_kv = PS[2][:, :]
        p_q = heads(PS[3][:, :], H)
        p_o = heads(PS[3][:, 0:256], H)
        p_p = heads(PS[4][:, 0:256], H)
        p_u = heads(PS[4][:, 256:512], H)
        p_r = heads(PS[5][:, :], H)
        p_kT = heads(PS[5][:, :], H)
        p_gram = [PS[5 + a][:, :].rearrange("p (h a n) -> p h a n", h=2, a=2) for a in range(2)]
        p_xnT = PS[6][:, 0:256]
        p_rank = PS[6][:, 0:C * E]
        p_tot = PS[6][:, C * E:2 * C * E]
        p_beta = PS[7][:, 0:H]
        p_oT = PS[7][:, 0:256]
        p_wo = PS[7][:, 0:256]
        p_xn2T = PS[7][:, 0:256]
        p_lg = PS[7][:, 0:E]
        p_gT = PS[0][:, :].rearrange("p (k n) -> p k n", k=KC)
        p_h = [PS[1 + m] for m in range(4)]
        p_yo = [PS[5 + a][:, :].rearrange("p (v n) -> p v n", v=2) for a in range(2)]

        s_const = sem("const_loaded")
        s_wload = [sem(f"{n}_loaded") for n in ("wk", "wvg", "wq", "wo")]
        s_wsh = sem("attention_weight_hi")
        s_wsl = sem("attention_weight_lo")
        s_x = [sem(f"x_loaded{c}") for c in range(C)]
        s_x1out = [sem(f"x1_stored{c}") for c in range(C)]
        s_w = [sem(f"w_loaded{q}") for q in range(2)]
        s_whi = sem("w_hi_ready")
        s_wlo = sem("w_lo_ready")
        s_init = sem("buffers_initialised")
        s_held = [sem("vector_waits_held"), sem("pool_waits_held")]
        pool_engine = nc.gpsimd
        s_xn = sem("xn_ready")
        s_xnTp = sem("xnT_in_psum")
        s_xnTs = sem("xnT_hi_in_sbuf")
        s_xnTl = sem("xnT_lo_in_sbuf")
        s_kps = sem("k_and_beta_in_psum")
        s_ksq = sem("k_squared")
        s_eb = sem("exp_beta_ready")
        s_karg = sem("k_scale_argument")
        s_kscale = sem("k_scale_ready")
        s_kp = sem("kprime_ready")
        s_kTp = sem("kT_in_psum")
        s_kTs = sem("kT_in_sbuf")
        s_qps = sem("qT_in_psum")
        s_qs = sem("qT_in_sbuf")
        s_vgps = sem("v_g_in_psum")
        s_th = sem("tanh_g_ready")
        s_gs = sem("v_and_gate_ready")
        s_gram = sem("gram_in_psum")
        s_nL = sem("neg_l_ready")
        s_Lh = sem("l_hi_ready")
        s_Ll = sem("l_lo_ready")
        s_AT = sem("masked_scores_ready")
        s_Xi = sem("inverse_initialised")
        s_yps = sem("y_in_psum")
        s_ys = sem("y_in_sbuf")
        s_xps = sem("update_in_psum")
        s_xup = sem("inverse_updated")
        s_rps = sem("residual_product_in_psum")
        s_er = sem("residual_product_in_sbuf")
        s_zps = sem("correction_in_psum")
        s_z = sem("corrected_inverse_ready")
        s_pps = sem("state_product_in_psum")
        s_r = sem("r_ready")
        s_wps = sem("w_in_psum")
        s_ws = sem("w_in_sbuf")
        s_ops = sem("o_in_psum")
        s_ups = sem("state_update_in_psum")
        s_s = sem("state_ready")
        s_osq = sem("o_squared")
        s_oarg = sem("o_scale_argument")
        s_ors = sem("o_scale_ready")
        s_on = sem("o_normalised")
        s_oTp = sem("oT_in_psum")
        s_oTs = sem("oT_hi_in_sbuf")
        s_oTl = sem("oT_lo_in_sbuf")
        s_wops = sem("attention_out_in_psum")
        s_res = sem("residual_ready")
        s_mv = sem("ln1_variance")
        s_rstd = sem("ln1_rstd")
        s_mv2 = sem("ln2_variance")
        s_rstd2 = sem("ln2_rstd")
        s_xn2 = sem("xn2_ready")
        s_xn2Tp = sem("xn2T_in_psum")
        s_xn2Ts = sem("xn2T_in_sbuf")
        s_lgps = sem("logits_in_psum")
        s_lg = sem("logits_ready")
        s_rd = sem("logit_differences")
        s_rexp = sem("logit_exponentials")
        s_both = sem("expert_masks_ready")
        s_rank = sem("ranks_in_psum")
        s_pos = sem("positions_ready")
        s_slot = sem("slots_ready")
        s_spare = sem("spare_rows_ready")
        s_scat = [sem(f"rows_scattered{c}") for c in range(C)]
        s_tail = sem("tail_tables_ready")
        s_pads = sem("pads_written")
        s_tabd = sem("table_in_dram")
        s_tab = sem("table_loaded")
        s_dve = sem("dve_step")
        s_xg = [sem(f"xg_loaded{q}") for q in range(4)]
        s_gTp = sem("xgT_in_psum")
        s_gTh = sem("xgT_hi_ready")
        s_gTl = sem("xgT_lo_ready")
        s_hps = sem("hidden_in_psum")
        s_gelu = sem("gelu_ready")
        s_hhi = sem("hidden_hi_ready")
        s_hlo = sem("hidden_lo_ready")
        s_yops = sem("expert_out_in_psum")
        s_yrow = sem("expert_rows_ready")
        s_acc = sem("rows_accumulated")

        block = ctx.enter_context(nc.Block())

        def up_to(eng, s, per, t, k):
            b, c = t
            value = b * (per * C) + (per * c + k)
            if not (isinstance(value, int) and value <= 0):
                eng.wait_ge(s, value)

        def hold(eng):
            eng.sem_inc(s_held[eng is pool_engine])

        def before_(t, n):
            return (t[0], t[1] - n)

        def after_(t, n=1):
            return (t[0], t[1] + n)

        def sequences(eng, body):
            body(0, 0, True, False)
            with eng.Fori(0, (B - 2) // 2) as pair:
                body(pair * 2 + 1, 1, False, False)
                body(pair * 2 + 2, 0, False, False)
            body(B - 1, 1, False, True)

        def even(ap, lev):
            s = 1 << lev
            return ap.rearrange("p h (n two s) -> p h n two s", two=2, s=s)[:, :, :, 0, :]

        def odd(ap, lev):
            s = 1 << lev
            return ap.rearrange("p h (n two s) -> p h n two s", two=2, s=s)[:, :, :, 1, :]

        def packed(ap, lev):
            return ap.rearrange("p h (n s) -> p h n s", s=1 << lev)

        def level_mask(lev, transposed, heads):
            m = mask_s[:, 2 * lev + transposed, :].rearrange("p (n s) -> p n s", s=1 << lev).unsqueeze(1)
            return m.broadcast_to([P, heads, 64 >> lev, 1 << lev])

        def col(ap, n):
            return ap.unsqueeze(2).broadcast_to([P, ap.shape[1], n])

        @block.sync
        def _(sp):
            early = [(fc[:, 0:FCONST], fconst), (mask_in, iconst.rearrange("p a b -> p (a b)")),
                     (wb_in[:, :, :], wb.rearrange("(k p) n -> p k n", p=P))]
            late = [(router_s[:, :, :], router.rearrange("(k p) n -> p k n", p=P)),
                    (normw_s[:, :], norm_w.partition_broadcast(P))]
            weights = [(wk_in, wk), (wvg_in, wvg), (wq_in, wq), (wo_in, wo)]
            sp.dma_start(x_s[:, 0, :], x[0, :, :]).then_inc(s_x[0], 16)
            for dst, src in early + late:
                sp.dma_start(dst, src).then_inc(s_const, 16)
            assert len(early + late) == CONST_LOADS
            for n, (dst, src) in enumerate(weights):
                sp.dma_start(dst, src.rearrange("(k p) n -> p k n", p=P)).then_inc(s_wload[n], 16)
            for c in range(1, 3):
                sp.dma_start(x_s[:, c, :], x[c, :, :]).then_inc(s_x[c], 16)

            def store(b, c):
                up_to(sp, s_res, 1, (b, c), 1)
                sp.dma_start(out[bass.ds((b * C + c) * P, P), :], x_s[:, c % C, :]).then_inc(s_x1out[c % C], 16)

            def body(b, par, first, last):
                for c in range(C):
                    up_to(sp, s_wlo, 2, (b, c), 0)
                    for q, src in enumerate((w1, w2)):
                        sp.dma_start(wst[:, q, :], src[bass.ds(b * C + c, 1), :, :].rearrange("a p n -> p (a n)")).then_inc(s_w[q], 16)
                    if not (first and c == 0):
                        store(b, c - 1)
                    if not (last and c >= 1):
                        if not (first and c == 0):
                            sp.wait_ge(s_x1out[(c - 1) % C], b * 16 + (16 if c else 0))
                            up_to(sp, s_xn2, 1, (b, c - 1), 1)
                        d = (c + 3) % C
                        sp.dma_start(x_s[:, d, :], x[bass.ds(b * C + (c + 3), 1), :, :].rearrange("a p n -> p (a n)")).then_inc(s_x[d], 16)
            sequences(sp, body)
            store(B - 1, C - 1)
            sp.wait_ge(s_tail, 1)
            sp.dma_start(table_dram, tab_i[:, :]).then_inc(s_tabd, 16)
            sp.dma_start(table_f_dram, tab_f[:, 0:1]).then_inc(s_tabd, 16)
            sp.wait_ge(s_tabd, 32)
            up_to(sp, s_ops, 1, (B - 1, C - 1), 1)
            sp.dma_start(tab[0:1, :], table_dram.rearrange("p n -> (p n)").unsqueeze(0)).then_inc(s_tab, 16)
            sp.dma_start(experts_b[:, 0:P], table_f_dram.rearrange("p n -> (p n)").partition_broadcast(P)).then_inc(s_tab, 16)
            sp.wait_ge(s_tab, 32)
            sp.wait_ge(s_pads, 16 * PADS)
            for c in range(C):
                sp.wait_ge(s_scat[c], 32 * B + 16)

            def load_rows(i, q):
                row = sp.value_load(tab[0:1, bass.ds(i * 8 + (2 * q + 1), 1)], min_val=0, max_val=SPARE)
                sp.dma_start(xg[:, q % 4, :, :], routed[bass.ds(row, PE_TOK), :].rearrange("(a p) n -> p a n", p=P))\
                    .then_inc(s_xg[q % 4], 16)

            for q in range(3):
                load_rows(0, q)

            def expert_body(i, last):
                for q in range(4):
                    if last and q >= 1:
                        continue
                    value = i * 4 + q
                    if not (isinstance(value, int) and value <= 0):
                        sp.wait_ge(s_yrow, value)
                    load_rows(i, q + 3)
            expert_body(0, False)
            with sp.Fori(1, MAXT // 4 - 1) as i:
                expert_body(i, False)
            expert_body(MAXT // 4 - 1, True)

        @block.gpsimd
        def _(pool):
            pool.memset(Y[:, :, :], 0.0).then_inc(s_init, 1)
            pool.memset(S[:, :, :], 0.0).then_inc(s_init, 1)
            pool.wait_ge(s_const, 16 * CONST_LOADS)

            def rsqrt(dst, src, n):
                return pool.tensor_tensor(dst, src, half_neg[:, 0:n], ALU.pow)

            def ln1(t):
                up_to(pool, s_mv, 1, t, 1)
                rsqrt(rstd[:, :], mv[:, 1:2], 1).then_inc(s_rstd, 1)

            def kscale_(t):
                up_to(pool, s_karg, 1, t, 1)
                rsqrt(kscale[:, :], karg[:, :], 2 * H).then_inc(s_kscale, 1)

            def init_inverse(t):
                par = t[1] % 2
                ident_h = ident.unsqueeze(1).broadcast_to([P, H, P])
                up_to(pool, s_z, 1, before_(t, 2), 1)
                hold(pool)
                pool.tensor_copy(X[:, par, :, :], ident_h).then_inc(s_Xi, 1)
                pool.tensor_copy(XT[:, par, :, :], ident_h).then_inc(s_Xi, 1)

            def l_low(t):
                up_to(pool, s_rps, 1, before_(t, 1), 1)
                up_to(pool, s_Lh, 1, t, 1)
                pool.tensor_tensor(Ll[:, :, :], nL, Lh[:, t[1] % 2, :, :], ALU.subtract).then_inc(s_Ll, 1)

            def epilogue(t):
                up_to(pool, s_oarg, 1, t, 1)
                rsqrt(ors[:, :], oarg[:, :], H).then_inc(s_ors, 1)

            def epilogue2(t):
                up_to(pool, s_mv2, 1, t, 1)
                rsqrt(rstd2[:, :], mv2[:, 1:2], 1).then_inc(s_rstd2, 1)

            def scatter(b, par):
                pool.wait_ge(s_slot, b + 1)
                hold(pool)
                for c in range(C):
                    for k in range(2):
                        pool.indirect_dma_start(
                            out=routed, out_offset=bass.IndirectOffsetOnAxis(ap=slot[:, k, c:c + 1], axis=0),
                            in_=rowA[:, par * C + c, :], in_offset=None).then_inc(s_scat[c], 16)

            ln1((0, 0))
            init_inverse((0, 0))
            ln1((0, 1))
            kscale_((0, 0))
            pool.memset(rowA[:, C:2 * C, :], 0.0).then_inc(s_spare, 1)
            pool.wait_ge(s_spare, 1)
            pool.tensor_scalar(rowA[:, C:2 * C, D + 3], rowA[:, C:2 * C, D + 3], lane, float(B * N), ALU.add, ALU.add).then_inc(s_spare, 1)
            pool.wait_ge(s_spare, 2)
            for c in range(C):
                part = c % 2 * 64
                pool.dma_start(routed[SPARE + 64 * c:SPARE + 64 * (c + 1), :], rowA[part:part + 64, C + c, :]).then_inc(s_scat[c], 16)

            def body(b, par, first, last):
                for c in range(C):
                    t = (b, c)
                    front, epi = not (last and c == C - 1), not (first and c == 0)
                    l_low(t)
                    if front:
                        kscale_(after_(t))
                    if epi:
                        epilogue(before_(t, 1))
                    if front:
                        init_inverse(after_(t))
                    if not (last and c >= C - 2):
                        ln1(after_(t, 2))
                    if epi:
                        epilogue2(before_(t, 1))
                    if c == 3 and not first:
                        scatter(b - 1, 1 - par)
            sequences(pool, body)
            epilogue((B - 1, C - 1))
            epilogue2((B - 1, C - 1))
            scatter(B - 1, 1)
            pool.wait_ge(s_tail, 1)
            for e in range(E):
                for a in range(2):
                    pool.indirect_dma_start(
                        out=routed, out_offset=bass.IndirectOffsetOnAxis(ap=pad_idx[:, a, e:e + 1], axis=0),
                        in_=zrow[:, :], in_offset=None).then_inc(s_pads, 16)
            pool.dma_start(out[B * N:B * N + P, :], zrow[:, 0:D]).then_inc(s_pads, 16)
            pool.wait_ge(s_pads, 16 * PADS)
            for c in range(C):
                pool.wait_ge(s_x1out[c], 16 * B)

            def accumulate(i, q):
                pool.wait_ge(s_yrow, i * 4 + (q + 1))
                for a in range(2):
                    value = i * 128 + (32 * q + 16 * a)
                    if not (isinstance(value, int) and value <= 0):
                        pool.wait_ge(s_acc, value)
                    hold(pool)
                    pool.indirect_dma_start(
                        out=out, out_offset=bass.IndirectOffsetOnAxis(ap=yidx[:, q, a:a + 1], axis=0),
                        in_=yrow[:, q % 2, a, :], in_offset=None, compute_op=ALU.add).then_inc(s_acc, 16)
            for q in range(4):
                accumulate(0, q)
            with pool.Fori(1, MAXT // 4) as i:
                for q in range(4):
                    accumulate(i, q)
            pool.wait_ge(s_acc, 32 * MAXT)

        @block.scalar
        def _(act):
            def evac(dst, src, scale=1.0):
                return act.activation(dst, src, ACT.Copy, scale=scale)

            def xnT_evac(t):
                up_to(act, s_qps, 1, before_(t, 1), 1)
                up_to(act, s_vgps, 1, before_(t, 1), 1)
                up_to(act, s_xnTp, 1, t, 1)
                evac(xnT[:, 0, :, :].rearrange("p k n -> p (k n)"), p_xnT).then_inc(s_xnTs, 1)

            def k_square(t):
                up_to(act, s_karg, 1, before_(t, 1), 1)
                up_to(act, s_Ll, 1, before_(t, 1), 1)
                up_to(act, s_kps, 1, t, 1)
                act.activation(sq[:, :, :].rearrange("p h n -> p (h n)"), p_kv, ACT.Square).then_inc(s_ksq, 1)
                act.activation(eb[:, :], p_beta, ACT.Exp, scale=-1.0 / A_SCALE).then_inc(s_eb, 1)

            def q_evac(t):
                up_to(act, s_ops, 1, before_(t, 2), 1)
                up_to(act, s_qps, 1, t, 1)
                act.activation(KQ[:, t[1] % 2, :, 1, :], p_q, ACT.Copy,
                               scale=float(DK) ** -0.5 / A_SCALE).then_inc(s_qs, 1)

            def kT_evac(t):
                up_to(act, s_kTp, 1, t, 1)
                evac(KQ[:, t[1] % 2, :, 0, :], p_kT).then_inc(s_kTs, 1)

            def tanh_g(t):
                up_to(act, s_on, 1, before_(t, 2), 1)
                up_to(act, s_vgps, 1, t, 1)
                act.activation(gs[:, t[1] % 2, :, :], p_kv[:, 256:512].rearrange("p (h n) -> p h n", h=H), ACT.Tanh,
                               scale=0.5 / A_SCALE).then_inc(s_th, 1)

            def l_high(t):
                up_to(act, s_yps, 7, before_(t, 2), 7)
                up_to(act, s_rps, 1, before_(t, 2), 1)
                up_to(act, s_nL, 1, t, 1)
                evac(Lh[:, t[1] % 2, :, :], nL).then_inc(s_Lh, 1)

            def y_evac(t, lev):
                up_to(act, s_yps, 7, t, lev + 1)
                evac(even(Y[:, :, :], lev), packed(p_y, lev)).then_inc(s_ys, 1)

            def r_evac(t):
                up_to(act, s_zps, 1, before_(t, 1), 1)
                up_to(act, s_rps, 1, t, 1)
                evac(ER[:, :, :], p_r).then_inc(s_er, 1)

            def w_evac(t):
                up_to(act, s_ops, 1, before_(t, 1), 1)
                up_to(act, s_s, 1, before_(t, 1), 1)
                up_to(act, s_wps, 1, t, 1)
                evac(W[:, :, :], p_p).then_inc(s_ws, 1)

            def o_square(t):
                up_to(act, s_on, 1, before_(t, 1), 1)
                up_to(act, s_ops, 1, t, 1)
                act.activation(osq[:, :, :], p_o, ACT.Square).then_inc(s_osq, 1)

            def oT_evac(t):
                up_to(act, s_oTp, 1, t, 1)
                evac(oT[:, 0, :, :].rearrange("p k n -> p (k n)"), p_oT).then_inc(s_oTs, 1)

            def xn2T_evac(t):
                up_to(act, s_xn2Tp, 1, t, 1)
                evac(xn2T[:, :, :].rearrange("p k n -> p (k n)"), p_xn2T).then_inc(s_xn2Ts, 1)

            def split_hi(b, c, q):
                act.wait_ge(s_w[q], b * (16 * C) + 16 * (c + 1))
                if q == 0:
                    dst, src = w1_hi[:, bass.ds(b * (C * PIECE) + c * PIECE, PIECE)], wst[:, q, :]
                else:
                    n = PIECE // D
                    dst = w2_s[:, bass.ds(b * (C * n) + c * n, n), 0, :]
                    src = wst[:, q, :].rearrange("p (m n) -> p m n", n=D)
                evac(dst, src, W_SCALE).then_inc(s_whi, 1)

            def weight_hi(n, dst, src):
                act.wait_ge(s_wload[n], 16)
                evac(dst, src, A_SCALE).then_inc(s_wsh, 1)

            def route_exp(b):
                act.wait_ge(s_rd, b + 1)
                act.activation(r8[1][:, :, :], r8[0][:, :, :], ACT.Exp).then_inc(s_rexp, 1)

            act.wait_ge(s_const, 16 * CONST_LOADS)
            act.wait_ge(s_init, 2)
            evac(wb_s[:, 0, :, :], wb_in[:, :, :], A_SCALE)
            weight_hi(0, wk_s[:, 0, :, :], wk_in)
            xnT_evac((0, 0))
            weight_hi(1, wvg_s[:, 0, :, :], wvg_in)
            weight_hi(2, wq_s[:, 0, :, :], wq_in)
            weight_hi(3, wo_s[:, 0, :, :], wo_in)
            k_square((0, 0))
            q_evac((0, 0))
            kT_evac((0, 0))
            tanh_g((0, 0))
            l_high((0, 0))

            def body(b, par, first, last):
                for c in range(C):
                    t = (b, c)
                    front, epi = not (last and c == C - 1), not (first and c == 0)
                    nxt, prv = after_(t), before_(t, 1)
                    if epi:
                        r_evac(prv)
                    if front:
                        xnT_evac(nxt)
                    if epi and not (first and c == 1):
                        xn2T_evac(before_(t, 2))
                    y_evac(t, 1)
                    if front:
                        k_square(nxt)
                    if epi:
                        w_evac(prv)
                    y_evac(t, 2)
                    split_hi(b, c, 0)
                    y_evac(t, 3)
                    if epi:
                        o_square(prv)
                    if c == 1 and not first:
                        route_exp(b - 1)
                    y_evac(t, 4)
                    if front:
                        kT_evac(nxt)
                        tanh_g(nxt)
                    y_evac(t, 5)
                    if epi:
                        oT_evac(prv)
                    if front:
                        q_evac(nxt)
                    y_evac(t, 6)
                    split_hi(b, c, 1)
                    if front:
                        l_high(nxt)
            sequences(act, body)
            last_tile = (B - 1, C - 1)
            r_evac(last_tile)
            xn2T_evac(before_(last_tile, 1))
            w_evac(last_tile)
            o_square(last_tile)
            oT_evac(last_tile)
            xn2T_evac(last_tile)
            route_exp(B - 1)

            def xT_hi(i, q):
                act.wait_ge(s_gTp, i * 4 + (q + 1))
                if not (isinstance(i, int) and i * 4 + q < 2):
                    act.wait_ge(s_hps, i * 16 + 4 * (q - 1))
                evac(xTh[:, q % 2, :, :], p_gT).then_inc(s_gTh, 1)

            def hidden(i, q):
                for m in range(4):
                    act.wait_ge(s_hps, i * 16 + (4 * q + m + 1))
                    if not (isinstance(i, int) and i * 4 + q < 1):
                        act.wait_ge(s_hlo, i * 16 + (4 * (q - 1) + m + 1))
                    if m == 0 and not (isinstance(i, int) and i * 4 + q < 2):
                        act.wait_ge(s_yops, i * 4 + (q - 1))
                    act.activation(hf[:, m, :], p_h[m][:, :], ACT.Gelu, scale=1.0 / W_SCALE).then_inc(s_gelu, 1)
                    act.wait_ge(s_gelu, i * 16 + (4 * q + m + 1))
                    evac(hhi[:, q % 2, 2 * m:2 * m + 2, :], hf[:, m, :].rearrange("p (m n) -> p m n", m=2),
                         H_SCALE).then_inc(s_hhi, 1)

            xT_hi(0, 0)
            xT_hi(0, 1)
            hidden(0, 0)

            def expert_body(i, last):
                for q in range(4):
                    if not (last and q >= 2):
                        xT_hi(i, q + 2)
                    if not (last and q == 3):
                        hidden(i, q + 1)
            expert_body(0, False)
            with act.Fori(1, MAXT // 4 - 1) as i:
                expert_body(i, False)
            expert_body(MAXT // 4 - 1, True)

        @block.tensor
        def _(pe):
            def mm(dst, lhsT, rhs, start=True, stop=True, **kw):
                return pe.matmul(dst, lhsT, rhs, start=start, stop=stop, **kw)

            def xnT_make(t):
                up_to(pe, s_AT, 2, before_(t, 1), 2)
                up_to(pe, s_xn, 1, t, 1)
                for k in range(KC):
                    last = pe.transpose(p_xnT[:, k * P:(k + 1) * P], xn[:, k * P:(k + 1) * P], ident)
                last.then_inc(s_xnTp, 1)

            PARTS = ((0, 0), (0, 1), (1, 0))

            def split_mm(dst, lhs, rhs, k):
                for n, (a, b) in enumerate(PARTS):
                    last = mm(dst, lhs(a, k), rhs(b, k), k == 0 and n == 0, k == KC - 1 and n == 2)
                return last

            def xnT_of(part, k):
                return xnT[:, part, k, :]

            def k_proj(t, k):
                if k == 0:
                    up_to(pe, s_gs, 1, before_(t, 1), 1)
                last = split_mm(p_kv, xnT_of, lambda part, k: wk_s[:, part, k, :], k)
                if k == KC - 1:
                    last.then_inc(s_kps, 1)

            def beta_proj(t):
                up_to(pe, s_xnTs, 1, t, 1)
                up_to(pe, s_xnTl, 1, t, 1)
                up_to(pe, s_lg, 1, before_(t, 3), 1)
                for k in range(KC):
                    split_mm(p_beta, xnT_of, lambda part, k: wb_s[:, part, k, :], k)

            def q_proj(t, a):
                if a == 0:
                    up_to(pe, s_on, 1, before_(t, 2), 1)
                for h in range(2 * a, 2 * a + 2):
                    for k in range(KC):
                        last = split_mm(p_q[:, h, :], lambda part, k: wq_s[:, part, k, h * DK:(h + 1) * DK], xnT_of, k)
                if a == 1:
                    last.then_inc(s_qps, 1)

            def k_transposes(t):
                up_to(pe, s_z, 1, before_(t, 2), 1)
                up_to(pe, s_kp, 1, t, 1)
                for h in range(H):
                    last = pe.transpose(p_kT[:, h, :], Kp[:, t[1] % 2, h, :], ident)
                last.then_inc(s_kTp, 1)

            def vg_proj(t, k):
                up_to(pe, s_kp, 1, t, 1)
                last = split_mm(p_kv, xnT_of, lambda part, k: wvg_s[:, part, k, :], k)
                if k == KC - 1:
                    last.then_inc(s_vgps, 1)

            def gram(t, a, ranked=None):
                up_to(pe, s_kTs, 1, t, 1)
                up_to(pe, s_qs, 1, t, 1)
                if ranked is not None:
                    pe.wait_ge(s_pos, ranked)
                for h in range(2):
                    hh = KQ[:, t[1] % 2, 2 * a + h, :, :]
                    last = mm(p_gram[a][:, h, :, :], hh[:, 0, :], hh)
                last.then_inc(s_gram, 1)

            def y_make(t, lev):
                par = t[1] % 2
                if lev == 0:
                    up_to(pe, s_Lh, 1, t, 1)
                    up_to(pe, s_Xi, 2, t, 2)
                else:
                    up_to(pe, s_xup, 7, t, lev)
                for h in range(H):
                    last = mm(packed(p_y, lev)[:, h], Lh[:, par, h, :], even(X[:, par, :, :], lev)[:, h])
                last.then_inc(s_yps, 1)

            def x_make(t, lev):
                par = t[1] % 2
                up_to(pe, s_ys, 6, t, lev)
                for h in range(H):
                    mm(packed(p_x, lev)[:, h], XT[:, par, h, :], even(Y[:, :, :], lev)[:, h])
                    last = mm(packed(p_xt, lev)[:, h], Y[:, h, :], odd(XT[:, par, :, :], lev)[:, h])
                last.then_inc(s_xps, 1)

            def residual_make(t, final=False):
                par = t[1] % 2
                if not final:
                    up_to(pe, s_AT, 2, after_(t), 1)
                up_to(pe, s_Ll, 1, t, 1)
                up_to(pe, s_xup, 7, t, 7)
                for h in range(H):
                    mm(p_r[:, h, :], Lh[:, par, h, :], X[:, par, h, :], True, False)
                    mm(p_r[:, h, :], Ll[:, h, :], X[:, par, h, :], False, False)
                    last = mm(p_r[:, h, :], negI[:, :], X[:, par, h, :], False, True)
                last.then_inc(s_rps, 1)

            def correction_make(t):
                up_to(pe, s_er, 1, t, 1)
                for h in range(H):
                    last = mm(p_r[:, h, :], ER[:, h, :], XT[:, t[1] % 2, h, :])
                last.then_inc(s_zps, 1)

            def p_make(t):
                up_to(pe, s_ws, 1, before_(t, 1), 1)
                up_to(pe, s_s, 1, before_(t, 1), 1)
                for h in range(H):
                    last = mm(p_p[:, h, :], KQ[:, t[1] % 2, h, 0, :], S[:, h, :])
                last.then_inc(s_pps, 1)

            def w_make(t):
                up_to(pe, s_r, 1, t, 1)
                up_to(pe, s_z, 1, t, 1)
                for h in range(H):
                    last = mm(p_p[:, h, :], Z[:, h, :], R[:, h, :])
                last.then_inc(s_wps, 1)

            def out_state(t, final=False):
                if final:
                    up_to(pe, s_on, 1, before_(t, 1), 1)
                else:
                    up_to(pe, s_qs, 1, after_(t), 1)
                for h in range(H):
                    mm(p_o[:, h, :], KQ[:, t[1] % 2, h, 1, :], S[:, h, :], h == 0, False, skip_group_check=True)

            def state_make(t):
                up_to(pe, s_ws, 1, t, 1)
                if t[1] % C < C - 1:
                    for h in range(H):
                        last = mm(p_u[:, h, :], Kp[:, t[1] % 2, h, :], W[:, h, :])
                    last.then_inc(s_ups, 1)

            def out_chunk(t):
                up_to(pe, s_AT, 2, t, 2)
                for h in range(H):
                    last = mm(p_o[:, h, :], AT[:, t[1] % 2, h, :], W[:, h, :], False, h == H - 1, skip_group_check=True)
                last.then_inc(s_ops, 1)

            def oT_make(t, beta_tile):
                up_to(pe, s_eb, 1, beta_tile, 1)
                up_to(pe, s_on, 1, t, 1)
                for k in range(KC):
                    last = pe.transpose(p_oT[:, k * P:(k + 1) * P], oo[:, 2 * k:2 * k + 2, :].rearrange("p h n -> p (h n)"), ident)
                last.then_inc(s_oTp, 1)

            def wo_make(t):
                up_to(pe, s_oTs, 1, t, 1)
                up_to(pe, s_oTl, 1, t, 1)
                for k in range(KC):
                    last = split_mm(p_wo, lambda part, k: oT[:, part, k, :], lambda part, k: wo_s[:, part, k, :], k)
                last.then_inc(s_wops, 1)

            def xn2T_make(t, row):
                up_to(pe, s_xn2, 1, t, 1)
                for k in range(KC):
                    last = pe.transpose(p_xn2T[:, k * P:(k + 1) * P], rowA[:, row, k * P:(k + 1) * P], ident)
                last.then_inc(s_xn2Tp, 1)

            def logits_make(t):
                up_to(pe, s_lg, 1, before_(t, 1), 1)
                up_to(pe, s_xn2Ts, 1, t, 1)
                for k in range(KC):
                    last = mm(p_lg, xn2T[:, k, :], router_s[:, k, :], k == 0, k == KC - 1)
                last.then_inc(s_lgps, 1)

            def rank(b):
                pe.wait_ge(s_both, b + 1)
                m = both[:, :, :].rearrange("p c e -> p (c e)")
                mm(p_rank, before, m)
                mm(p_tot, ones, m).then_inc(s_rank, 1)

            pe.wait_ge(s_const, 16 * CONST_LOADS)
            pe.wait_ge(s_init, 2)
            t0 = (0, 0)
            xnT_make(t0)
            pe.wait_ge(s_wsh, 1)
            pe.wait_ge(s_wsl, 1)
            beta_proj(t0)
            k_proj(t0, 0)
            k_proj(t0, 1)
            pe.wait_ge(s_wsh, 4)
            pe.wait_ge(s_wsl, 4)
            q_proj(t0, 0)
            q_proj(t0, 1)
            k_transposes(t0)
            vg_proj(t0, 0)
            vg_proj(t0, 1)
            gram(t0, 0)
            gram(t0, 1)

            def body(b, par, first, last):
                for c in range(C):
                    t = (b, c)
                    front, epi = not (last and c == C - 1), not (first and c == 0)
                    nxt, prv = after_(t), before_(t, 1)
                    if epi:
                        residual_make(prv)
                        p_make(prv)
                    y_make(t, 0)
                    if front:
                        xnT_make(nxt)
                    if epi and not (first and c == 1):
                        logits_make(before_(t, 2))
                    y_make(t, 1)
                    if epi:
                        correction_make(prv)
                    if front:
                        beta_proj(nxt)
                        k_proj(nxt, 0)
                    x_make(t, 1)
                    if front:
                        k_proj(nxt, 1)
                    y_make(t, 2)
                    if epi:
                        w_make(prv)
                    x_make(t, 2)
                    if epi:
                        out_state(prv)
                    y_make(t, 3)
                    if epi:
                        state_make(prv)
                    if c == 2 and not first:
                        rank(b - 1)
                    x_make(t, 3)
                    if epi:
                        out_chunk(prv)
                    y_make(t, 4)
                    if front:
                        k_transposes(nxt)
                        vg_proj(nxt, 0)
                    x_make(t, 4)
                    if front:
                        vg_proj(nxt, 1)
                    y_make(t, 5)
                    if front:
                        q_proj(nxt, 0)
                    x_make(t, 5)
                    if epi:
                        oT_make(prv, nxt if front else t)
                    if front:
                        q_proj(nxt, 1)
                    y_make(t, 6)
                    if epi:
                        wo_make(prv)
                    x_make(t, 6)
                    if front:
                        gram(nxt, 0)
                        gram(nxt, 1, b if c == 2 and not first else None)
                    if epi:
                        xn2T_make(prv, (par * C + c - 1) % (2 * C))
            sequences(pe, body)
            last_tile = (B - 1, C - 1)
            residual_make(last_tile, True)
            p_make(last_tile)
            logits_make(before_(last_tile, 1))
            correction_make(last_tile)
            w_make(last_tile)
            out_state(last_tile, True)
            state_make(last_tile)
            out_chunk(last_tile)
            oT_make(last_tile, last_tile)
            wo_make(last_tile)
            xn2T_make(last_tile, 2 * C - 1)
            logits_make(last_tile)
            rank(B - 1)

            pe.wait_ge(s_tab, 32)
            pe.wait_ge(s_whi, 2 * T)
            pe.wait_ge(s_wlo, 2 * T)
            pe.wait_ge(s_slot, B)

            def xT_make(i, q):
                pe.wait_ge(s_xg[q % 4], i * 16 + 16 * (q // 4 + 1))
                if not (isinstance(i, int) and i * 4 + q < 1):
                    pe.wait_ge(s_gTl, i * 4 + q)
                for a in range(2):
                    for k in range(KC):
                        last = pe.transpose(p_gT[:, k, a * P:(a + 1) * P], xg[:, q % 4, a, k * P:(k + 1) * P], ident)
                last.then_inc(s_gTp, 1)

            def expert_of(i, q):
                return pe.value_load(tab[0:1, bass.ds(i * 8 + 2 * q, 1)], min_val=0, max_val=E - 1)

            def up(i, q):
                e = expert_of(i, q)
                pe.wait_ge(s_gTh, i * 4 + (q + 1))
                pe.wait_ge(s_gTl, i * 4 + (q + 1))
                hi, lo = xTh[:, q % 2, :, :], xTl[:, q % 2, :, :]
                for m in range(KH):
                    if m % 2 == 0 and not (isinstance(i, int) and i * 4 + q < 1):
                        pe.wait_ge(s_gelu, i * 16 + (4 * (q - 1) + m // 2 + 1))
                    dst = p_h[m // 2][:, (m % 2) * PE_TOK:(m % 2 + 1) * PE_TOK]
                    for k in range(KC):
                        off = e * HID + (k * E * HID + m * P)
                        wh, wl = w1_hi[:, bass.ds(off, P)], w1_lo[:, bass.ds(off, P)]
                        mm(dst, wh, hi[:, k, :], k == 0, False)
                        mm(dst, wh, lo[:, k, :], False, False)
                        last = mm(dst, wl, hi[:, k, :], False, k == KC - 1)
                    if m % 2 == 1:
                        last.then_inc(s_hps, 1)

            def down(i, q):
                e = expert_of(i, q)
                if not (isinstance(i, int) and i * 4 + q < 1):
                    pe.wait_ge(s_yrow, i * 4 + q)
                for m in range(KH):
                    if m % 2 == 0:
                        pe.wait_ge(s_hhi, i * 16 + (4 * q + m // 2 + 1))
                        pe.wait_ge(s_hlo, i * 16 + (4 * q + m // 2 + 1))
                    w = w2_s[:, bass.ds(e + m * E, 1), :, :].rearrange("p e v n -> p (e v n)")
                    for a in range(2):
                        both_parts = p_yo[a].rearrange("p v n -> p (v n)")
                        mm(both_parts, hhi[:, q % 2, m, a * P:(a + 1) * P], w, m == 0, False)
                        last = mm(p_yo[a][:, 0, :], hlo[:, q % 2, m, a * P:(a + 1) * P], w[:, 0:D], False, m == KH - 1)
                last.then_inc(s_yops, 1)

            xT_make(0, 0)
            xT_make(0, 1)
            up(0, 0)

            def expert_body(i, last):
                for q in range(4):
                    if not (last and q >= 2):
                        xT_make(i, q + 2)
                    if not (last and q == 3):
                        up(i, q + 1)
                    down(i, q)
            expert_body(0, False)
            with pe.Fori(1, MAXT // 4 - 1) as i:
                expert_body(i, False)
            expert_body(MAXT // 4 - 1, True)

        @block.vector
        def _(dve):
            class Own:
                base, n = 0, 0

            def step(ins):
                Own.n += 1
                ins.then_inc(s_dve, 1)

            def settled():
                dve.wait_ge(s_dve, Own.base + Own.n)

            def link(ins):
                step(ins)
                settled()

            def ln1_stats(t):
                b, c = t
                dve.wait_ge(s_x[c % C], (b + c // C) * 16 + 16)
                link(dve.bn_stats(st6[:, :], x_s[:, c % C, :]))
                hold(dve)
                link(dve.bn_aggr(mv[:, :], st6[:, :]))
                dve.tensor_scalar(mv[:, 1:2], mv[:, 1:2], EPS, None, ALU.add).then_inc(s_mv, 1)

            def ln1(t):
                up_to(dve, s_rstd, 1, t, 1)
                up_to(dve, s_xnTp, 1, before_(t, 1), 1)
                dve.tensor_scalar(xn[:, :], x_s[:, t[1] % C, :], mv[:, 0:1], rstd[:, 0:1],
                                  ALU.subtract, ALU.mult).then_inc(s_xn, 1)

            def xnT_low(t):
                up_to(dve, s_qps, 1, before_(t, 1), 1)
                up_to(dve, s_vgps, 1, before_(t, 1), 1)
                up_to(dve, s_xnTs, 1, t, 1)
                dve.tensor_tensor(xnT[:, 1, :, :].rearrange("p k n -> p (k n)"), p_xnT,
                                  xnT[:, 0, :, :].rearrange("p k n -> p (k n)"), ALU.subtract).then_inc(s_xnTl, 1)

            def oT_low(t):
                up_to(dve, s_oTs, 1, t, 1)
                dve.tensor_tensor(oT[:, 1, :, :].rearrange("p k n -> p (k n)"), p_oT,
                                  oT[:, 0, :, :].rearrange("p k n -> p (k n)"), ALU.subtract).then_inc(s_oTl, 1)

            def k_norm(t):
                up_to(dve, s_ksq, 1, t, 1)
                up_to(dve, s_eb, 1, t, 1)
                link(dve.tensor_reduce(ks[:, 0:H], sq[:, :, :], AX.X, ALU.add))
                step(dve.tensor_scalar(karg[:, H:2 * H], eb[:, :], 1.0, A_SCALE ** 2, ALU.add, ALU.mult))
                link(dve.tensor_scalar(ks[:, H:2 * H], ks[:, 0:H], A_SCALE ** -2, 1e-12, ALU.mult, ALU.add))
                dve.tensor_tensor(karg[:, 0:H], ks[:, H:2 * H], karg[:, H:2 * H], ALU.mult).then_inc(s_karg, 1)

            def k_prime(t):
                up_to(dve, s_ops, 1, before_(t, 2), 1)
                up_to(dve, s_kscale, 1, t, 1)
                dve.tensor_tensor(Kp[:, t[1] % 2, :, :], p_kv.rearrange("p (h n) -> p h n", h=H),
                                  col(kscale[:, 0:H], DK), ALU.mult).then_inc(s_kp, 1)

            def v_gate(t):
                up_to(dve, s_vgps, 1, t, 1)
                up_to(dve, s_th, 1, t, 1)
                par = t[1] % 2
                v, g = p_kv[:, 0:256].rearrange("p (h n) -> p h n", h=H), p_kv[:, 256:512].rearrange("p (h n) -> p h n", h=H)
                step(dve.tensor_tensor(Vp[:, par, :, :], v, col(kscale[:, H:2 * H], DV), ALU.mult))
                link(dve.scalar_tensor_tensor(gs[:, par, :, :], gs[:, par, :, :], 1.0, g, ALU.add, ALU.mult))
                dve.tensor_tensor(gs[:, par, :, :], gs[:, par, :, :], normw_s[:, :].unsqueeze(1).broadcast_to([P, H, DV]),
                                  ALU.mult).then_inc(s_gs, 1)

            def masked_gram(t, a):
                up_to(dve, s_ops, 1, before_(t, 2), 1)
                up_to(dve, s_gram, 2, t, a + 1)
                two = slice(2 * a, 2 * a + 2)
                last = dve.tensor_tensor(nL[:, two, :], p_gram[a][:, :, 0, :],
                                         before_neg.unsqueeze(1).broadcast_to([P, 2, P]), ALU.mult)
                if a == 1:
                    last.then_inc(s_nL, 1)
                dve.tensor_tensor(AT[:, t[1] % 2, two, :], p_gram[a][:, :, 1, :],
                                  causal.unsqueeze(1).broadcast_to([P, 2, P]), ALU.mult).then_inc(s_AT, 1)

            def level_zero_t(t):
                up_to(dve, s_Xi, 2, t, 2)
                up_to(dve, s_Lh, 1, t, 1)
                hold(dve)
                par = t[1] % 2
                dve.copy_predicated(odd(XT[:, par, :, :], 0), level_mask(0, 1, H), odd(Lh[:, par, :, :], 0))

            def level_zero(t):
                up_to(dve, s_yps, 7, t, 1)
                hold(dve)
                dve.copy_predicated(even(X[:, t[1] % 2, :, :], 0), level_mask(0, 0, H), packed(p_y, 0)).then_inc(s_xup, 1)

            def level_update(t, lev):
                up_to(dve, s_xps, 6, t, lev)
                hold(dve)
                par = t[1] % 2
                dve.copy_predicated(even(X[:, par, :, :], lev), level_mask(lev, 0, H), packed(p_x, lev))
                dve.copy_predicated(odd(XT[:, par, :, :], lev), level_mask(lev, 1, H), packed(p_xt, lev)).then_inc(s_xup, 1)

            def correct(t):
                up_to(dve, s_wps, 1, before_(t, 1), 1)
                up_to(dve, s_zps, 1, t, 1)
                dve.scalar_tensor_tensor(Z[:, :, :], XT[:, t[1] % 2, :, :], 2.0, p_r, ALU.mult, ALU.add).then_inc(s_z, 1)

            def r_make(t):
                up_to(dve, s_wps, 1, before_(t, 1), 1)
                up_to(dve, s_pps, 1, t, 1)
                dve.tensor_tensor(R[:, :, :], Vp[:, t[1] % 2, :, :], p_p, ALU.subtract).then_inc(s_r, 1)

            def state(t):
                up_to(dve, s_ops, 1, t, 1)
                if t[1] % C < C - 1:
                    dve.wait_ge(s_ups, t[0] * (C - 1) + (t[1] + 1))
                    dve.tensor_tensor(S[:, :, :], S[:, :, :], p_u, ALU.add).then_inc(s_s, 1)
                else:
                    dve.memset(S[:, :, :], 0.0).then_inc(s_s, 1)

            def o_scale(t):
                up_to(dve, s_osq, 1, t, 1)
                link(dve.tensor_reduce(osum[:, :], osq[:, :, :], AX.X, ALU.add))
                dve.tensor_scalar(oarg[:, :], osum[:, :], 1.0 / DV, EPS, ALU.mult, ALU.add).then_inc(s_oarg, 1)

            def o_norm(t):
                up_to(dve, s_ors, 1, t, 1)
                up_to(dve, s_oTp, 1, before_(t, 1), 1)
                link(dve.tensor_tensor(osq[:, :, :], p_o, col(ors[:, :], DV), ALU.mult))
                dve.tensor_tensor(oo[:, :, :], osq[:, :, :], gs[:, t[1] % 2, :, :], ALU.mult).then_inc(s_on, 1)

            def residual(t):
                up_to(dve, s_wops, 1, t, 1)
                s_ = t[1] % C
                dve.scalar_tensor_tensor(x_s[:, s_, :], p_wo, 1.0 / A_SCALE, x_s[:, s_, :], ALU.mult, ALU.add).then_inc(s_res, 1)
                up_to(dve, s_res, 1, t, 1)
                link(dve.bn_stats(st6b[:, :], x_s[:, s_, :]))
                hold(dve)
                link(dve.bn_aggr(mv2[:, :], st6b[:, :]))
                dve.tensor_scalar(mv2[:, 1:2], mv2[:, 1:2], EPS, None, ALU.add).then_inc(s_mv2, 1)

            def ln2(t, row, scattered):
                if scattered is not None:
                    dve.wait_ge(s_scat[t[1] % C], scattered)
                up_to(dve, s_rstd2, 1, t, 1)
                dve.tensor_scalar(rowA[:, row, 0:D], x_s[:, t[1] % C, :], mv2[:, 0:1], rstd2[:, 0:1],
                                  ALU.subtract, ALU.mult).then_inc(s_xn2, 1)

            def logits_copy(t):
                up_to(dve, s_lgps, 1, t, 1)
                dve.tensor_copy(logits[:, t[1] % C, :], p_lg).then_inc(s_lg, 1)

            def split_lo(b, c, q):
                dve.wait_ge(s_whi, b * (2 * C) + (2 * c + q + 1))
                if q == 0:
                    at = bass.ds(b * (C * PIECE) + c * PIECE, PIECE)
                    lo, hi, src = w1_lo[:, at], w1_hi[:, at], wst[:, q, :]
                else:
                    n = PIECE // D
                    at = bass.ds(b * (C * n) + c * n, n)
                    lo, hi, src = w2_s[:, at, 1, :], w2_s[:, at, 0, :], wst[:, q, :].rearrange("p (m n) -> p m n", n=D)
                dve.scalar_tensor_tensor(lo, src, W_SCALE, hi, ALU.mult, ALU.subtract).then_inc(s_wlo, 1)

            def weight_lo(n, parts, src):
                dve.wait_ge(s_wsh, n + 1)
                return dve.scalar_tensor_tensor(parts[:, 1, :, :], src, A_SCALE, parts[:, 0, :, :], ALU.mult, ALU.subtract)

            def route_masks(b, par):
                diff, ex, a0, a1, a2, a3 = r8[0:6]
                m1, tm, m2, ssum, g1, g2, g2s, tm2, gd = r1
                rows = rowA[:, par * C:(par + 1) * C, :]
                pref_c = pref.unsqueeze(1).broadcast_to([P, C, E])
                dve.wait_ge(s_lg, b * C + C)
                step(dve.tensor_reduce(m1[:, :], logits[:, :, :], AX.X, ALU.max))
                yield
                dve.tensor_tensor(diff[:, :, :], logits[:, :, :], col(m1[:, :], E), ALU.subtract).then_inc(s_rd, 1)
                yield
                dve.wait_ge(s_rd, b + 1)
                step(dve.scalar_tensor_tensor(a0[:, :, :], diff[:, :, :], 0.0, pref_c, ALU.is_equal, ALU.mult))
                yield
                step(dve.tensor_reduce(tm[:, :], a0[:, :, :], AX.X, ALU.max))
                yield
                step(dve.tensor_tensor(first[:, :, :], a0[:, :, :], col(tm[:, :], E), ALU.is_equal))
                step(dve.tensor_scalar(rows[:, :, D + 2], tm[:, :], -1.0, float(E), ALU.mult, ALU.add))
                yield
                step(dve.scalar_tensor_tensor(a1[:, :, :], first[:, :, :], -1e30, diff[:, :, :], ALU.mult, ALU.add))
                yield
                step(dve.tensor_reduce(m2[:, :], a1[:, :, :], AX.X, ALU.max))
                yield
                step(dve.tensor_tensor(a2[:, :, :], a1[:, :, :], col(m2[:, :], E), ALU.is_equal))
                yield
                step(dve.tensor_tensor(a3[:, :, :], a2[:, :, :], pref_c, ALU.mult))
                yield
                step(dve.tensor_reduce(tm2[:, :], a3[:, :, :], AX.X, ALU.max))
                yield
                step(dve.tensor_tensor(second[:, :, :], a3[:, :, :], col(tm2[:, :], E), ALU.is_equal))
                yield
                dve.tensor_tensor(both[:, :, :], first[:, :, :], second[:, :, :], ALU.add).then_inc(s_both, 1)
                dve.wait_ge(s_rexp, b + 1)
                step(dve.tensor_reduce(ssum[:, :], ex[:, :, :], AX.X, ALU.add))
                step(dve.tensor_tensor(a0[:, :, :], ex[:, :, :], second[:, :, :], ALU.mult))
                yield
                step(dve.tensor_reduce(g2[:, :], a0[:, :, :], AX.X, ALU.add))
                step(dve.reciprocal(g1[:, :], ssum[:, :]))
                yield
                step(dve.tensor_tensor(g2s[:, :], g2[:, :], g1[:, :], ALU.mult))
                yield
                step(dve.tensor_tensor(rows[:, :, D + 1], g1[:, :], g2s[:, :], ALU.subtract))
                step(dve.tensor_copy(rows[:, :, D], g2s[:, :]))
                step(dve.tensor_copy(rows[:, :, D + 3], fc[:, bass.ds(b * C + 529, C)]))
                yield

            def route_slots(b, scattered):
                dve.wait_ge(s_rank, b + 1)
                step(dve.tensor_copy(rbase[:, 0, :], run[:, :]))
                for c in range(C):
                    yield
                    dst = rbase[:, c + 1, :] if c < C - 1 else run[:, :]
                    step(dve.tensor_tensor(dst, rbase[:, c, :], p_tot[:, c * E:(c + 1) * E], ALU.add))
                yield
                dve.tensor_tensor(pos[:, :, :], rbase[:, :, :], p_rank.rearrange("p (c e) -> p c e", c=C), ALU.add).then_inc(s_pos, 1)
                yield
                dve.wait_ge(s_pos, b + 1)
                for k, m in enumerate((first, second)):
                    step(dve.tensor_tensor(r8[6 + k][:, :, :], pos[:, :, :], m[:, :, :], ALU.mult))
                yield
                for k in range(2):
                    step(dve.tensor_reduce(r1[k][:, :], r8[6 + k][:, :, :], AX.X, ALU.add))
                yield
                for c in range(C):
                    dve.wait_ge(s_scat[c], scattered)
                step(dve.tensor_copy(slot[:, 0, :], r1[0][:, :]))
                dve.tensor_copy(slot[:, 1, :], r1[1][:, :]).then_inc(s_slot, 1)
                yield

            def on(gen):
                if gen is not None:
                    settled()
                    next(gen, None)

            def all_of(gen):
                for _ in gen:
                    settled()

            dve.wait_ge(s_const, 16 * CONST_LOADS)
            dve.wait_ge(s_init, 2)
            step(dve.tensor_scalar(negI[:, :], ident, -1.0, None, ALU.mult))
            step(dve.tensor_scalar(before_neg, before, -1.0, None, ALU.mult))
            step(dve.tensor_scalar(normw_s[:, :], normw_s[:, :], 0.5 / A_SCALE, None, ALU.mult))
            step(dve.tensor_copy(mask_s[:, :, :].rearrange("p a b -> p (a b)"), mask_in))
            link(dve.tensor_copy(run[:, :], region))
            t0 = (0, 0)
            ln1_stats(t0)
            ln1(t0)
            weight_lo(0, wb_s, wb_in[:, :, :])
            weight_lo(0, wk_s, wk_in).then_inc(s_wsl, 1)
            xnT_low(t0)
            ln1_stats((0, 1))
            ln1((0, 1))
            weight_lo(1, wvg_s, wvg_in).then_inc(s_wsl, 1)
            weight_lo(2, wq_s, wq_in).then_inc(s_wsl, 1)
            weight_lo(3, wo_s, wo_in).then_inc(s_wsl, 1)
            k_norm(t0)
            k_prime(t0)
            v_gate(t0)
            masked_gram(t0, 0)
            masked_gram(t0, 1)

            def body(b, par, first_, last_):
                gen = None
                for c in range(C):
                    t = (b, c)
                    front, epi = not (last_ and c == C - 1), not (first_ and c == 0)
                    nxt, prv = after_(t), before_(t, 1)
                    front2 = not (last_ and c >= C - 2)
                    level_zero_t(t)
                    if epi:
                        r_make(prv)
                    level_zero(t)
                    if epi and not (first_ and c == 1):
                        logits_copy(before_(t, 2))
                    if c == 1 and not first_:
                        gen = route_masks(b - 1, 1 - par)
                    if front:
                        xnT_low(nxt)
                    on(gen)
                    if epi:
                        correct(prv)
                    on(gen)
                    level_update(t, 1)
                    on(gen)
                    if front:
                        k_norm(nxt)
                    on(gen)
                    if front2:
                        ln1_stats(after_(t, 2))
                    on(gen)
                    level_update(t, 2)
                    on(gen)
                    split_lo(b, c, 0)
                    on(gen)
                    level_update(t, 3)
                    if epi:
                        state(prv)
                    on(gen)
                    if c == 2 and not first_:
                        gen = route_slots(b - 1, (b - 1) * 32 + 16)
                        on(gen)
                    if front:
                        k_prime(nxt)
                    on(gen)
                    if epi:
                        o_scale(prv)
                    on(gen)
                    level_update(t, 4)
                    on(gen)
                    if epi:
                        o_norm(prv)
                    on(gen)
                    level_update(t, 5)
                    on(gen)
                    if front:
                        v_gate(nxt)
                    on(gen)
                    if epi:
                        oT_low(prv)
                    on(gen)
                    if front2:
                        ln1(after_(t, 2))
                    on(gen)
                    level_update(t, 6)
                    on(gen)
                    if epi:
                        residual(prv)
                    on(gen)
                    if front:
                        masked_gram(nxt, 0)
                        on(gen)
                        masked_gram(nxt, 1)
                    on(gen)
                    split_lo(b, c, 1)
                    on(gen)
                    if epi:
                        ln2(prv, (par * C + c - 1) % (2 * C), None if first_ or c == 0 else (b - 1) * 32 + 16)
                    if gen is not None:
                        all_of(gen)
                        gen = None

            start = Own.n
            body(0, 0, True, False)
            per_seq = OWN_PER_SEQ
            first_n = Own.n
            with dve.Fori(0, (B - 2) // 2) as pair:
                for n, par in enumerate((1, 0)):
                    Own.base, Own.n = pair * (2 * per_seq) + (first_n + n * per_seq), 0
                    body(pair * 2 + (1 + n), par, False, False)
                    assert Own.n == per_seq, Own.n
            Own.base, Own.n = first_n + (B - 2) * per_seq, 0
            body(B - 1, 1, False, True)
            last_tile = (B - 1, C - 1)
            r_make(last_tile)
            logits_copy(before_(last_tile, 1))
            correct(last_tile)
            state(last_tile)
            o_scale(last_tile)
            o_norm(last_tile)
            oT_low(last_tile)
            residual(last_tile)
            ln2(last_tile, 2 * C - 1, None)
            logits_copy(last_tile)
            all_of(route_masks(B - 1, 1))
            all_of(route_slots(B - 1, 32 * (B - 1) + 16))

            cnt, ntf, cum, prev, ge, oneh, rw, tmp = t8
            settled()
            step(dve.memset(zrow[:, 0:D + 3], 0.0))
            step(dve.tensor_scalar(zrow[:, D + 3:D + 4], lane, float(B * N), None, ALU.add))
            link(dve.tensor_tensor(cnt[:, :], run[:, :], region, ALU.subtract))
            for a in range(2):
                step(dve.tensor_scalar(pad_idx[:, a, :], run[:, :], lane, float(a * P), ALU.add, ALU.add))
            link(dve.tensor_scalar(t8i[:, :], cnt[:, :], float(PE_TOK - 1), None, ALU.add))
            link(dve.tensor_scalar(t8j[:, :], t8i[:, :], PE_TOK.bit_length() - 1, None, ALU.arith_shift_right))
            link(dve.tensor_copy(ntf[:, :], t8j[:, :]))
            link(dve.tensor_tensor_scan(cum[:, :], ones[:, 0:E], ntf[:, :], 0.0, ALU.mult, ALU.add))
            link(dve.tensor_tensor(prev[:, :], cum[:, :], ntf[:, :], ALU.subtract))
            link(dve.tensor_scalar(ge[:, :], cum[:, :], lane, None, ALU.is_le))
            step(dve.tensor_scalar(oneh[:, 0:1], ge[:, 0:1], -1.0, 1.0, ALU.mult, ALU.add))
            step(dve.tensor_tensor(oneh[:, 1:E], ge[:, 0:E - 1], ge[:, 1:E], ALU.subtract))
            link(dve.tensor_scalar(rw[:, :], prev[:, :], lane, -float(PE_TOK), ALU.subtract, ALU.mult))
            link(dve.tensor_tensor(tmp[:, :], rw[:, :], region, ALU.add))
            link(dve.tensor_tensor(rw[:, :], tmp[:, :], oneh[:, :], ALU.mult))
            step(dve.tensor_reduce(tab_f[:, 0:1], ge[:, 0:E - 1], AX.X, ALU.add))
            link(dve.tensor_reduce(cnt[:, 0:1], rw[:, :], AX.X, ALU.add))
            link(dve.scalar_tensor_tensor(tab_f[:, 1:2], ge[:, E - 1:E], float(SPARE), cnt[:, 0:1], ALU.mult, ALU.add))
            dve.tensor_copy(tab_i[:, :], tab_f[:, :]).then_inc(s_tail, 1)

            def xT_lo(i, q):
                dve.wait_ge(s_gTh, i * 4 + (q + 1))
                dve.tensor_tensor(xTl[:, q % 2, :, :], p_gT, xTh[:, q % 2, :, :], ALU.subtract).then_inc(s_gTl, 1)

            def hidden_lo(i, q):
                for m in range(4):
                    dve.wait_ge(s_hhi, i * 16 + (4 * q + m + 1))
                    two = slice(2 * m, 2 * m + 2)
                    dve.scalar_tensor_tensor(hlo[:, q % 2, two, :], hf[:, m, :].rearrange("p (m n) -> p m n", m=2), H_SCALE,
                                             hhi[:, q % 2, two, :], ALU.mult, ALU.subtract).then_inc(s_hlo, 1)

            def rows_out(i, q):
                if not (isinstance(i, int) and i * 4 + q < 2):
                    dve.wait_ge(s_acc, i * 128 + 32 * (q - 1))
                w, par = xg[:, q, :, :], q % 2
                step(dve.tensor_copy(yidx[:, q, :], w[:, :, D + 3]))
                step(dve.tensor_scalar(gsel[:, par, :], w[:, :, D + 2], experts_b[:, bass.ds(i * 4 + q, 1)],
                                       1.0 / (W_SCALE * H_SCALE), ALU.is_equal, ALU.mult))
                settled()
                link(dve.tensor_tensor(gsel[:, par, :], gsel[:, par, :], w[:, :, D + 1], ALU.mult))
                link(dve.scalar_tensor_tensor(gate[:, par, :], w[:, :, D], 1.0 / (W_SCALE * H_SCALE), gsel[:, par, :],
                                              ALU.mult, ALU.add))
                dve.wait_ge(s_yops, i * 4 + (q + 1))
                for a in range(2):
                    step(dve.tensor_scalar(yrow[:, par, a, :], p_yo[a][:, 0, :], gate[:, par, a:a + 1],
                                           None, ALU.mult))
                settled()
                for a in range(2):
                    last = dve.scalar_tensor_tensor(yrow[:, par, a, :], p_yo[a][:, 1, :], gate[:, par, a:a + 1],
                                                    yrow[:, par, a, :], ALU.mult, ALU.add)
                last.then_inc(s_yrow, 1)

            dve.wait_ge(s_xg[0], 16)
            xT_lo(0, 0)
            xT_lo(0, 1)
            hidden_lo(0, 0)

            def expert_body(i, last):
                for q in range(4):
                    if not (last and q >= 2):
                        xT_lo(i, q + 2)
                    if not (last and q == 3):
                        hidden_lo(i, q + 1)
                    rows_out(i, q)
            before_experts = Own.base + Own.n
            expert_body(0, False)
            per_body = Own.base + Own.n - before_experts
            with dve.Fori(1, MAXT // 4 - 1) as i:
                Own.base, Own.n = i * per_body + before_experts, 0
                expert_body(i, False)
            Own.base, Own.n = before_experts + (MAXT // 4 - 1) * per_body, 0
            expert_body(MAXT // 4 - 1, True)


FCONST = 577
CONST_LOADS = 5
OWN_PER_SEQ = 73


def constants():
    import numpy as np
    f = np.zeros((P, FCONST), np.float32)
    j, i = np.arange(P)[:, None], np.arange(P)[None, :]
    f[:, 0:128] = j == i
    f[:, 128:256] = j <= i
    f[:, 256:384] = j < i
    f[:, 384:512] = 1.0
    f[:, 512:520] = E - np.arange(E)
    f[:, 520:528] = REGION * np.arange(E)
    f[:, 528] = np.arange(P)
    f[:, 529:529 + T] = P * np.arange(T)[None, :] + j
    f[:, 561:577] = -0.5
    m = np.zeros((P, 2 * LEVELS, 64), np.int32)
    for lev in range(LEVELS):
        s = 1 << lev
        lower = (j // s == i // s + 1) & ((i // s) % 2 == 0)
        m[:, 2 * lev, :] = lower.reshape(P, -1, 2, s)[:, :, 0, :].reshape(P, 64)
        m[:, 2 * lev + 1, :] = lower.T.reshape(P, -1, 2, s)[:, :, 1, :].reshape(P, 64)
    return f, m


def kernel(**inputs):
    import numpy as np
    import concourse.bacc as bacc
    from concourse.bass_utils import run_bass_kernel_spmd

    g = {k: np.asarray(v) for k, v in inputs.items()}
    fconst, iconst = constants()
    w1 = g["L0_ffn_w1"].transpose(2, 0, 1).reshape(KC, P, T // KC, PIECE).transpose(0, 2, 1, 3).reshape(T, P, PIECE)
    w2 = g["L0_ffn_w2"].transpose(2, 0, 1).reshape(KH, P, T // KH, PIECE).transpose(0, 2, 1, 3).reshape(T, P, PIECE)
    arrays = {
        "x": g["L0_attn_x"].reshape(T, P, D),
        "wq": g["L0_attn_Wq"], "wk": g["L0_attn_Wk"],
        "wvg": np.concatenate([g["L0_attn_Wv"], g["L0_attn_Wg"]], axis=1),
        "wb": g["L0_attn_Wb"], "wo": g["L0_attn_Wo"], "norm_w": g["L0_attn_norm_w"],
        "router": g["L0_ffn_router_w"].T,
        "w1": w1, "w2": w2, "fconst": fconst, "iconst": iconst,
    }
    arrays = {k: np.ascontiguousarray(v) for k, v in arrays.items()}
    nc = bacc.Bacc("TRN2", target_bir_lowering=False, num_devices=1)
    args = [nc.dram_tensor(k, a.shape, mybir.dt.from_np(a.dtype), kind="ExternalInput").ap() for k, a in arrays.items()]
    out = nc.dram_tensor("out", (B * N + P, D), mybir.dt.float32, kind="ExternalOutput").ap()
    build(nc, *args, out)
    r = run_bass_kernel_spmd(nc, [arrays], core_ids=[0])
    return r.results[0]["out"][:B * N].reshape(B, N, D)
```

```python
import concourse.bass as bass
from concourse import mybir
from contextlib import ExitStack

P = 128
B, N, D = 8, 512, 256
H, DK, DV = 4, 128, 64
E, HID = 8, 1024
T = B * N // P
C = N // P
KC = D // P
KH = HID // P
EPS = 1e-5
PE_TOK = 2 * P
REGION = B * N + PE_TOK
SPARE = E * REGION
ROWS = SPARE + PE_TOK
RW = D + 4
MAXT = 2 * B * N // PE_TOK + E - 1
LAST = MAXT % 4
assert LAST == 3
A_SCALE = 64.0
K_SCALE = 64.0
R_SCALE = 16.0
S_SCALE = 16.0
O_SCALE = K_SCALE * S_SCALE
assert O_SCALE == K_SCALE * R_SCALE
PADS = E + 1
LEVELS = 7
W_SCALE = 256.0
H_SCALE = 64.0
PIECE = 2 * E * HID // T


def build(nc, x, wq, wk, wvg, wb, wo, norm_w, router, w1, w2, fconst, iconst, out):
    fp32, fp16, i32 = mybir.dt.float32, mybir.dt.float16, mybir.dt.int32
    ALU, ACT, AX = mybir.AluOpType, mybir.ActivationFunctionType, mybir.AxisListType
    ctx = ExitStack()
    with ctx:
        def sb(name, shape, dt=fp32):
            return ctx.enter_context(nc.sbuf_tensor(name, shape, dt))

        def sem(name):
            return ctx.enter_context(nc.semaphore(name))

        routed = nc.dram_tensor("routed_rows", [ROWS, RW], fp32, kind="Internal").ap()
        table_dram = nc.dram_tensor("tile_table_dram", [P, 2], i32, kind="Internal").ap()
        table_f_dram = nc.dram_tensor("tile_experts_dram", [P, 1], fp32, kind="Internal").ap()

        w1_hi = sb("w1_hi", [P, KC * E * HID], fp16)
        w1_lo = sb("w1_lo", [P, KC * E * HID], fp16)
        w2_s = sb("w2_s", [P, KH * E, 2, D], fp16)
        wqk = sb("wqk", [P, 2, 2, KC, H * DK], fp16)
        wq_s, wk_s = wqk[:, 0, :, :, :], wqk[:, 1, :, :, :]
        wvg_s = sb("wvg_s", [P, 2, KC, 2 * H * DV], fp16)
        wb_s = sb("wb_s", [P, 2, KC, H], fp16)
        wo_s = sb("wo_s", [P, 2, KC, D], fp16)
        wb_in = sb("wb_in", [P, KC, H])
        router_s = sb("router_s", [P, KC, E])
        normw_s = sb("normw_s", [P, DV])
        stage = w2_s[:, :, :, :].rearrange("p m v n -> p (m v n)").bitcast(fp32)
        def staged(width, before):
            n = KC * width
            at = KH * E * D - before - n
            return stage[:, at:at + n].rearrange("p (k n) -> p k n", k=KC), before + n
        wk_in, used = staged(H * DK, 0)
        wvg_in, used = staged(2 * H * DV, used)
        wq_in, used = staged(H * DK, used)
        wo_in, used = staged(D, used)
        fc = sb("fc", [P, FCONST])
        ident = fc[:, 0:128]
        causal = fc[:, 128:256]
        before_neg = fc[:, 256:384]
        ones = fc[:, 384:512]
        pref = fc[:, 512:520]
        region = fc[:, 520:528]
        lane = fc[:, 528:529]
        token_id = fc[:, 529:529 + T]
        half_neg = fc[:, 561:577]
        mask_s = sb("mask_s", [P, 2 * LEVELS, 64], mybir.dt.int8)

        x_s = sb("x_s", [P, C, D])
        xn = sb("xn", [P, D])
        xnT = sb("xnT", [P, 2, KC, P], fp16)
        KQ = sb("KQ", [P, 2, 2, H, 2, P], fp16)
        KpAT = sb("KpAT", [P, 2, 2, H, DK])
        Kp = KpAT[:, 0, :, :, :]
        mask_in = Kp[:, :, :, :].rearrange("p s h n -> p (s h n)")[:, 0:2 * LEVELS * 64].bitcast(i32)
        Vp = sb("Vp", [P, 2, H, DV])
        gs = sb("gs", [P, 2, H, DV])
        AT = KpAT[:, 1, :, :, :]
        Kp_s = sb("Kp_s", [P, 2, H, DK], fp16)
        AT_s = sb("AT_s", [P, 2, H, P], fp16)
        R_s = sb("R_s", [P, 2, H, DV], fp16)
        W_s = sb("W_s", [P, 2, H, DV], fp16)
        S_s = sb("S_s", [P, 2, H, DV], fp16)
        Lh = sb("Lh", [P, 2, H, P], fp16)
        Ll = sb("Ll", [P, H, P], fp16)
        X = sb("X", [P, 2, H, P], fp16)
        XT = sb("XT", [P, 2, H, P], fp16)
        Y = sb("Y", [P, H, P], fp16)
        ER = sb("ER", [P, H, P], fp16)
        dXT = sb("dXT", [P, H, P], fp16)
        negI = sb("negI", [P, P], fp16)
        S = sb("S", [P, H, DV])
        sq = sb("sq", [P, H, DK])
        nL = sq[:, :, :]
        osq = sb("osq", [P, H, DV])
        oT = sb("oT", [P, 2, KC, P], fp16)
        rowA = sb("rowA", [P, 2 * C, RW])
        xn2T = sb("xn2T", [P, KC, P])
        wst = sb("wst", [P, PIECE])
        st6 = sb("st6", [P, 6])
        mv = sb("mv", [P, 2])
        rstd = sb("rstd", [P, 1])
        eb = sb("eb", [P, H])
        ks = sb("ks", [P, 2 * H])
        karg = sb("karg", [P, 2 * H])
        kscale = sb("kscale", [P, 2 * H])
        osum = sb("osum", [P, H])
        oarg = sb("oarg", [P, H])
        ors = sb("ors", [P, H])
        st6b = sb("st6b", [P, 6])
        mv2 = sb("mv2", [P, 2])
        rstd2 = sb("rstd2", [P, 1])
        logits = sb("logits", [P, C, E])
        r8 = [sb(f"r8_{i}", [P, C, E]) for i in range(8)]
        r1 = [sb(f"r1_{i}", [P, C]) for i in range(9)]
        first = sb("first", [P, C, E])
        second = sb("second", [P, C, E])
        both = sb("both", [P, C, E])
        run = sb("run", [P, E])
        rbase = sb("rbase", [P, C, E])
        pos = sb("pos", [P, C, E])
        slot = sb("slot", [P, 2, C], i32)
        zrow = sq[:, :, :].rearrange("p h n -> p (h n)")[:, 0:RW]
        t8 = [r8[i][:, 0, :] for i in range(8)]
        t8i = sb("t8i", [P, E], i32)
        t8j = sb("t8j", [P, E], i32)
        pad_row = sb("pad_row", [P, E], i32)
        tab_f = sb("tab_f", [P, 2])
        tab_i = sb("tab_i", [P, 2], i32)
        tab = S[:, :, :].rearrange("p h n -> p (h n)").bitcast(i32)
        experts_b = Vp[:, 0, :, :].rearrange("p h n -> p (h n)")
        xg = rowA[:, :, :].rearrange("p (q a) n -> p q a n", a=2)
        x_f = x_s[:, :, :].rearrange("p c n -> p (c n)").bitcast(fp16).rearrange("p (s k n) -> p s k n", s=4, k=KC)
        xTh, xTl = x_f[:, 0:2, :, :], x_f[:, 2:4, :, :]
        hf = KQ[:, :, :, :, :, :].rearrange("p s v h a n -> p (s v h a n)").bitcast(fp32).rearrange("p (m n) -> p m n", m=4)
        hhi = wqk[:, :, :, :, :].rearrange("p s v k n -> p (s v k n)").rearrange("p (s m n) -> p s m n", s=2, m=KH)
        hlo = KpAT[:, :, :, :, :].rearrange("p a s h n -> p (a s h n)").bitcast(fp16).rearrange("p (s m n) -> p s m n", s=2, m=KH)
        yrow = wvg_s[:, :, :, :].rearrange("p v k n -> p (v k n)").bitcast(fp32).rearrange("p (q a n) -> p q a n", q=2, a=2)
        yidx = sb("yidx", [P, 4, 2], i32)
        gate = sb("gate", [P, 2, 2])
        gsel = sb("gsel", [P, 2, 2])

        PS = [ctx.enter_context(nc.psum_tensor(f"ps{i}", [P, 512], fp32)) for i in range(8)]
        def heads(ap, n):
            return ap.rearrange("p (h n) -> p h n", h=n)
        p_y = heads(PS[0][:, 0:256], H)
        p_x = heads(PS[1][:, 0:256], H)
        p_xt = heads(PS[1][:, 256:512], H)
        p_kv = PS[2][:, :]
        p_r = heads(PS[3][:, :], H)
        p_o = heads(PS[3][:, 0:256], H)
        p_p = heads(PS[4][:, 0:256], H)
        p_u = heads(PS[4][:, 256:512], H)
        p_q = heads(PS[5][:, :], H)
        p_kT = heads(PS[5][:, :], H)
        p_gram = [PS[5 + a][:, :].rearrange("p (h a n) -> p h a n", h=2, a=2) for a in range(2)]
        p_xnT = PS[6][:, 0:256]
        p_rank = PS[6][:, 0:C * E]
        p_tot = PS[6][:, C * E:2 * C * E]
        p_beta = PS[7][:, 0:H]
        p_oT = PS[7][:, 0:256]
        p_wo = PS[7][:, 0:256]
        p_xn2T = PS[7][:, 0:256]
        p_lg = PS[7][:, 0:E]
        p_gT = PS[0][:, :].rearrange("p (k n) -> p k n", k=KC)
        p_h = [PS[1 + m] for m in range(4)]
        p_yo = [PS[5 + a][:, :].rearrange("p (v n) -> p v n", v=2) for a in range(2)]

        s_const = sem("const_loaded")
        s_wload = [sem(f"{n}_loaded") for n in ("wk", "wvg", "wq", "wo")]
        s_wsh = sem("attention_weight_hi")
        s_wsl = sem("attention_weight_lo")
        s_x = [sem(f"x_loaded{c}") for c in range(C)]
        s_x1out = [sem(f"x1_stored{c}") for c in range(C)]
        s_w = [sem(f"w_loaded{q}") for q in range(2)]
        s_whi = sem("w_hi_ready")
        s_wlo = sem("w_lo_ready")
        s_init = sem("buffers_initialised")
        s_held = [sem("vector_waits_held"), sem("pool_waits_held")]
        pool_engine = nc.gpsimd
        s_xn = sem("xn_ready")
        s_xnTp = sem("xnT_in_psum")
        s_xnTs = sem("xnT_hi_in_sbuf")
        s_xnTl = sem("xnT_lo_in_sbuf")
        s_bps = sem("beta_in_psum")
        s_kps = sem("k_in_psum")
        s_ksq = sem("k_squared")
        s_eb = sem("exp_beta_ready")
        s_karg = sem("k_scale_argument")
        s_kscale = sem("k_scale_ready")
        s_kp = sem("kprime_ready")
        s_kTp = sem("kT_in_psum")
        s_kTs = sem("kT_hi_in_sbuf")
        s_kTl = sem("kT_lo_in_sbuf")
        s_kh = sem("kprime_hi_ready")
        s_kl = sem("kprime_lo_ready")
        s_qps = sem("qT_in_psum")
        s_qs = sem("qT_hi_in_sbuf")
        s_ql = sem("qT_lo_in_sbuf")
        s_vgps = sem("v_g_in_psum")
        s_th = sem("tanh_g_ready")
        s_gs = sem("v_and_gate_ready")
        s_gram = sem("gram_in_psum")
        s_nL = sem("neg_l_ready")
        s_Lh = sem("l_hi_ready")
        s_Ll = sem("l_lo_ready")
        s_AT = sem("masked_scores_ready")
        s_ATh = sem("scores_hi_ready")
        s_ATl = sem("scores_lo_ready")
        s_Xi = sem("inverse_initialised")
        s_yps = sem("y_in_psum")
        s_ys = sem("y_in_sbuf")
        s_xps = sem("update_in_psum")
        s_xup = sem("inverse_updated")
        s_rps = sem("residual_product_in_psum")
        s_er = sem("residual_product_in_sbuf")
        s_zps = sem("correction_in_psum")
        s_z = sem("corrected_inverse_ready")
        s_pps = sem("state_product_in_psum")
        s_r = sem("r_ready")
        s_rh = sem("r_hi_ready")
        s_rl = sem("r_lo_ready")
        s_wps = sem("w_in_psum")
        s_ws = sem("w_hi_in_sbuf")
        s_wl = sem("w_lo_in_sbuf")
        s_ops = sem("o_in_psum")
        s_ups = sem("state_update_in_psum")
        s_s = sem("state_ready")
        s_sh = sem("state_hi_ready")
        s_sl = sem("state_lo_ready")
        s_osq = sem("o_squared")
        s_oarg = sem("o_scale_argument")
        s_ors = sem("o_scale_ready")
        s_on = sem("o_normalised")
        s_oTp = sem("oT_in_psum")
        s_oTs = sem("oT_hi_in_sbuf")
        s_oTl = sem("oT_lo_in_sbuf")
        s_wops = sem("attention_out_in_psum")
        s_res = sem("residual_ready")
        s_mv = sem("ln1_variance")
        s_rstd = sem("ln1_rstd")
        s_mv2 = sem("ln2_variance")
        s_rstd2 = sem("ln2_rstd")
        s_xn2 = sem("xn2_ready")
        s_xn2Tp = sem("xn2T_in_psum")
        s_xn2Ts = sem("xn2T_in_sbuf")
        s_lgps = sem("logits_in_psum")
        s_lg = sem("logits_ready")
        s_rd = sem("logit_differences")
        s_rexp = sem("logit_exponentials")
        s_both = sem("expert_masks_ready")
        s_rank = sem("ranks_in_psum")
        s_pos = sem("positions_ready")
        s_slot = sem("slots_ready")
        s_spare = sem("spare_rows_ready")
        s_scat = [sem(f"rows_scattered{c}") for c in range(C)]
        s_tail = sem("tail_tables_ready")
        s_pads = sem("pads_written")
        s_tabd = sem("table_in_dram")
        s_tab = sem("table_loaded")
        s_dve = sem("dve_step")
        s_xg = [sem(f"xg_loaded{q}") for q in range(4)]
        s_gTp = sem("xgT_in_psum")
        s_gTh = sem("xgT_hi_ready")
        s_gTl = sem("xgT_lo_ready")
        s_hps = sem("hidden_in_psum")
        s_gelu = sem("gelu_ready")
        s_hhi = sem("hidden_hi_ready")
        s_hlo = sem("hidden_lo_ready")
        s_yops = sem("expert_out_in_psum")
        s_yrow = sem("expert_rows_ready")
        s_acc = sem("rows_accumulated")

        block = ctx.enter_context(nc.Block())

        def up_to(eng, s, per, t, k):
            b, c = t
            value = b * (per * C) + (per * c + k)
            if not (isinstance(value, int) and value <= 0):
                eng.wait_ge(s, value)

        def hold(eng):
            eng.sem_inc(s_held[eng is pool_engine])

        def before_(t, n):
            return (t[0], t[1] - n)

        def after_(t, n=1):
            return (t[0], t[1] + n)

        def sequences(eng, body):
            body(0, 0, True, False)
            with eng.Fori(0, (B - 2) // 2) as pair:
                body(pair * 2 + 1, 1, False, False)
                body(pair * 2 + 2, 0, False, False)
            body(B - 1, 1, False, True)

        def even(ap, lev):
            s = 1 << lev
            return ap.rearrange("p h (n two s) -> p h n two s", two=2, s=s)[:, :, :, 0, :]

        def odd(ap, lev):
            s = 1 << lev
            return ap.rearrange("p h (n two s) -> p h n two s", two=2, s=s)[:, :, :, 1, :]

        def packed(ap, lev):
            return ap.rearrange("p h (n s) -> p h n s", s=1 << lev)

        def level_mask(lev, transposed, heads):
            m = mask_s[:, 2 * lev + transposed, :].rearrange("p (n s) -> p n s", s=1 << lev).unsqueeze(1)
            return m.broadcast_to([P, heads, 64 >> lev, 1 << lev])

        def col(ap, n):
            return ap.unsqueeze(2).broadcast_to([P, ap.shape[1], n])

        def pad(eng, e):
            row = eng.value_load(pad_row[0:1, e:e + 1], min_val=0, max_val=SPARE - PE_TOK)
            eng.dma_start(routed[bass.ds(row, PE_TOK), :].rearrange("(a p) n -> p a n", p=P),
                          zrow.unsqueeze(1).broadcast_to([P, PE_TOK // P, RW])).then_inc(s_pads, 16)

        @block.sync
        def _(sp):
            early = [(fc[:, 0:FCONST], fconst), (mask_in, iconst.rearrange("p a b -> p (a b)")),
                     (wb_in[:, :, :], wb.rearrange("(k p) n -> p k n", p=P))]
            late = [(router_s[:, :, :], router.rearrange("(k p) n -> p k n", p=P)),
                    (normw_s[:, :], norm_w.partition_broadcast(P))]
            weights = [(wk_in, wk), (wvg_in, wvg), (wq_in, wq), (wo_in, wo)]
            sp.dma_start(x_s[:, 0, :], x[0, :, :]).then_inc(s_x[0], 16)
            for dst, src in early + late:
                sp.dma_start(dst, src).then_inc(s_const, 16)
            assert len(early + late) == CONST_LOADS
            for n, (dst, src) in enumerate(weights):
                sp.dma_start(dst, src.rearrange("(k p) n -> p k n", p=P)).then_inc(s_wload[n], 16)
            for c in range(1, C):
                sp.dma_start(x_s[:, c, :], x[c, :, :]).then_inc(s_x[c], 16)

            def store(b, c):
                up_to(sp, s_res, 1, (b, c), 1)
                sp.dma_start(out[bass.ds((b * C + c) * P, P), :], x_s[:, c % C, :]).then_inc(s_x1out[c % C], 16)

            def piece(b, c, q):
                up_to(sp, s_wlo, 2, (b, c), q)
                sp.dma_start(wst[:, :], (w1, w2)[q][bass.ds(b * C + c, 1), :, :].rearrange("a p n -> p (a n)")).then_inc(s_w[q], 16)

            def body(b, par, first, last):
                for c in range(C):
                    piece(b, c, 0)
                    if not (first and c < 2):
                        store(b, c - 2)
                        if not (last and c >= 2):
                            d = (c + 2) % C
                            sp.wait_ge(s_x1out[d], b * 16 + (16 if c >= 2 else 0))
                            up_to(sp, s_xn2, 1, (b, c - 2), 1)
                            sp.dma_start(x_s[:, d, :], x[bass.ds(b * C + (c + 2), 1), :, :].rearrange("a p n -> p (a n)")).then_inc(s_x[d], 16)
                    piece(b, c, 1)
            sequences(sp, body)
            store(B - 1, C - 2)
            store(B - 1, C - 1)
            sp.wait_ge(s_tail, 1)
            pad(sp, 0)
            sp.wait_ge(s_tail, 2)
            sp.dma_start(table_dram, tab_i[:, :]).then_inc(s_tabd, 16)
            sp.dma_start(table_f_dram, tab_f[:, 0:1]).then_inc(s_tabd, 16)
            pad(sp, 1)
            pad(sp, 2)
            sp.wait_ge(s_tabd, 32)
            up_to(sp, s_ops, 1, (B - 1, C - 1), 1)
            sp.dma_start(tab[0:1, :], table_dram.rearrange("p n -> (p n)").unsqueeze(0)).then_inc(s_tab, 16)
            sp.dma_start(experts_b[:, 0:P], table_f_dram.rearrange("p n -> (p n)").partition_broadcast(P)).then_inc(s_tab, 16)
            pad(sp, 3)
            sp.dma_start(out[B * N:B * N + P, :], zrow[:, 0:D]).then_inc(s_pads, 16)
            sp.wait_ge(s_tab, 32)
            sp.wait_ge(s_pads, 16 * PADS)
            for c in range(C):
                sp.wait_ge(s_scat[c], 32 * B + 16)

            def load_rows(i, q):
                row = sp.value_load(tab[0:1, bass.ds(i * 8 + (2 * q + 1), 1)], min_val=0, max_val=SPARE)
                sp.dma_start(xg[:, q % 4, :, :], routed[bass.ds(row, PE_TOK), :].rearrange("(a p) n -> p a n", p=P))\
                    .then_inc(s_xg[q % 4], 16)

            for q in range(3):
                load_rows(0, q)

            def expert_body(i, last):
                for q in range(0 if last else 4):
                    value = i * 4 + q
                    if not (isinstance(value, int) and value <= 0):
                        sp.wait_ge(s_yrow, value)
                    load_rows(i, q + 3)
            expert_body(0, False)
            with sp.Fori(1, MAXT // 4) as i:
                expert_body(i, False)
            expert_body(MAXT // 4, True)

        @block.gpsimd
        def _(pool):
            pool.memset(Y[:, :, :], 0.0).then_inc(s_init, 1)
            pool.memset(S[:, :, :], 0.0)
            pool.memset(S_s[:, :, :, :], 0.0).then_inc(s_init, 1)
            pool.wait_ge(s_const, 16 * CONST_LOADS)

            def rsqrt(dst, src, n):
                return pool.tensor_tensor(dst, src, half_neg[:, 0:n], ALU.pow)

            def ln1(t):
                up_to(pool, s_mv, 1, t, 1)
                rsqrt(rstd[:, :], mv[:, 1:2], 1).then_inc(s_rstd, 1)

            def kscale_(t):
                up_to(pool, s_karg, 1, t, 1)
                rsqrt(kscale[:, :], karg[:, :], 2 * H).then_inc(s_kscale, 1)

            def split_lo(b, c, q):
                pool.wait_ge(s_whi, b * (2 * C) + (2 * c + q + 1))
                if q == 0:
                    at = bass.ds(b * (C * PIECE) + c * PIECE, PIECE)
                    lo, hi, src = w1_lo[:, at], w1_hi[:, at], wst[:, :]
                else:
                    n = PIECE // D
                    at = bass.ds(b * (C * n) + c * n, n)
                    lo, hi, src = w2_s[:, at, 1, :], w2_s[:, at, 0, :], wst[:, :].rearrange("p (m n) -> p m n", n=D)
                pool.tensor_tensor(lo, src, hi, ALU.subtract).then_inc(s_wlo, 1)

            def low_parts(t):
                par = t[1] % 2
                up_to(pool, s_ops, 1, before_(t, 1), 1)
                up_to(pool, s_kh, 1, t, 1)
                pool.tensor_tensor(Kp_s[:, 1, :, :], Kp[:, par, :, :], Kp_s[:, 0, :, :], ALU.subtract).then_inc(s_kl, 1)
                up_to(pool, s_ATh, 1, t, 1)
                pool.tensor_tensor(AT_s[:, 1, :, :], AT[:, par, :, :], AT_s[:, 0, :, :], ALU.subtract).then_inc(s_ATl, 1)

            def l_low(t):
                up_to(pool, s_rps, 1, before_(t, 1), 1)
                up_to(pool, s_Lh, 1, t, 1)
                pool.tensor_tensor(Ll[:, :, :], nL, Lh[:, t[1] % 2, :, :], ALU.subtract).then_inc(s_Ll, 1)

            def epilogue(t):
                up_to(pool, s_oarg, 1, t, 1)
                rsqrt(ors[:, :], oarg[:, :], H).then_inc(s_ors, 1)

            def epilogue2(t):
                up_to(pool, s_mv2, 1, t, 1)
                rsqrt(rstd2[:, :], mv2[:, 1:2], 1).then_inc(s_rstd2, 1)

            def scatter(b, par, c):
                pool.wait_ge(s_slot, b + 1)
                hold(pool)
                for k in range(2):
                    pool.indirect_dma_start(
                        out=routed, out_offset=bass.IndirectOffsetOnAxis(ap=slot[:, k, c:c + 1], axis=0),
                        in_=rowA[:, par * C + c, :], in_offset=None).then_inc(s_scat[c], 16)

            ln1((0, 0))
            ln1((0, 1))
            kscale_((0, 0))
            pool.memset(rowA[:, C:2 * C, :], 0.0).then_inc(s_spare, 1)
            pool.wait_ge(s_spare, 1)
            pool.tensor_scalar(rowA[:, C:2 * C, D + 3], rowA[:, C:2 * C, D + 3], lane, float(B * N), ALU.add, ALU.add).then_inc(s_spare, 1)
            pool.wait_ge(s_spare, 2)
            for c in range(C):
                part = c % 2 * 64
                pool.dma_start(routed[SPARE + 64 * c:SPARE + 64 * (c + 1), :], rowA[part:part + 64, C + c, :]).then_inc(s_scat[c], 16)

            def body(b, par, first, last):
                for c in range(C):
                    t = (b, c)
                    front, epi = not (last and c == C - 1), not (first and c == 0)
                    routed_now = c == 3 and not first
                    l_low(t)
                    if epi:
                        low_parts(before_(t, 1))
                    if epi and not (first and c == 1):
                        epilogue2(before_(t, 2))
                    if routed_now:
                        scatter(b - 1, 1 - par, 1)
                    if front:
                        kscale_(after_(t))
                    split_lo(b, c, 0)
                    if routed_now:
                        scatter(b - 1, 1 - par, 2)
                    if epi:
                        epilogue(before_(t, 1))
                    if not (last and c >= C - 2):
                        ln1(after_(t, 2))
                    split_lo(b, c, 1)
                    if routed_now:
                        scatter(b - 1, 1 - par, 3)
                    if c == 2 and not first:
                        scatter(b - 1, 1 - par, 0)
            sequences(pool, body)
            low_parts((B - 1, C - 1))
            epilogue2((B - 1, C - 2))
            epilogue((B - 1, C - 1))
            epilogue2((B - 1, C - 1))
            for c in range(C):
                scatter(B - 1, 1, c)
            pool.wait_ge(s_pads, 16 * PADS)
            for c in range(C):
                pool.wait_ge(s_x1out[c], 16 * B)

            def accumulate(i, q):
                pool.wait_ge(s_yrow, i * 4 + (q + 1))
                for a in range(2):
                    value = i * 128 + (32 * q + 16 * a)
                    if not (isinstance(value, int) and value <= 0):
                        pool.wait_ge(s_acc, value)
                    hold(pool)
                    pool.indirect_dma_start(
                        out=out, out_offset=bass.IndirectOffsetOnAxis(ap=yidx[:, q, a:a + 1], axis=0),
                        in_=yrow[:, q % 2, a, :], in_offset=None, compute_op=ALU.add).then_inc(s_acc, 16)
            for q in range(4):
                accumulate(0, q)
            with pool.Fori(1, MAXT // 4) as i:
                for q in range(4):
                    accumulate(i, q)
            for q in range(LAST):
                accumulate(MAXT // 4, q)
            pool.wait_ge(s_acc, 32 * MAXT)

        @block.scalar
        def _(act):
            def evac(dst, src, scale=1.0):
                return act.activation(dst, src, ACT.Copy, scale=scale)

            def xnT_evac(t):
                up_to(act, s_qps, 1, before_(t, 1), 1)
                up_to(act, s_vgps, 1, before_(t, 1), 1)
                up_to(act, s_xnTp, 1, t, 1)
                evac(xnT[:, 0, :, :].rearrange("p k n -> p (k n)"), p_xnT).then_inc(s_xnTs, 1)

            def k_square(t):
                up_to(act, s_karg, 1, before_(t, 1), 1)
                up_to(act, s_Ll, 1, before_(t, 1), 1)
                up_to(act, s_kps, 1, t, 1)
                for h in range(H):
                    act.activation(sq[:, h, :], p_kv[:, h * DK:(h + 1) * DK], ACT.Square, accum_out=ks[:, h:h + 1]).then_inc(s_ksq, 1)

            def beta_exp(t):
                up_to(act, s_karg, 1, before_(t, 1), 1)
                up_to(act, s_bps, 1, t, 1)
                act.activation(eb[:, :], p_beta, ACT.Exp, scale=-1.0 / A_SCALE).then_inc(s_eb, 1)

            def q_evac(t):
                up_to(act, s_ops, 1, before_(t, 2), 1)
                up_to(act, s_qps, 1, t, 1)
                act.activation(KQ[:, t[1] % 2, 0, :, 1, :], p_q, ACT.Copy, scale=Q_SCALE).then_inc(s_qs, 1)

            def kT_evac(t):
                up_to(act, s_kTp, 1, t, 1)
                evac(KQ[:, t[1] % 2, 0, :, 0, :], p_kT).then_inc(s_kTs, 1)

            def kprime_hi(t):
                up_to(act, s_ops, 1, before_(t, 1), 1)
                up_to(act, s_kp, 1, t, 1)
                evac(Kp_s[:, 0, :, :], Kp[:, t[1] % 2, :, :]).then_inc(s_kh, 1)

            def scores_hi(t):
                up_to(act, s_ops, 1, before_(t, 1), 1)
                up_to(act, s_AT, 2, t, 2)
                evac(AT_s[:, 0, :, :], AT[:, t[1] % 2, :, :]).then_inc(s_ATh, 1)

            def r_hi(t):
                up_to(act, s_wps, 1, before_(t, 1), 1)
                up_to(act, s_r, 1, t, 1)
                evac(R_s[:, 0, :, :], Vp[:, t[1] % 2, :, :], R_SCALE).then_inc(s_rh, 1)

            def state_hi(t):
                up_to(act, s_s, 1, t, 1)
                evac(S_s[:, 0, :, :], S[:, :, :], S_SCALE).then_inc(s_sh, 1)

            def tanh_g(t):
                up_to(act, s_on, 1, before_(t, 2), 1)
                up_to(act, s_vgps, 1, t, 1)
                act.activation(gs[:, t[1] % 2, :, :], p_kv[:, 256:512].rearrange("p (h n) -> p h n", h=H), ACT.Tanh,
                               scale=0.5 / A_SCALE).then_inc(s_th, 1)

            def l_high(t):
                up_to(act, s_yps, 7, before_(t, 2), 7)
                up_to(act, s_rps, 1, before_(t, 2), 1)
                up_to(act, s_nL, 1, t, 1)
                evac(Lh[:, t[1] % 2, :, :], nL).then_inc(s_Lh, 1)

            def y_evac(t, lev):
                up_to(act, s_yps, 7, t, lev + 1)
                evac(even(Y[:, :, :], lev), packed(p_y, lev)).then_inc(s_ys, 1)

            def r_evac(t):
                up_to(act, s_zps, 1, before_(t, 1), 1)
                up_to(act, s_rps, 1, t, 1)
                evac(ER[:, :, :], p_r).then_inc(s_er, 1)

            def w_evac(t):
                up_to(act, s_ops, 1, before_(t, 1), 1)
                up_to(act, s_s, 1, before_(t, 1), 1)
                up_to(act, s_wps, 1, t, 1)
                evac(W_s[:, 0, :, :], p_p).then_inc(s_ws, 1)

            def o_square(t):
                up_to(act, s_oTp, 1, before_(t, 1), 1)
                up_to(act, s_ops, 1, t, 1)
                for h in range(H):
                    act.activation(osq[:, h, :], p_o[:, h, :], ACT.Square, scale=1.0 / O_SCALE,
                                   accum_out=osum[:, h:h + 1]).then_inc(s_osq, 1)

            def init_inverse(t, which):
                up_to(act, s_wps, 1, before_(t, 2), 1)
                evac(which[:, t[1] % 2, :, :], ident.unsqueeze(1).broadcast_to([P, H, P])).then_inc(s_Xi, 1)

            def oT_evac(t):
                up_to(act, s_oTp, 1, t, 1)
                evac(oT[:, 0, :, :].rearrange("p k n -> p (k n)"), p_oT).then_inc(s_oTs, 1)

            def xn2T_evac(t):
                up_to(act, s_xn2Tp, 1, t, 1)
                evac(xn2T[:, :, :].rearrange("p k n -> p (k n)"), p_xn2T).then_inc(s_xn2Ts, 1)

            def split_hi(b, c, q):
                act.wait_ge(s_w[q], b * (16 * C) + 16 * (c + 1))
                if q == 0:
                    dst, src = w1_hi[:, bass.ds(b * (C * PIECE) + c * PIECE, PIECE)], wst[:, :]
                else:
                    n = PIECE // D
                    dst = w2_s[:, bass.ds(b * (C * n) + c * n, n), 0, :]
                    src = wst[:, :].rearrange("p (m n) -> p m n", n=D)
                evac(dst, src, W_SCALE)
                evac(wst[:, :], wst[:, :], W_SCALE).then_inc(s_whi, 1)

            def weight_hi(n, dst, src):
                act.wait_ge(s_wload[n], 16)
                evac(dst, src, A_SCALE).then_inc(s_wsh, 1)

            def route_exp(b):
                act.wait_ge(s_rd, b + 1)
                act.activation(r8[1][:, :, :], r8[0][:, :, :], ACT.Exp).then_inc(s_rexp, 1)

            act.wait_ge(s_const, 16 * CONST_LOADS)
            act.wait_ge(s_init, 2)
            evac(wb_s[:, 0, :, :], wb_in[:, :, :], A_SCALE)
            weight_hi(0, wk_s[:, 0, :, :], wk_in)
            xnT_evac((0, 0))
            weight_hi(1, wvg_s[:, 0, :, :], wvg_in)
            weight_hi(2, wq_s[:, 0, :, :], wq_in)
            weight_hi(3, wo_s[:, 0, :, :], wo_in)
            beta_exp((0, 0))
            k_square((0, 0))
            q_evac((0, 0))
            kT_evac((0, 0))
            tanh_g((0, 0))
            init_inverse((0, 0), X)
            init_inverse((0, 0), XT)
            l_high((0, 0))

            def body(b, par, first, last):
                for c in range(C):
                    t = (b, c)
                    front, epi = not (last and c == C - 1), not (first and c == 0)
                    nxt, prv = after_(t), before_(t, 1)
                    if epi:
                        r_evac(prv)
                    if front:
                        xnT_evac(nxt)
                    y_evac(t, 1)
                    if epi:
                        r_hi(prv)
                        kprime_hi(prv)
                        scores_hi(prv)
                    y_evac(t, 2)
                    if epi:
                        w_evac(prv)
                    split_hi(b, c, 0)
                    y_evac(t, 3)
                    if c == 2 and not first:
                        route_exp(b - 1)
                    if front:
                        beta_exp(nxt)
                        k_square(nxt)
                        init_inverse(nxt, X)
                    y_evac(t, 4)
                    if epi:
                        o_square(prv)
                    if front:
                        q_evac(nxt)
                    y_evac(t, 5)
                    if epi and not (first and c == 1):
                        xn2T_evac(before_(t, 2))
                    if epi:
                        state_hi(prv)
                    if front:
                        init_inverse(nxt, XT)
                        kT_evac(nxt)
                    y_evac(t, 6)
                    split_hi(b, c, 1)
                    if epi:
                        oT_evac(prv)
                    if front:
                        l_high(nxt)
                        tanh_g(nxt)
            sequences(act, body)
            last_tile = (B - 1, C - 1)
            r_evac(last_tile)
            r_hi(last_tile)
            kprime_hi(last_tile)
            scores_hi(last_tile)
            w_evac(last_tile)
            xn2T_evac(before_(last_tile, 1))
            o_square(last_tile)
            oT_evac(last_tile)
            xn2T_evac(last_tile)
            route_exp(B - 1)
            act.wait_ge(s_tail, 1)
            for e in range(4, E):
                pad(act, e)

            def xT_hi(i, q):
                act.wait_ge(s_gTp, i * 4 + (q + 1))
                if not (isinstance(i, int) and i * 4 + q < 2):
                    act.wait_ge(s_hps, i * 16 + 4 * (q - 1))
                evac(xTh[:, q % 2, :, :], p_gT).then_inc(s_gTh, 1)

            def hidden(i, q):
                for m in range(4):
                    act.wait_ge(s_hps, i * 16 + (4 * q + m + 1))
                    if not (isinstance(i, int) and i * 4 + q < 1):
                        act.wait_ge(s_hlo, i * 16 + (4 * (q - 1) + m + 1))
                    if m == 0 and not (isinstance(i, int) and i * 4 + q < 2):
                        act.wait_ge(s_yops, i * 4 + (q - 1))
                    act.activation(hf[:, m, :], p_h[m][:, :], ACT.Gelu, scale=1.0 / W_SCALE).then_inc(s_gelu, 1)
                    act.wait_ge(s_gelu, i * 16 + (4 * q + m + 1))
                    evac(hhi[:, q % 2, 2 * m:2 * m + 2, :], hf[:, m, :].rearrange("p (m n) -> p m n", m=2),
                         H_SCALE).then_inc(s_hhi, 1)

            xT_hi(0, 0)
            xT_hi(0, 1)
            hidden(0, 0)

            def expert_body(i, last):
                for q in range(LAST if last else 4):
                    if not (last and q + 2 >= LAST):
                        xT_hi(i, q + 2)
                    if not (last and q + 1 >= LAST):
                        hidden(i, q + 1)
            expert_body(0, False)
            with act.Fori(1, MAXT // 4) as i:
                expert_body(i, False)
            expert_body(MAXT // 4, True)

        @block.tensor
        def _(pe):
            def mm(dst, lhsT, rhs, start=True, stop=True, **kw):
                return pe.matmul(dst, lhsT, rhs, start=start, stop=stop, **kw)

            PARTS = ((0, 0), (0, 1), (1, 0))

            def product(dst, lhs, rhs, start=True, stop=True, **kw):
                for n, (a, b) in enumerate(PARTS):
                    last = mm(dst, lhs[a], rhs[b], start and n == 0, stop and n == 2, **kw)
                return last

            def split_mm(dst, lhs, rhs, k):
                for n, (a, b) in enumerate(PARTS):
                    last = mm(dst, lhs(a, k), rhs(b, k), k == 0 and n == 0, k == KC - 1 and n == 2)
                return last

            def xnT_of(part, k):
                return xnT[:, part, k, :]

            def xnT_make(t):
                up_to(pe, s_AT, 2, before_(t, 1), 2)
                up_to(pe, s_xn, 1, t, 1)
                for k in range(KC):
                    last = pe.transpose(p_xnT[:, k * P:(k + 1) * P], xn[:, k * P:(k + 1) * P], ident)
                last.then_inc(s_xnTp, 1)

            def k_proj(t, k):
                if k == 0:
                    up_to(pe, s_gs, 1, before_(t, 1), 1)
                last = split_mm(p_kv, xnT_of, lambda part, k: wk_s[:, part, k, :], k)
                if k == KC - 1:
                    last.then_inc(s_kps, 1)

            def beta_proj(t):
                up_to(pe, s_xnTs, 1, t, 1)
                up_to(pe, s_xnTl, 1, t, 1)
                up_to(pe, s_res, 1, before_(t, 3), 1)
                for k in range(KC):
                    last = split_mm(p_beta, xnT_of, lambda part, k: wb_s[:, part, k, :], k)
                last.then_inc(s_bps, 1)

            def q_proj(t, a):
                if a == 0:
                    up_to(pe, s_AT, 2, before_(t, 1), 1)
                for h in range(2 * a, 2 * a + 2):
                    for k in range(KC):
                        last = split_mm(p_q[:, h, :], lambda part, k: wq_s[:, part, k, h * DK:(h + 1) * DK], xnT_of, k)
                if a == 1:
                    last.then_inc(s_qps, 1)

            def k_transposes(t):
                up_to(pe, s_qs, 1, t, 1)
                up_to(pe, s_ql, 1, t, 1)
                up_to(pe, s_kp, 1, t, 1)
                for h in range(H):
                    last = pe.transpose(p_kT[:, h, :], Kp[:, t[1] % 2, h, :], ident)
                last.then_inc(s_kTp, 1)

            def vg_proj(t, k):
                up_to(pe, s_kp, 1, t, 1)
                last = split_mm(p_kv, xnT_of, lambda part, k: wvg_s[:, part, k, :], k)
                if k == KC - 1:
                    last.then_inc(s_vgps, 1)

            def gram(t, a, ranked=None):
                for s in (s_kTs, s_kTl, s_qs, s_ql):
                    up_to(pe, s, 1, t, 1)
                if ranked is not None:
                    pe.wait_ge(s_pos, ranked)
                for h in range(2):
                    hh = [KQ[:, t[1] % 2, part, 2 * a + h, :, :] for part in range(2)]
                    last = product(p_gram[a][:, h, :, :], [x[:, 0, :] for x in hh], hh)
                last.then_inc(s_gram, 1)

            def y_make(t, lev):
                par = t[1] % 2
                if lev == 0:
                    up_to(pe, s_Lh, 1, t, 1)
                    up_to(pe, s_Xi, 2, t, 2)
                else:
                    up_to(pe, s_xup, 7, t, lev)
                for h in range(H):
                    last = mm(packed(p_y, lev)[:, h], Lh[:, par, h, :], even(X[:, par, :, :], lev)[:, h])
                last.then_inc(s_yps, 1)

            def x_make(t, lev):
                par = t[1] % 2
                up_to(pe, s_ys, 6, t, lev)
                for h in range(H):
                    mm(packed(p_x, lev)[:, h], XT[:, par, h, :], even(Y[:, :, :], lev)[:, h])
                    last = mm(packed(p_xt, lev)[:, h], Y[:, h, :], odd(XT[:, par, :, :], lev)[:, h])
                last.then_inc(s_xps, 1)

            def residual_make(t):
                par = t[1] % 2
                up_to(pe, s_on, 1, before_(t, 1), 1)
                up_to(pe, s_Ll, 1, t, 1)
                up_to(pe, s_xup, 7, t, 7)
                for h in range(H):
                    mm(p_r[:, h, :], Lh[:, par, h, :], X[:, par, h, :], True, False)
                    mm(p_r[:, h, :], Ll[:, h, :], X[:, par, h, :], False, False)
                    last = mm(p_r[:, h, :], negI[:, :], X[:, par, h, :], False, True)
                last.then_inc(s_rps, 1)

            def correction_make(t):
                up_to(pe, s_er, 1, t, 1)
                for h in range(H):
                    last = mm(p_r[:, h, :], ER[:, h, :], XT[:, t[1] % 2, h, :])
                last.then_inc(s_zps, 1)

            def kq(t, h, a):
                return [KQ[:, t[1] % 2, part, h, a, :] for part in range(2)]

            def parts(ap, h):
                return [ap[:, part, h, :] for part in range(2)]

            def p_make(t):
                for s in (s_ws, s_wl, s_sh, s_sl):
                    up_to(pe, s, 1, before_(t, 1), 1)
                for h in range(H):
                    last = product(p_p[:, h, :], kq(t, h, 0), parts(S_s, h))
                last.then_inc(s_pps, 1)

            def w_make(t):
                for s in (s_rh, s_rl, s_z):
                    up_to(pe, s, 1, t, 1)
                for h in range(H):
                    last = product(p_p[:, h, :], (XT[:, t[1] % 2, h, :], dXT[:, h, :]), parts(R_s, h))
                last.then_inc(s_wps, 1)

            def out_state(t):
                up_to(pe, s_z, 1, t, 1)
                for h in range(H):
                    product(p_o[:, h, :], kq(t, h, 1), parts(S_s, h), h == 0, False, skip_group_check=True)

            def state_make(t):
                for s in (s_ws, s_wl, s_kh, s_kl):
                    up_to(pe, s, 1, t, 1)
                if t[1] % C < C - 1:
                    for h in range(H):
                        last = product(p_u[:, h, :], parts(Kp_s, h), parts(W_s, h))
                    last.then_inc(s_ups, 1)

            def out_chunk(t):
                up_to(pe, s_ATh, 1, t, 1)
                up_to(pe, s_ATl, 1, t, 1)
                for h in range(H):
                    last = product(p_o[:, h, :], parts(AT_s, h), parts(W_s, h), False, h == H - 1, skip_group_check=True)
                last.then_inc(s_ops, 1)

            def oT_make(t):
                up_to(pe, s_lg, 1, before_(t, 1), 1)
                up_to(pe, s_on, 1, t, 1)
                for k in range(KC):
                    last = pe.transpose(p_oT[:, k * P:(k + 1) * P], osq[:, 2 * k:2 * k + 2, :].rearrange("p h n -> p (h n)"), ident)
                last.then_inc(s_oTp, 1)

            def wo_make(t):
                up_to(pe, s_oTs, 1, t, 1)
                up_to(pe, s_oTl, 1, t, 1)
                for k in range(KC):
                    last = split_mm(p_wo, lambda part, k: oT[:, part, k, :], lambda part, k: wo_s[:, part, k, :], k)
                last.then_inc(s_wops, 1)

            def xn2T_make(t, row, beta_tile=None):
                if beta_tile is None:
                    up_to(pe, s_res, 1, t, 1)
                else:
                    up_to(pe, s_eb, 1, beta_tile, 1)
                up_to(pe, s_xn2, 1, t, 1)
                for k in range(KC):
                    last = pe.transpose(p_xn2T[:, k * P:(k + 1) * P], rowA[:, row, k * P:(k + 1) * P], ident)
                last.then_inc(s_xn2Tp, 1)

            def logits_make(t):
                up_to(pe, s_xn2Ts, 1, t, 1)
                for k in range(KC):
                    last = mm(p_lg, xn2T[:, k, :], router_s[:, k, :], k == 0, k == KC - 1)
                last.then_inc(s_lgps, 1)

            def rank(b):
                pe.wait_ge(s_both, b + 1)
                m = both[:, :, :].rearrange("p c e -> p (c e)")
                mm(p_rank, before_neg, m)
                mm(p_tot, ones, m).then_inc(s_rank, 1)

            pe.wait_ge(s_const, 16 * CONST_LOADS)
            pe.wait_ge(s_init, 2)
            t0 = (0, 0)
            xnT_make(t0)
            pe.wait_ge(s_wsh, 1)
            pe.wait_ge(s_wsl, 1)
            beta_proj(t0)
            k_proj(t0, 0)
            k_proj(t0, 1)
            pe.wait_ge(s_wsh, 4)
            pe.wait_ge(s_wsl, 4)
            q_proj(t0, 0)
            q_proj(t0, 1)
            k_transposes(t0)
            vg_proj(t0, 0)
            vg_proj(t0, 1)
            gram(t0, 0)
            gram(t0, 1)

            def body(b, par, first, last):
                for c in range(C):
                    t = (b, c)
                    front, epi = not (last and c == C - 1), not (first and c == 0)
                    nxt, prv = after_(t), before_(t, 1)
                    epi2 = epi and not (first and c == 1)
                    y_make(t, 0)
                    if epi:
                        residual_make(prv)
                        p_make(prv)
                    if front:
                        xnT_make(nxt)
                    y_make(t, 1)
                    if epi:
                        correction_make(prv)
                    x_make(t, 1)
                    if epi2:
                        wo_make(before_(t, 2))
                    if front:
                        k_proj(nxt, 0)
                    y_make(t, 2)
                    x_make(t, 2)
                    if epi:
                        w_make(prv)
                    if front:
                        k_proj(nxt, 1)
                    y_make(t, 3)
                    if epi:
                        out_state(prv)
                    if front:
                        beta_proj(nxt)
                    x_make(t, 3)
                    if front:
                        q_proj(nxt, 0)
                    if epi:
                        state_make(prv)
                        out_chunk(prv)
                    y_make(t, 4)
                    if front:
                        q_proj(nxt, 1)
                    x_make(t, 4)
                    if epi2:
                        xn2T_make(before_(t, 2), (par * C + c - 2) % (2 * C), nxt if front else None)
                    y_make(t, 5)
                    x_make(t, 5)
                    if front:
                        k_transposes(nxt)
                    if epi2:
                        logits_make(before_(t, 2))
                    y_make(t, 6)
                    if c == 2 and not first:
                        rank(b - 1)
                    x_make(t, 6)
                    if front:
                        gram(nxt, 0)
                        gram(nxt, 1, b if c == 2 and not first else None)
                    if epi:
                        oT_make(prv)
                    if front:
                        vg_proj(nxt, 0)
                        vg_proj(nxt, 1)
            sequences(pe, body)
            last_tile = (B - 1, C - 1)
            residual_make(last_tile)
            p_make(last_tile)
            correction_make(last_tile)
            wo_make(before_(last_tile, 1))
            w_make(last_tile)
            out_state(last_tile)
            state_make(last_tile)
            out_chunk(last_tile)
            xn2T_make(before_(last_tile, 1), 2 * C - 2)
            logits_make(before_(last_tile, 1))
            oT_make(last_tile)
            wo_make(last_tile)
            xn2T_make(last_tile, 2 * C - 1)
            logits_make(last_tile)
            rank(B - 1)

            pe.wait_ge(s_tab, 32)
            pe.wait_ge(s_whi, 2 * T)
            pe.wait_ge(s_wlo, 2 * T)
            pe.wait_ge(s_slot, B)

            def xT_make(i, q):
                pe.wait_ge(s_xg[q % 4], i * 16 + 16 * (q // 4 + 1))
                if not (isinstance(i, int) and i * 4 + q < 1):
                    pe.wait_ge(s_gTl, i * 4 + q)
                for a in range(2):
                    for k in range(KC):
                        last = pe.transpose(p_gT[:, k, a * P:(a + 1) * P], xg[:, q % 4, a, k * P:(k + 1) * P], ident)
                last.then_inc(s_gTp, 1)

            def expert_of(i, q):
                return pe.value_load(tab[0:1, bass.ds(i * 8 + 2 * q, 1)], min_val=0, max_val=E - 1)

            def up(i, q):
                e = expert_of(i, q)
                pe.wait_ge(s_gTh, i * 4 + (q + 1))
                pe.wait_ge(s_gTl, i * 4 + (q + 1))
                hi, lo = xTh[:, q % 2, :, :], xTl[:, q % 2, :, :]
                for m in range(KH):
                    if m % 2 == 0 and not (isinstance(i, int) and i * 4 + q < 1):
                        pe.wait_ge(s_gelu, i * 16 + (4 * (q - 1) + m // 2 + 1))
                    dst = p_h[m // 2][:, (m % 2) * PE_TOK:(m % 2 + 1) * PE_TOK]
                    for k in range(KC):
                        off = e * HID + (k * E * HID + m * P)
                        wh, wl = w1_hi[:, bass.ds(off, P)], w1_lo[:, bass.ds(off, P)]
                        mm(dst, wh, hi[:, k, :], k == 0, False)
                        mm(dst, wh, lo[:, k, :], False, False)
                        last = mm(dst, wl, hi[:, k, :], False, k == KC - 1)
                    if m % 2 == 1:
                        last.then_inc(s_hps, 1)

            def down(i, q):
                e = expert_of(i, q)
                if not (isinstance(i, int) and i * 4 + q < 1):
                    pe.wait_ge(s_yrow, i * 4 + q)
                for m in range(KH):
                    if m % 2 == 0:
                        pe.wait_ge(s_hhi, i * 16 + (4 * q + m // 2 + 1))
                        pe.wait_ge(s_hlo, i * 16 + (4 * q + m // 2 + 1))
                    w = w2_s[:, bass.ds(e + m * E, 1), :, :].rearrange("p e v n -> p (e v n)")
                    for a in range(2):
                        both_parts = p_yo[a].rearrange("p v n -> p (v n)")
                        mm(both_parts, hhi[:, q % 2, m, a * P:(a + 1) * P], w, m == 0, False)
                        last = mm(p_yo[a][:, 0, :], hlo[:, q % 2, m, a * P:(a + 1) * P], w[:, 0:D], False, m == KH - 1)
                last.then_inc(s_yops, 1)

            xT_make(0, 0)
            xT_make(0, 1)
            up(0, 0)

            def expert_body(i, last):
                for q in range(LAST if last else 4):
                    if not (last and q + 2 >= LAST):
                        xT_make(i, q + 2)
                    if not (last and q + 1 >= LAST):
                        up(i, q + 1)
                    down(i, q)
            expert_body(0, False)
            with pe.Fori(1, MAXT // 4) as i:
                expert_body(i, False)
            expert_body(MAXT // 4, True)

        @block.vector
        def _(dve):
            class Own:
                base, n = 0, 0

            def step(ins):
                Own.n += 1
                ins.then_inc(s_dve, 1)

            def settled():
                dve.wait_ge(s_dve, Own.base + Own.n)

            def link(ins):
                step(ins)
                settled()

            def ln1_stats(t):
                b, c = t
                dve.wait_ge(s_x[c % C], (b + c // C) * 16 + 16)
                link(dve.bn_stats(st6[:, :], x_s[:, c % C, :]))
                hold(dve)
                link(dve.bn_aggr(mv[:, :], st6[:, :]))
                dve.tensor_scalar(mv[:, 1:2], mv[:, 1:2], EPS, None, ALU.add).then_inc(s_mv, 1)

            def ln1(t):
                up_to(dve, s_rstd, 1, t, 1)
                up_to(dve, s_xnTp, 1, before_(t, 1), 1)
                dve.tensor_scalar(xn[:, :], x_s[:, t[1] % C, :], mv[:, 0:1], rstd[:, 0:1],
                                  ALU.subtract, ALU.mult).then_inc(s_xn, 1)

            def xnT_low(t):
                up_to(dve, s_qps, 1, before_(t, 1), 1)
                up_to(dve, s_vgps, 1, before_(t, 1), 1)
                up_to(dve, s_xnTs, 1, t, 1)
                dve.tensor_tensor(xnT[:, 1, :, :].rearrange("p k n -> p (k n)"), p_xnT,
                                  xnT[:, 0, :, :].rearrange("p k n -> p (k n)"), ALU.subtract).then_inc(s_xnTl, 1)

            def oT_low(t):
                up_to(dve, s_oTs, 1, t, 1)
                dve.tensor_tensor(oT[:, 1, :, :].rearrange("p k n -> p (k n)"), p_oT,
                                  oT[:, 0, :, :].rearrange("p k n -> p (k n)"), ALU.subtract).then_inc(s_oTl, 1)

            def kT_low(t):
                up_to(dve, s_kTs, 1, t, 1)
                kT = KQ[:, t[1] % 2, :, :, 0, :]
                dve.tensor_tensor(kT[:, 1, :, :], p_kT, kT[:, 0, :, :], ALU.subtract).then_inc(s_kTl, 1)

            def q_low(t):
                up_to(dve, s_qs, 1, t, 1)
                qT = KQ[:, t[1] % 2, :, :, 1, :]
                dve.scalar_tensor_tensor(qT[:, 1, :, :], p_q, Q_SCALE, qT[:, 0, :, :], ALU.mult, ALU.subtract).then_inc(s_ql, 1)

            def k_norm(t):
                up_to(dve, s_ksq, 4, t, 4)
                up_to(dve, s_eb, 1, t, 1)
                step(dve.tensor_scalar(karg[:, H:2 * H], eb[:, :], 1.0, A_SCALE ** 2, ALU.add, ALU.mult))
                link(dve.tensor_scalar(ks[:, H:2 * H], ks[:, 0:H], (A_SCALE * K_SCALE) ** -2, 1e-12 * K_SCALE ** -2, ALU.mult, ALU.add))
                dve.tensor_tensor(karg[:, 0:H], ks[:, H:2 * H], karg[:, H:2 * H], ALU.mult).then_inc(s_karg, 1)

            def k_prime(t):
                up_to(dve, s_ops, 1, before_(t, 2), 1)
                up_to(dve, s_kscale, 1, t, 1)
                dve.tensor_tensor(Kp[:, t[1] % 2, :, :], p_kv.rearrange("p (h n) -> p h n", h=H),
                                  col(kscale[:, 0:H], DK), ALU.mult).then_inc(s_kp, 1)

            def v_gate(t):
                up_to(dve, s_vgps, 1, t, 1)
                up_to(dve, s_th, 1, t, 1)
                par = t[1] % 2
                v, g = p_kv[:, 0:256].rearrange("p (h n) -> p h n", h=H), p_kv[:, 256:512].rearrange("p (h n) -> p h n", h=H)
                step(dve.tensor_tensor(Vp[:, par, :, :], v, col(kscale[:, H:2 * H], DV), ALU.mult))
                link(dve.scalar_tensor_tensor(gs[:, par, :, :], gs[:, par, :, :], 1.0, g, ALU.add, ALU.mult))
                dve.tensor_tensor(gs[:, par, :, :], gs[:, par, :, :], normw_s[:, :].unsqueeze(1).broadcast_to([P, H, DV]),
                                  ALU.mult).then_inc(s_gs, 1)

            def masked_l(t):
                for a in range(2):
                    up_to(dve, s_gram, 2, t, a + 1)
                    last = dve.tensor_tensor(nL[:, 2 * a:2 * a + 2, :], p_gram[a][:, :, 0, :],
                                             before_neg.unsqueeze(1).broadcast_to([P, 2, P]), ALU.mult)
                last.then_inc(s_nL, 1)

            def masked_scores(t):
                up_to(dve, s_ops, 1, before_(t, 2), 1)
                for a in range(2):
                    dve.tensor_tensor(AT[:, t[1] % 2, 2 * a:2 * a + 2, :], p_gram[a][:, :, 1, :],
                                      causal.unsqueeze(1).broadcast_to([P, 2, P]), ALU.mult).then_inc(s_AT, 1)

            def level_zero_t(t):
                up_to(dve, s_Xi, 2, t, 2)
                up_to(dve, s_Lh, 1, t, 1)
                hold(dve)
                par = t[1] % 2
                dve.copy_predicated(odd(XT[:, par, :, :], 0), level_mask(0, 1, H), odd(Lh[:, par, :, :], 0))

            def level_zero(t):
                up_to(dve, s_yps, 7, t, 1)
                hold(dve)
                dve.copy_predicated(even(X[:, t[1] % 2, :, :], 0), level_mask(0, 0, H), packed(p_y, 0)).then_inc(s_xup, 1)

            def level_update(t, lev):
                up_to(dve, s_xps, 6, t, lev)
                hold(dve)
                par = t[1] % 2
                dve.copy_predicated(even(X[:, par, :, :], lev), level_mask(lev, 0, H), packed(p_x, lev))
                dve.copy_predicated(odd(XT[:, par, :, :], lev), level_mask(lev, 1, H), packed(p_xt, lev)).then_inc(s_xup, 1)

            def correct(t):
                up_to(dve, s_wps, 1, before_(t, 1), 1)
                up_to(dve, s_zps, 1, t, 1)
                dve.tensor_tensor(dXT[:, :, :], p_r, XT[:, t[1] % 2, :, :], ALU.add).then_inc(s_z, 1)

            def r_make(t):
                up_to(dve, s_pps, 1, t, 1)
                r = Vp[:, t[1] % 2, :, :]
                dve.scalar_tensor_tensor(r, p_p, -1.0 / (K_SCALE * S_SCALE), r, ALU.mult, ALU.add).then_inc(s_r, 1)

            def r_low(t):
                up_to(dve, s_wps, 1, before_(t, 1), 1)
                up_to(dve, s_rh, 1, t, 1)
                dve.scalar_tensor_tensor(R_s[:, 1, :, :], Vp[:, t[1] % 2, :, :], R_SCALE, R_s[:, 0, :, :],
                                         ALU.mult, ALU.subtract).then_inc(s_rl, 1)

            def w_low(t):
                up_to(dve, s_ws, 1, t, 1)
                dve.tensor_tensor(W_s[:, 1, :, :], p_p, W_s[:, 0, :, :], ALU.subtract).then_inc(s_wl, 1)

            def state_low(t):
                up_to(dve, s_sh, 1, t, 1)
                dve.scalar_tensor_tensor(S_s[:, 1, :, :], S[:, :, :], S_SCALE, S_s[:, 0, :, :],
                                         ALU.mult, ALU.subtract).then_inc(s_sl, 1)

            def state(t):
                up_to(dve, s_ops, 1, t, 1)
                if t[1] % C < C - 1:
                    dve.wait_ge(s_ups, t[0] * (C - 1) + (t[1] + 1))
                    dve.scalar_tensor_tensor(S[:, :, :], p_u, 1.0 / (K_SCALE * R_SCALE), S[:, :, :],
                                             ALU.mult, ALU.add).then_inc(s_s, 1)
                else:
                    dve.memset(S[:, :, :], 0.0).then_inc(s_s, 1)

            def o_scale(t):
                up_to(dve, s_osq, 4, t, 4)
                dve.tensor_scalar(oarg[:, :], osum[:, :], O_SCALE ** 2 / DV, O_SCALE ** 2 * EPS, ALU.mult, ALU.add).then_inc(s_oarg, 1)

            def o_norm(t):
                up_to(dve, s_ors, 1, t, 1)
                link(dve.tensor_tensor(osq[:, :, :], p_o, col(ors[:, :], DV), ALU.mult))
                dve.tensor_tensor(osq[:, :, :], osq[:, :, :], gs[:, t[1] % 2, :, :], ALU.mult).then_inc(s_on, 1)

            def residual(t):
                up_to(dve, s_wops, 1, t, 1)
                s_ = t[1] % C
                dve.scalar_tensor_tensor(x_s[:, s_, :], p_wo, 1.0 / A_SCALE, x_s[:, s_, :], ALU.mult, ALU.add).then_inc(s_res, 1)

            def ln2_stats(t):
                s_ = t[1] % C
                up_to(dve, s_res, 1, t, 1)
                link(dve.bn_stats(st6b[:, :], x_s[:, s_, :]))
                hold(dve)
                link(dve.bn_aggr(mv2[:, :], st6b[:, :]))
                dve.tensor_scalar(mv2[:, 1:2], mv2[:, 1:2], EPS, None, ALU.add).then_inc(s_mv2, 1)

            def ln2(t, row, scattered):
                if scattered is not None:
                    dve.wait_ge(s_scat[t[1] % C], scattered)
                up_to(dve, s_rstd2, 1, t, 1)
                dve.tensor_scalar(rowA[:, row, 0:D], x_s[:, t[1] % C, :], mv2[:, 0:1], rstd2[:, 0:1],
                                  ALU.subtract, ALU.mult).then_inc(s_xn2, 1)

            def logits_copy(t):
                up_to(dve, s_lgps, 1, t, 1)
                dve.tensor_copy(logits[:, t[1] % C, :], p_lg).then_inc(s_lg, 1)

            def weight_lo(n, parts, src):
                dve.wait_ge(s_wsh, n + 1)
                return dve.scalar_tensor_tensor(parts[:, 1, :, :], src, A_SCALE, parts[:, 0, :, :], ALU.mult, ALU.subtract)

            def route_masks(b, par):
                diff, ex, a0, a1, a2, a3 = r8[0:6]
                m1, tm, m2, ssum, g1, g2, g2s, tm2, gd = r1
                rows = rowA[:, par * C:(par + 1) * C, :]
                pref_c = pref.unsqueeze(1).broadcast_to([P, C, E])
                dve.wait_ge(s_lg, b * C + C)
                step(dve.tensor_reduce(m1[:, :], logits[:, :, :], AX.X, ALU.max))
                yield
                dve.tensor_tensor(diff[:, :, :], logits[:, :, :], col(m1[:, :], E), ALU.subtract).then_inc(s_rd, 1)
                yield
                dve.wait_ge(s_rd, b + 1)
                step(dve.scalar_tensor_tensor(a0[:, :, :], diff[:, :, :], 0.0, pref_c, ALU.is_equal, ALU.mult))
                yield
                step(dve.tensor_reduce(tm[:, :], a0[:, :, :], AX.X, ALU.max))
                yield
                step(dve.tensor_tensor(first[:, :, :], a0[:, :, :], col(tm[:, :], E), ALU.is_equal))
                step(dve.tensor_scalar(rows[:, :, D + 2], tm[:, :], -1.0, float(E), ALU.mult, ALU.add))
                yield
                step(dve.scalar_tensor_tensor(a1[:, :, :], first[:, :, :], -1e30, diff[:, :, :], ALU.mult, ALU.add))
                yield
                step(dve.tensor_reduce(m2[:, :], a1[:, :, :], AX.X, ALU.max))
                yield
                step(dve.tensor_tensor(a2[:, :, :], a1[:, :, :], col(m2[:, :], E), ALU.is_equal))
                yield
                step(dve.tensor_tensor(a3[:, :, :], a2[:, :, :], pref_c, ALU.mult))
                yield
                step(dve.tensor_reduce(tm2[:, :], a3[:, :, :], AX.X, ALU.max))
                yield
                step(dve.tensor_tensor(second[:, :, :], a3[:, :, :], col(tm2[:, :], E), ALU.is_equal))
                yield
                dve.tensor_tensor(both[:, :, :], first[:, :, :], second[:, :, :], ALU.add).then_inc(s_both, 1)
                dve.wait_ge(s_rexp, b + 1)
                step(dve.tensor_reduce(ssum[:, :], ex[:, :, :], AX.X, ALU.add))
                step(dve.tensor_tensor(a0[:, :, :], ex[:, :, :], second[:, :, :], ALU.mult))
                yield
                step(dve.tensor_reduce(g2[:, :], a0[:, :, :], AX.X, ALU.add))
                step(dve.reciprocal(g1[:, :], ssum[:, :]))
                yield
                step(dve.tensor_tensor(g2s[:, :], g2[:, :], g1[:, :], ALU.mult))
                yield
                step(dve.tensor_tensor(rows[:, :, D + 1], g1[:, :], g2s[:, :], ALU.subtract))
                step(dve.tensor_copy(rows[:, :, D], g2s[:, :]))
                step(dve.tensor_copy(rows[:, :, D + 3], fc[:, bass.ds(b * C + 529, C)]))
                yield

            def route_slots(b, scattered):
                dve.wait_ge(s_rank, b + 1)
                step(dve.tensor_copy(rbase[:, 0, :], run[:, :]))
                for c in range(C):
                    yield
                    dst = rbase[:, c + 1, :] if c < C - 1 else run[:, :]
                    step(dve.tensor_tensor(dst, rbase[:, c, :], p_tot[:, c * E:(c + 1) * E], ALU.add))
                yield
                dve.scalar_tensor_tensor(pos[:, :, :], p_rank.rearrange("p (c e) -> p c e", c=C), -K_SCALE ** 2, rbase[:, :, :],
                                         ALU.mult, ALU.add).then_inc(s_pos, 1)
                yield
                dve.wait_ge(s_pos, b + 1)
                for k, m in enumerate((first, second)):
                    step(dve.tensor_tensor(r8[6 + k][:, :, :], pos[:, :, :], m[:, :, :], ALU.mult))
                yield
                for k in range(2):
                    step(dve.tensor_reduce(r1[k][:, :], r8[6 + k][:, :, :], AX.X, ALU.add))
                yield
                for c in range(C):
                    dve.wait_ge(s_scat[c], scattered)
                step(dve.tensor_copy(slot[:, 0, :], r1[0][:, :]))
                dve.tensor_copy(slot[:, 1, :], r1[1][:, :]).then_inc(s_slot, 1)
                yield

            def on(gen):
                if gen is not None:
                    settled()
                    next(gen, None)

            def all_of(gen):
                settled()
                for _ in gen:
                    settled()

            dve.wait_ge(s_const, 16 * CONST_LOADS)
            dve.wait_ge(s_init, 2)
            step(dve.tensor_scalar(negI[:, :], ident, -1.0, None, ALU.mult))
            step(dve.tensor_scalar(before_neg, before_neg, -K_SCALE ** -2, None, ALU.mult))
            step(dve.tensor_scalar(causal, causal, 1.0 / K_SCALE, None, ALU.mult))
            step(dve.tensor_scalar(normw_s[:, :], normw_s[:, :], 0.5 / A_SCALE, None, ALU.mult))
            step(dve.tensor_copy(mask_s[:, :, :].rearrange("p a b -> p (a b)"), mask_in))
            link(dve.tensor_copy(run[:, :], region))
            t0 = (0, 0)
            ln1_stats(t0)
            ln1(t0)
            weight_lo(0, wb_s, wb_in[:, :, :])
            weight_lo(0, wk_s, wk_in).then_inc(s_wsl, 1)
            xnT_low(t0)
            ln1_stats((0, 1))
            weight_lo(1, wvg_s, wvg_in).then_inc(s_wsl, 1)
            weight_lo(2, wq_s, wq_in).then_inc(s_wsl, 1)
            weight_lo(3, wo_s, wo_in).then_inc(s_wsl, 1)
            k_norm(t0)
            k_prime(t0)
            q_low(t0)
            kT_low(t0)
            masked_l(t0)
            masked_scores(t0)

            def body(b, par, first_, last_):
                gen = None
                for c in range(C):
                    t = (b, c)
                    front, epi = not (last_ and c == C - 1), not (first_ and c == 0)
                    nxt, prv = after_(t), before_(t, 1)
                    front2 = not (last_ and c >= C - 2)
                    epi2 = epi and not (first_ and c == 1)
                    if c == 2 and not first_:
                        gen = route_masks(b - 1, 1 - par)
                    level_zero_t(t)
                    on(gen)
                    if front:
                        ln1(nxt)
                    level_zero(t)
                    on(gen)
                    if epi:
                        r_make(prv)
                    if front:
                        xnT_low(nxt)
                    on(gen)
                    v_gate(t)
                    on(gen)
                    level_update(t, 1)
                    on(gen)
                    if epi:
                        r_low(prv)
                        correct(prv)
                    on(gen)
                    if epi2:
                        residual(before_(t, 2))
                    on(gen)
                    level_update(t, 2)
                    on(gen)
                    if epi:
                        w_low(prv)
                    on(gen)
                    if epi2:
                        ln2_stats(before_(t, 2))
                    on(gen)
                    level_update(t, 3)
                    on(gen)
                    if front:
                        k_norm(nxt)
                    if epi:
                        state(prv)
                    on(gen)
                    if epi2:
                        ln2(before_(t, 2), (par * C + c - 2) % (2 * C), None if first_ or c < 2 else (b - 1) * 32 + 16)
                    on(gen)
                    level_update(t, 4)
                    on(gen)
                    if front:
                        q_low(nxt)
                    on(gen)
                    if front:
                        k_prime(nxt)
                    on(gen)
                    if epi:
                        o_scale(prv)
                    on(gen)
                    level_update(t, 5)
                    if gen is not None:
                        all_of(gen)
                    if epi:
                        state_low(prv)
                    if front:
                        kT_low(nxt)
                    if front2:
                        ln1_stats(after_(t, 2))
                    if c == 2 and not first_:
                        gen = route_slots(b - 1, (b - 1) * 32 + 16)
                        on(gen)
                    if epi2:
                        logits_copy(before_(t, 2))
                    on(gen)
                    level_update(t, 6)
                    on(gen)
                    if epi:
                        o_norm(prv)
                    on(gen)
                    if gen is not None:
                        all_of(gen)
                        gen = None
                    if front:
                        masked_l(nxt)
                    if epi:
                        oT_low(prv)
                    if front:
                        masked_scores(nxt)

            start = Own.n
            body(0, 0, True, False)
            per_seq = OWN_PER_SEQ
            first_n = Own.n
            with dve.Fori(0, (B - 2) // 2) as pair:
                for n, par in enumerate((1, 0)):
                    Own.base, Own.n = pair * (2 * per_seq) + (first_n + n * per_seq), 0
                    body(pair * 2 + (1 + n), par, False, False)
                    assert Own.n == per_seq, Own.n
            Own.base, Own.n = first_n + (B - 2) * per_seq, 0
            body(B - 1, 1, False, True)
            last_tile = (B - 1, C - 1)
            before_last = before_(last_tile, 1)
            r_make(last_tile)
            r_low(last_tile)
            correct(last_tile)
            residual(before_last)
            ln2_stats(before_last)
            w_low(last_tile)
            ln2(before_last, 2 * C - 2, 32 * (B - 2) + 16)
            state(last_tile)
            o_scale(last_tile)
            logits_copy(before_last)
            o_norm(last_tile)
            oT_low(last_tile)
            residual(last_tile)
            ln2_stats(last_tile)
            ln2(last_tile, 2 * C - 1, 32 * (B - 2) + 16)
            logits_copy(last_tile)
            all_of(route_masks(B - 1, 1))
            all_of(route_slots(B - 1, 32 * (B - 1) + 16))

            cnt, ntf, cum, prev, ge, oneh, rw, tmp = t8
            settled()
            step(dve.memset(zrow[:, 0:D + 3], 0.0))
            step(dve.tensor_scalar(zrow[:, D + 3:D + 4], lane, float(B * N), None, ALU.add))
            link(dve.tensor_tensor(cnt[:, :], run[:, :], region, ALU.subtract))
            dve.tensor_copy(pad_row[:, :], run[:, :]).then_inc(s_tail, 1)
            link(dve.tensor_scalar(t8i[:, :], cnt[:, :], float(PE_TOK - 1), None, ALU.add))
            link(dve.tensor_scalar(t8j[:, :], t8i[:, :], PE_TOK.bit_length() - 1, None, ALU.arith_shift_right))
            link(dve.tensor_copy(ntf[:, :], t8j[:, :]))
            link(dve.tensor_tensor_scan(cum[:, :], ones[:, 0:E], ntf[:, :], 0.0, ALU.mult, ALU.add))
            link(dve.tensor_tensor(prev[:, :], cum[:, :], ntf[:, :], ALU.subtract))
            link(dve.tensor_scalar(ge[:, :], cum[:, :], lane, None, ALU.is_le))
            step(dve.tensor_scalar(oneh[:, 0:1], ge[:, 0:1], -1.0, 1.0, ALU.mult, ALU.add))
            step(dve.tensor_tensor(oneh[:, 1:E], ge[:, 0:E - 1], ge[:, 1:E], ALU.subtract))
            link(dve.tensor_scalar(rw[:, :], prev[:, :], lane, -float(PE_TOK), ALU.subtract, ALU.mult))
            link(dve.tensor_tensor(tmp[:, :], rw[:, :], region, ALU.add))
            link(dve.tensor_tensor(rw[:, :], tmp[:, :], oneh[:, :], ALU.mult))
            step(dve.tensor_reduce(tab_f[:, 0:1], ge[:, 0:E - 1], AX.X, ALU.add))
            link(dve.tensor_reduce(cnt[:, 0:1], rw[:, :], AX.X, ALU.add))
            link(dve.scalar_tensor_tensor(tab_f[:, 1:2], ge[:, E - 1:E], float(SPARE), cnt[:, 0:1], ALU.mult, ALU.add))
            dve.tensor_copy(tab_i[:, :], tab_f[:, :]).then_inc(s_tail, 1)

            def xT_lo(i, q):
                dve.wait_ge(s_gTh, i * 4 + (q + 1))
                dve.tensor_tensor(xTl[:, q % 2, :, :], p_gT, xTh[:, q % 2, :, :], ALU.subtract).then_inc(s_gTl, 1)

            def hidden_lo(i, q):
                for m in range(4):
                    dve.wait_ge(s_hhi, i * 16 + (4 * q + m + 1))
                    two = slice(2 * m, 2 * m + 2)
                    dve.scalar_tensor_tensor(hlo[:, q % 2, two, :], hf[:, m, :].rearrange("p (m n) -> p m n", m=2), H_SCALE,
                                             hhi[:, q % 2, two, :], ALU.mult, ALU.subtract).then_inc(s_hlo, 1)

            def rows_out(i, q):
                if not (isinstance(i, int) and i * 4 + q < 2):
                    dve.wait_ge(s_acc, i * 128 + 32 * (q - 1))
                w, par = xg[:, q, :, :], q % 2
                step(dve.tensor_copy(yidx[:, q, :], w[:, :, D + 3]))
                step(dve.tensor_scalar(gsel[:, par, :], w[:, :, D + 2], experts_b[:, bass.ds(i * 4 + q, 1)],
                                       1.0 / (W_SCALE * H_SCALE), ALU.is_equal, ALU.mult))
                settled()
                link(dve.tensor_tensor(gsel[:, par, :], gsel[:, par, :], w[:, :, D + 1], ALU.mult))
                link(dve.scalar_tensor_tensor(gate[:, par, :], w[:, :, D], 1.0 / (W_SCALE * H_SCALE), gsel[:, par, :],
                                              ALU.mult, ALU.add))
                dve.wait_ge(s_yops, i * 4 + (q + 1))
                for a in range(2):
                    step(dve.tensor_scalar(yrow[:, par, a, :], p_yo[a][:, 0, :], gate[:, par, a:a + 1],
                                           None, ALU.mult))
                settled()
                for a in range(2):
                    last = dve.scalar_tensor_tensor(yrow[:, par, a, :], p_yo[a][:, 1, :], gate[:, par, a:a + 1],
                                                    yrow[:, par, a, :], ALU.mult, ALU.add)
                last.then_inc(s_yrow, 1)

            dve.wait_ge(s_xg[0], 16)
            xT_lo(0, 0)
            xT_lo(0, 1)
            hidden_lo(0, 0)

            def expert_body(i, last):
                for q in range(LAST if last else 4):
                    if not (last and q + 2 >= LAST):
                        xT_lo(i, q + 2)
                    if not (last and q + 1 >= LAST):
                        hidden_lo(i, q + 1)
                    rows_out(i, q)
            before_experts = Own.base + Own.n
            expert_body(0, False)
            per_body = Own.base + Own.n - before_experts
            with dve.Fori(1, MAXT // 4) as i:
                Own.base, Own.n = i * per_body + before_experts, 0
                expert_body(i, False)
            Own.base, Own.n = before_experts + (MAXT // 4) * per_body, 0
            expert_body(MAXT // 4, True)


FCONST = 577
Q_SCALE = K_SCALE * float(DK) ** -0.5 / A_SCALE
CONST_LOADS = 5
OWN_PER_SEQ = 65


def constants():
    import numpy as np
    f = np.zeros((P, FCONST), np.float32)
    j, i = np.arange(P)[:, None], np.arange(P)[None, :]
    f[:, 0:128] = j == i
    f[:, 128:256] = j <= i
    f[:, 256:384] = j < i
    f[:, 384:512] = 1.0
    f[:, 512:520] = E - np.arange(E)
    f[:, 520:528] = REGION * np.arange(E)
    f[:, 528] = np.arange(P)
    f[:, 529:529 + T] = P * np.arange(T)[None, :] + j
    f[:, 561:577] = -0.5
    m = np.zeros((P, 2 * LEVELS, 64), np.int32)
    for lev in range(LEVELS):
        s = 1 << lev
        lower = (j // s == i // s + 1) & ((i // s) % 2 == 0)
        m[:, 2 * lev, :] = lower.reshape(P, -1, 2, s)[:, :, 0, :].reshape(P, 64)
        m[:, 2 * lev + 1, :] = lower.T.reshape(P, -1, 2, s)[:, :, 1, :].reshape(P, 64)
    return f, m


def kernel(**inputs):
    import numpy as np
    import concourse.bacc as bacc
    from concourse.bass_utils import run_bass_kernel_spmd

    g = {k: np.asarray(v) for k, v in inputs.items()}
    fconst, iconst = constants()
    w1 = g["L0_ffn_w1"].transpose(2, 0, 1).reshape(KC, P, T // KC, PIECE).transpose(0, 2, 1, 3).reshape(T, P, PIECE)
    w2 = g["L0_ffn_w2"].transpose(2, 0, 1).reshape(KH, P, T // KH, PIECE).transpose(0, 2, 1, 3).reshape(T, P, PIECE)
    arrays = {
        "x": g["L0_attn_x"].reshape(T, P, D),
        "wq": g["L0_attn_Wq"], "wk": g["L0_attn_Wk"],
        "wvg": np.concatenate([g["L0_attn_Wv"], g["L0_attn_Wg"]], axis=1),
        "wb": g["L0_attn_Wb"], "wo": g["L0_attn_Wo"], "norm_w": g["L0_attn_norm_w"],
        "router": g["L0_ffn_router_w"].T,
        "w1": w1, "w2": w2, "fconst": fconst, "iconst": iconst,
    }
    arrays = {k: np.ascontiguousarray(v) for k, v in arrays.items()}
    nc = bacc.Bacc("TRN2", target_bir_lowering=False, num_devices=1)
    args = [nc.dram_tensor(k, a.shape, mybir.dt.from_np(a.dtype), kind="ExternalInput").ap() for k, a in arrays.items()]
    out = nc.dram_tensor("out", (B * N + P, D), mybir.dt.float32, kind="ExternalOutput").ap()
    build(nc, *args, out)
    r = run_bass_kernel_spmd(nc, [arrays], core_ids=[0])
    return r.results[0]["out"][:B * N].reshape(B, N, D)
```
